# Optimizing a Trainium2 kernel written in Bass

```python
import numpy as np
import jax
import jax.numpy as jnp

def _softmax(x, axis=-1):
    return jax.nn.softmax(x, axis=axis)

def _gelu(x):
    return jax.nn.gelu(x, approximate=True)

def _silu(x):
    return jax.nn.silu(x)

def _sigmoid(x):
    return jax.nn.sigmoid(x)

def _layernorm(x, axis=-1, eps=1e-05):
    m = jnp.mean(x, axis=axis, keepdims=True)
    v = jnp.var(x, axis=axis, keepdims=True)
    return (x - m) / jnp.sqrt(v + eps)

def _scatter_add(tgt, idx, src, axis=0):
    return tgt.at[idx].add(src)

def _segment_sum(src, seg, n):
    return jax.ops.segment_sum(src, seg, n)
kernel_name = 'mk_early_fusion_d2_tok_img512_r4_0c64f0'

def setup_inputs(seed: int=0):
    np.random.seed(seed)
    _w = jnp.asarray

    def _rec_inputs():
        import jax
        import jax.numpy as jnp
        _rk = jax.random.key(seed)
        x = -0.000178447 + 0.99995 * jax.random.normal(jax.random.fold_in(_rk, 1), (64, 3, 176, 208), jnp.float32)
        txt = -0.051393 + 1.14128 * jax.random.normal(jax.random.fold_in(_rk, 2), (64, 128, 128), jnp.float32)
        return (x, txt)
    x, txt = _rec_inputs()

    def _L0_tok_setup():
        import jax, jax.numpy as jnp
        import numpy as np
        P1, P2, C = (16, 16, 3)
        PW, PH = (176 // P1, 208 // P2)
        key = jax.random.key(seed)
        k1, k2, k3, k4, k5 = jax.random.split(key, 5)
        B, D = (64, 128)
        patch_dim = P1 * P2 * C
        return {'x': jax.random.normal(k1, (B, C, PW * P1, PH * P2), dtype=jnp.float32), 'W': jax.random.normal(k2, (D, patch_dim), dtype=jnp.float32) * 0.02, 'b': jax.random.normal(k3, (D,), dtype=jnp.float32) * 0.02, 'cls_token': jax.random.uniform(k4, (1, 1, D), dtype=jnp.float32), 'pos_emb': jax.random.normal(k5, (1, PW * PH + 1, 1), dtype=jnp.float32)}
    _L0_tok_all = _L0_tok_setup()
    _L0_tok_in = {k: v for k, v in _L0_tok_all.items() if k in ('W', 'b', 'cls_token', 'pos_emb')}
    del _L0_tok_all

    def _L0_attn_setup():
        import jax, jax.numpy as jnp
        import numpy as np
        NUM_HEAD = 8
        DIM_MODEL = 128
        DIM_HEAD = DIM_MODEL // NUM_HEAD
        LN_EPS = 1e-05
        key = jax.random.key(seed)
        ks = jax.random.split(key, 12)
        B, L, D = (4, 512, DIM_MODEL)
        s = 0.02
        return {'x': jax.random.normal(ks[0], (B, L, D), dtype=jnp.float32), 'Wq': jax.random.normal(ks[1], (D, D), dtype=jnp.float32) * s, 'bq': jnp.zeros((D,), dtype=jnp.float32), 'Wk': jax.random.normal(ks[2], (D, D), dtype=jnp.float32) * s, 'bk': jnp.zeros((D,), dtype=jnp.float32), 'Wv': jax.random.normal(ks[3], (D, D), dtype=jnp.float32) * s, 'bv': jnp.zeros((D,), dtype=jnp.float32), 'Wo': jax.random.normal(ks[4], (D, D), dtype=jnp.float32) * s, 'bo': jnp.zeros((D,), dtype=jnp.float32), 'gamma': jnp.ones((D,), dtype=jnp.float32), 'beta': jnp.zeros((D,), dtype=jnp.float32)}
    _L0_attn_all = _L0_attn_setup()
    _L0_attn_in = {k: v for k, v in _L0_attn_all.items() if k in ('Wq', 'bq', 'Wk', 'bk', 'Wv', 'bv', 'Wo', 'bo', 'gamma', 'beta')}
    del _L0_attn_all

    def _L0_ffn_setup():
        import jax, jax.numpy as jnp
        import numpy as np
        B, S, D, H, E = (4, 512, 128, 256, 8)
        key = jax.random.key(seed)
        ks = jax.random.split(key, 4)
        x = jax.random.normal(ks[0], (B, S, D), jnp.float32)
        Wr = jax.random.normal(ks[1], (E, D), jnp.float32) * 0.02
        br = jnp.zeros((E,), jnp.float32)
        W1 = jax.random.normal(ks[2], (E, D, H), jnp.float32) * 0.02
        b1 = jnp.zeros((E, H), jnp.float32)
        W2 = jax.random.normal(ks[3], (E, H, D), jnp.float32) * 0.02
        b2 = jnp.zeros((E, D), jnp.float32)
        return {'x': x, 'Wr': Wr, 'br': br, 'W1': W1, 'b1': b1, 'W2': W2, 'b2': b2}
    _L0_ffn_all = _L0_ffn_setup()
    _L0_ffn_in = {k: v for k, v in _L0_ffn_all.items() if k in ('Wr', 'br', 'W1', 'b1', 'W2', 'b2')}
    del _L0_ffn_all

    def _L1_attn_setup():
        import jax, jax.numpy as jnp
        import numpy as np
        HEADS = 8
        D_MODEL = 128
        NU = 1
        EPS = 1e-06
        SEQ = 1024
        BATCH = 8
        DK = D_MODEL // HEADS
        PHI = 2 * NU * DK

        def dpfp(x):
            x = jnp.concatenate([jax.nn.relu(x), jax.nn.relu(-x)], axis=-1)
            x_rolled = jnp.concatenate([jnp.roll(x, j, axis=-1) for j in range(1, NU + 1)], axis=-1)
            x_repeat = jnp.concatenate([x] * NU, axis=-1)
            y = x_repeat * x_rolled
            return y / (jnp.sum(y, axis=-1, keepdims=True) + EPS)
        key = jax.random.key(seed)
        ks = jax.random.split(key, 7)
        s = 0.02
        return {'x': jax.random.normal(ks[0], (SEQ, BATCH, D_MODEL), dtype=jnp.float32), 'Wq': jax.random.normal(ks[1], (D_MODEL, HEADS * DK), dtype=jnp.float32) * s, 'Wk': jax.random.normal(ks[2], (D_MODEL, HEADS * DK), dtype=jnp.float32) * s, 'Wv': jax.random.normal(ks[3], (D_MODEL, HEADS * DK), dtype=jnp.float32) * s, 'Wg': jax.random.normal(ks[4], (D_MODEL, HEADS), dtype=jnp.float32) * s, 'Wo': jax.random.normal(ks[5], (D_MODEL, D_MODEL), dtype=jnp.float32) * s, 'bo': jnp.zeros((D_MODEL,), dtype=jnp.float32)}
    _L1_attn_all = _L1_attn_setup()
    _L1_attn_in = {k: v for k, v in _L1_attn_all.items() if k in ('Wq', 'Wk', 'Wv', 'Wg', 'Wo', 'bo')}
    del _L1_attn_all

    def _L1_ffn_setup():
        import jax, jax.numpy as jnp
        import numpy as np
        B, S, D, E, O = (256, 64, 128, 16, 128)
        key = jax.random.key(seed)
        k_x, k_wg, k_bg, k_we, k_be = jax.random.split(key, 5)
        scale_g = 1.0 / np.sqrt(D)
        scale_e = 1.0 / np.sqrt(D)
        return {'x': jax.random.normal(k_x, (B, S, D), dtype=jnp.float32), 'Wg': jax.random.uniform(k_wg, (D, E), jnp.float32, -scale_g, scale_g), 'bg': jax.random.uniform(k_bg, (E,), jnp.float32, -scale_g, scale_g), 'We': jax.random.uniform(k_we, (E, D, O), jnp.float32, -scale_e, scale_e), 'be': jax.random.uniform(k_be, (E, O), jnp.float32, -scale_e, scale_e)}
    _L1_ffn_all = _L1_ffn_setup()
    _L1_ffn_in = {k: v for k, v in _L1_ffn_all.items() if k in ('Wg', 'bg', 'We', 'be')}
    del _L1_ffn_all
    return {'x': x, 'txt': txt, 'L0_tok_W': _L0_tok_in['W'], 'L0_tok_b': _L0_tok_in['b'], 'L0_tok_cls_token': _L0_tok_in['cls_token'], 'L0_tok_pos_emb': _L0_tok_in['pos_emb'], 'L0_attn_Wq': _L0_attn_in['Wq'], 'L0_attn_bq': _L0_attn_in['bq'], 'L0_attn_Wk': _L0_attn_in['Wk'], 'L0_attn_bk': _L0_attn_in['bk'], 'L0_attn_Wv': _L0_attn_in['Wv'], 'L0_attn_bv': _L0_attn_in['bv'], 'L0_attn_Wo': _L0_attn_in['Wo'], 'L0_attn_bo': _L0_attn_in['bo'], 'L0_attn_gamma': _L0_attn_in['gamma'], 'L0_attn_beta': _L0_attn_in['beta'], 'L0_ffn_Wr': _L0_ffn_in['Wr'], 'L0_ffn_br': _L0_ffn_in['br'], 'L0_ffn_W1': _L0_ffn_in['W1'], 'L0_ffn_b1': _L0_ffn_in['b1'], 'L0_ffn_W2': _L0_ffn_in['W2'], 'L0_ffn_b2': _L0_ffn_in['b2'], 'L1_attn_Wq': _L1_attn_in['Wq'], 'L1_attn_Wk': _L1_attn_in['Wk'], 'L1_attn_Wv': _L1_attn_in['Wv'], 'L1_attn_Wg': _L1_attn_in['Wg'], 'L1_attn_Wo': _L1_attn_in['Wo'], 'L1_attn_bo': _L1_attn_in['bo'], 'L1_ffn_Wg': _L1_ffn_in['Wg'], 'L1_ffn_bg': _L1_ffn_in['bg'], 'L1_ffn_We': _L1_ffn_in['We'], 'L1_ffn_be': _L1_ffn_in['be']}

def reference(x, txt, L0_tok_W, L0_tok_b, L0_tok_cls_token, L0_tok_pos_emb, L0_attn_Wq, L0_attn_bq, L0_attn_Wk, L0_attn_bk, L0_attn_Wv, L0_attn_bv, L0_attn_Wo, L0_attn_bo, L0_attn_gamma, L0_attn_beta, L0_ffn_Wr, L0_ffn_br, L0_ffn_W1, L0_ffn_b1, L0_ffn_W2, L0_ffn_b2, L1_attn_Wq, L1_attn_Wk, L1_attn_Wv, L1_attn_Wg, L1_attn_Wo, L1_attn_bo, L1_ffn_Wg, L1_ffn_bg, L1_ffn_We, L1_ffn_be):
    import jax
    import jax.numpy as jnp

    def _L0_tok_ref(x, W, b, cls_token, pos_emb):
        import jax, jax.numpy as jnp
        import numpy as np
        P1, P2, C = (16, 16, 3)
        PW, PH = (176 // P1, 208 // P2)
        B = x.shape[0]
        patches = x.reshape(B, C, PW, P1, PH, P2)
        patches = patches.transpose(0, 2, 4, 3, 5, 1).reshape(B, PW * PH, P1 * P2 * C)
        proj = jnp.einsum('bnp,dp->bnd', patches, W) + b
        cls = jnp.broadcast_to(cls_token, (B, 1, cls_token.shape[-1]))
        out = jnp.concatenate([cls, proj], axis=1) + pos_emb
        return out

    def _L0_attn_ref(x, Wq, bq, Wk, bk, Wv, bv, Wo, bo, gamma, beta):
        import jax, jax.numpy as jnp
        import numpy as np
        NUM_HEAD = 8
        DIM_MODEL = 128
        DIM_HEAD = DIM_MODEL // NUM_HEAD
        LN_EPS = 1e-05
        B, L, D = x.shape
        H, dh = (NUM_HEAD, D // NUM_HEAD)
        Q = x @ Wq.T + bq
        K = x @ Wk.T + bk
        V = x @ Wv.T + bv
        Q = Q.reshape(B * H, L, dh)
        K = K.reshape(B * H, L, dh)
        V = V.reshape(B * H, L, dh)
        scale = dh ** (-0.5)
        attn = jax.nn.softmax(jnp.einsum('bqd,bkd->bqk', Q, K) * scale, axis=-1)
        context = jnp.einsum('bqk,bkd->bqd', attn, V)
        context = context.reshape(B, L, D)
        out = context @ Wo.T + bo
        out = out + x
        mu = jnp.mean(out, axis=-1, keepdims=True)
        var = jnp.mean(jnp.square(out - mu), axis=-1, keepdims=True)
        out = (out - mu) / jnp.sqrt(var + LN_EPS) * gamma + beta
        return out

    def _L0_ffn_ref(x, Wr, br, W1, b1, W2, b2):
        import jax, jax.numpy as jnp
        import numpy as np
        B, S, D, H, E = (4, 512, 128, 256, 8)
        b, s, d = x.shape
        n = b * s
        e = Wr.shape[0]
        xf = x.reshape(n, d)
        logits = xf @ Wr.T + br
        probs = jax.nn.softmax(logits, axis=-1)
        top2_prob, top2_idx = jax.lax.top_k(probs, 2)
        comb = jnp.zeros((n, e), x.dtype).at[jnp.arange(n)[:, None], top2_idx].add(top2_prob)
        h = jax.nn.gelu(jnp.einsum('nd,edh->enh', xf, W1) + b1[:, None, :], approximate=False)
        o = jnp.einsum('enh,ehd->end', h, W2) + b2[:, None, :]
        y = jnp.einsum('ne,end->nd', comb, o)
        return y.reshape(b, s, d)

    def _L1_attn_ref(x, Wq, Wk, Wv, Wg, Wo, bo):
        import jax, jax.numpy as jnp
        import numpy as np
        HEADS = 8
        D_MODEL = 128
        NU = 1
        EPS = 1e-06
        SEQ = 1024
        BATCH = 8
        DK = D_MODEL // HEADS
        PHI = 2 * NU * DK

        def dpfp(x):
            x = jnp.concatenate([jax.nn.relu(x), jax.nn.relu(-x)], axis=-1)
            x_rolled = jnp.concatenate([jnp.roll(x, j, axis=-1) for j in range(1, NU + 1)], axis=-1)
            x_repeat = jnp.concatenate([x] * NU, axis=-1)
            y = x_repeat * x_rolled
            return y / (jnp.sum(y, axis=-1, keepdims=True) + EPS)
        S, B, D = x.shape
        q = dpfp((x @ Wq).reshape(S, B, HEADS, DK))
        k = dpfp((x @ Wk).reshape(S, B, HEADS, DK))
        v = (x @ Wv).reshape(S, B, HEADS, DK)
        beta = jax.nn.sigmoid((x @ Wg).reshape(S, B, HEADS, 1))

        def step(W, qkvb):
            qi, ki, vi, bi = qkvb
            v_exist = jnp.einsum('bhvk,bhk->bhv', W, ki)
            W = W + jnp.einsum('bhv,bhk->bhvk', bi * (vi - v_exist), ki)
            out = jnp.einsum('bhvk,bhk->bhv', W, qi)
            return (W, out)
        W0 = jnp.zeros((B, HEADS, DK, PHI), dtype=x.dtype)
        _, outs = jax.lax.scan(step, W0, (q, k, v, beta))
        out = outs.reshape(S, B, HEADS * DK)
        return out @ Wo + bo

    def _L1_ffn_ref(x, Wg, bg, We, be):
        import jax, jax.numpy as jnp
        import numpy as np
        B, S, D, E, O = (256, 64, 128, 16, 128)
        scores = jax.nn.softmax(jnp.mean(x, axis=1) @ Wg + bg, axis=-1)
        idx = jnp.argmax(scores, axis=-1)
        gate = jnp.take_along_axis(scores, idx[:, None], axis=-1)
        W_sel = We[idx]
        b_sel = be[idx]
        y = jnp.einsum('bsd,bdo->bso', x, W_sel) + b_sel[:, None, :]
        return gate[:, :, None] * y
    h = _L0_tok_ref(x, L0_tok_W, L0_tok_b, L0_tok_cls_token, L0_tok_pos_emb)
    h = jnp.concatenate([h, txt], axis=1)
    h = h + _L0_attn_ref(_layernorm(h, axis=-1), L0_attn_Wq, L0_attn_bq, L0_attn_Wk, L0_attn_bk, L0_attn_Wv, L0_attn_bv, L0_attn_Wo, L0_attn_bo, L0_attn_gamma, L0_attn_beta)
    h = h + _L0_ffn_ref(_layernorm(h, axis=-1), L0_ffn_Wr, L0_ffn_br, L0_ffn_W1, L0_ffn_b1, L0_ffn_W2, L0_ffn_b2)
    h = h + _L1_attn_ref(_layernorm(h, axis=-1), L1_attn_Wq, L1_attn_Wk, L1_attn_Wv, L1_attn_Wg, L1_attn_Wo, L1_attn_bo)
    h = h + _L1_ffn_ref(_layernorm(h, axis=-1), L1_ffn_Wg, L1_ffn_bg, L1_ffn_We, L1_ffn_be)
    return h

_drawn_inputs = setup_inputs


def setup_inputs(seed=0):
    import zlib

    import numpy as np

    out = dict(_drawn_inputs(seed))
    spreads = {'L0_attn_bq': (0.0, 0.8),
     'L0_attn_bk': (0.0, 0.8),
     'L0_attn_bv': (0.0, 0.8),
     'L0_attn_bo': (0.0, 0.1),
     'L0_attn_gamma': (1.0, 0.2),
     'L0_attn_beta': (0.0, 0.1),
     'L0_ffn_br': (0.0, 0.691),
     'L0_ffn_b1': (0.0, 0.8),
     'L0_ffn_b2': (0.0, 0.621),
     'L1_attn_bo': (0.0, 0.1)}
    factors = {'L0_attn_Wq': 8.0,
     'L0_attn_Wk': 8.0,
     'L0_attn_Wv': 8.0,
     'L0_attn_Wo': 8.0,
     'L0_ffn_Wr': 5.651,
     'L0_ffn_W1': 8.0,
     'L0_ffn_W2': 8.0,
     'L1_attn_Wq': 8.0,
     'L1_attn_Wk': 8.0,
     'L1_attn_Wv': 8.0,
     'L1_attn_Wg': 8.0,
     'L1_attn_Wo': 8.0,
     'L1_ffn_Wg': 2.913,
     'L1_ffn_bg': 2.973,
     'L1_ffn_We': 2.898,
     'L1_ffn_be': 24.851}
    for name, (base, spread) in spreads.items():
        noise = np.random.default_rng([zlib.crc32(name.encode()), seed]).standard_normal(out[name].shape)
        drawn = base * np.exp(spread * noise) if base else spread * noise
        out[name] = jnp.asarray(drawn.astype(out[name].dtype))
    for name, factor in factors.items():
        out[name] = (out[name] * factor).astype(out[name].dtype)
    return out
```

```python
import concourse.bass as bass
from concourse import mybir
from contextlib import ExitStack

B = 64
D = 128
PATCHES = 143
LX = PATCHES + 1
TXT = 128
L = LX + TXT
KC = 768 // 128
H = 8
DH = D // H
T = L // H
E1 = 8
HID = 256
E2 = 16
PHI = 2 * DH
G = 17
TOK2 = 256
LEFT = L - TOK2
RT = -(-L // 3)
RTILES = ((0, 0), (1, RT), (2, L - RT))
KT = ((0, RT), (RT, RT), (2 * RT, L - 2 * RT))
FRONT_STEPS, MEM_STEPS, BACK_STEPS = 26, 7 * G - 1, 9
VECS = ("tok_b", "cls", "bq", "bk", "bv", "bo", "gamma", "beta", "bo1") + tuple(f"b1_{i}" for i in range(2 * E1))
NV = len(VECS)


def early_fusion(nc, x, txt, tok_w, pos, vecs, wqkv, wo, wr, br, w1, w2, b2, wp, wo1, wg, bg, we, be,
                 ident, head_mask, tok_pick, tri, expert_rows, expert_numbers, out):
    f32 = mybir.dt.float32
    u32 = mybir.dt.uint32
    ALU = mybir.AluOpType
    ACT = mybir.ActivationFunctionType
    AX = mybir.AxisListType

    ctx = ExitStack()
    with ctx:
        def sb(name, shape, dt=f32):
            return ctx.enter_context(nc.sbuf_tensor(name, shape, dt))

        def dram(name, shape):
            return nc.dram_tensor(name, shape, f32).ap()

        tokw_s = sb("tokw_s", [128, KC, D])
        vec_s = sb("vec_s", [128, NV])
        wqkv_s = sb("wqkv_s", [128, 3, D])
        wo_s = sb("wo_s", [128, D])
        wr_s = sb("wr_s", [128, E1])
        br_s = sb("br_s", [128, E1])
        w1_s = sb("w1_s", [128, E1, HID])
        w2_s = sb("w2_s", [128, E1, 2, D])
        b2_s = sb("b2_s", [E1, D])
        wp_s = sb("wp_s", [128, 3 * D + H])
        wo1_s = sb("wo1_s", [128, D])
        wg_s = sb("wg_s", [128, E2])
        bg_s = sb("bg_s", [1, E2])
        enum_s = sb("enum_s", [1, E2])
        we_s = sb("we_s", [128, E2 * D])
        be_s = sb("be_s", [128, E2])
        ident_s = sb("ident_s", [128, 128])
        hmask_s = sb("hmask_s", [128, H])
        pick_s = sb("pick_s", [128, LEFT])
        tri_s = sb("tri_s", [128, E1, E1])
        erow_s = sb("erow_s", [E1, E1, 128])
        pos_s = sb("pos_s", [128, LX])
        mean_w = sb("mean_w", [128, 128])
        ones_row = sb("ones_row", [1, 128])
        eps_s = sb("eps_s", [128, 1])

        def vec(name):
            i = VECS.index(name)
            return vec_s[:, i:i + 1]

        xb = sb("xb", [128, KC, PATCHES])
        h0 = sb("h0", [128, L])
        xc = sb("xc", [128, L])
        sq = sb("sq", [128, L])
        sd = sb("sd", [128, L])
        rs = sb("rs", [128, L])
        xn1 = sb("xn1", [128, L])
        qkvT = sb("qkvT", [128, 3, L])
        qkd = sb("qkd", [DH + 1, 3, H, L])
        vaug = sb("vaug", [RT, H, 3, DH + 1])
        zero_row = sb("zero_row", [1, L])
        nmx = sb("nmx", [RT, 3])
        pT = sb("pT", [RT, 3, L])
        ctxu = sb("ctxu", [DH + 1, H, L])
        cfm = sb("cfm", [128, L])
        den = sb("den", [128, L])
        y1 = sb("y1", [128, L])
        z1 = sb("z1", [128, L])
        z2 = sb("z2", [128, L])
        h1 = sb("h1", [128, L])
        x2 = sb("x2", [128, L])
        lg = sb("lg", [RT, 3, E1])
        ex = sb("ex", [RT, 3, E1])
        r8 = sb("r8", [RT, 3])
        cmp1 = sb("cmp1", [RT, 3, E1, E1])
        cmp2 = sb("cmp2", [RT, 3, E1, E1])
        rank = sb("rank", [RT, 3, E1])
        comb = sb("comb", [RT, 3, E1])
        combT = sb("combT", [E1, L])
        gl = sb("gl", [128, 2, 2, L])
        hs = sb("hs", [128, 2, 2, L])
        h2 = sb("h2", [128, L])
        x3 = sb("x3", [128, L])
        x3r = sb("x3r", [128, H, LEFT])
        msk = sb("msk", [128, 3 * D + H])
        sel = sb("sel", [128, 3 * DH + 1])
        relu = sb("relu", [128, 2, G, PHI])
        feat = sb("feat", [128, 2, G, PHI])
        fsum = sb("fsum", [128, 2, G])
        khqh = sb("khqh", [128, 2, G, PHI])
        val = sb("val", [128, G, DH])
        bta = sb("bta", [128, G])
        mem = sb("mem", [128, G, DH, PHI])
        tmp = sb("tmp", [128, DH, PHI])
        cc = sb("cc", [128, DH])
        rd = sb("rd", [128, G, DH])
        spread = sb("spread", [128, H, DH])
        so = sb("so", [128, L])
        h3 = sb("h3", [128, L])
        x4 = sb("x4", [128, L])
        msum = sb("msum", [128, 1])
        sc = sb("sc", [1, E2])
        notbest = sb("notbest", [1, E2])
        best = sb("best", [1, 1])
        topi = sb("topi", [1, 1], u32)
        stat = sb("stat", [1, 4])
        gcol = sb("gcol", [128, 1])
        wsel = sb("wsel", [128, D])
        bsel = sb("bsel", [128, 1])
        fin = sb("fin", [128, L])

        P = ctx.enter_context(nc.psum_tensor("P", [128, 8, 512], f32))
        qkv_d = dram("qkv_d", [H, DH, 3 * L])
        ctx_d = dram("ctx_d", [H, DH + 1, L])

        def sem(name, per_image=1):
            return ctx.enter_context(nc.semaphore(name))

        consts_in = sem("consts_in")
        consts_set = sem("consts_set")
        consts_done = sem("consts_done")
        x_in = sem("x_in", 16)
        txt_in = sem("txt_in", 16)
        tok_mm = sem("tok_mm")
        h0_ready = sem("h0_ready")
        qkv_mm = sem("qkv_mm", 3)
        qkv_out = sem("qkv_out", 3)
        qkv_stored = sem("qkv_stored", 16)
        qkd_in = [sem(f"qkd_in_{a}", 16 * H) for a in "qkv"]
        row_cleared = sem("row_cleared")
        zeros_set = sem("zeros_set")
        v_tr = sem("v_tr")
        vaug_ready = sem("vaug_ready")
        s_mm = sem("s_mm", H)
        max_ready = sem("max_ready", H)
        max_tr = sem("max_tr", H)
        max_row = sem("max_row", H)
        st_mm = sem("st_mm", H)
        probs = sem("probs", H)
        pv_mm = sem("pv_mm", H)
        ctx_out = sem("ctx_out", H)
        ctx_stored = sem("ctx_stored", 16)
        cfm_in = sem("cfm_in", 32)
        cfm_ready = sem("cfm_ready")
        wo_mm = sem("wo_mm")
        y1_ready = sem("y1_ready")
        z_ready = sem("z_ready")
        h1_ready = sem("h1_ready")
        router_mm = sem("router_mm")
        lg_ready = sem("lg_ready")
        ex_ready = sem("ex_ready")
        comb_ready = sem("comb_ready")
        comb_tr = sem("comb_tr")
        combT_ready = sem("combT_ready")
        up_mm = sem("up_mm", E1)
        gelu_done = sem("gelu_done", 2 * E1)
        bc_mm = sem("bc_mm", E1)
        hs_ready = sem("hs_ready", E1)
        down_mm = sem("down_mm", E1)
        h2_ready = sem("h2_ready")
        x3r_ready = sem("x3r_ready")
        proj_mm = sem("proj_mm", 3)
        proj_out = sem("proj_out", 2)
        sel_ready = sem("sel_ready")
        relu_done = sem("relu_done", 2)
        egate = sem("egate", 3)
        rd_ready = sem("rd_ready")
        spread_ready = sem("spread_ready")
        so_mm = sem("so_mm")
        so_ready = sem("so_ready")
        wo1_mm = sem("wo1_mm")
        h3_ready = sem("h3_ready")
        msum_ready = sem("msum_ready")
        score_mm = sem("score_mm")
        sc_ready = sem("sc_ready")
        sc_exp = sem("sc_exp")
        gate_ready = sem("gate_ready")
        gate_mm = sem("gate_mm")
        gcol_ready = sem("gcol_ready")
        wsel_ready = sem("wsel_ready", 2)
        y2_mm = sem("y2_mm")
        fin_ready = sem("fin_ready")
        out_stored = sem("out_stored", 16)

        class Norm:
            def __init__(self, name):
                self.mean_mm = sem(name + "_mean_mm")
                self.centred = sem(name + "_centred")
                self.squared = sem(name + "_squared")
                self.var_mm = sem(name + "_var_mm")
                self.sd_ready = sem(name + "_sd_ready")
                self.ready = sem(name + "_ready")

        ln1, lny, ln2, ln3, ln4 = (Norm(n) for n in ("ln1", "lny", "ln2", "ln3", "ln4"))

        class Chain:
            def __init__(self, eng, s, per_image):
                self.eng, self.s, self.n, self.b, self.per_image = eng, s, 0, 0, per_image

            def start(self, b):
                self.n, self.b = 0, b

            def link(self, ins):
                self.n += 1
                ins.then_inc(self.s, 1)
                self.eng.wait_ge(self.s, self.b * self.per_image + self.n)

            def end(self):
                assert self.n == self.per_image, (self.n, self.per_image)

        front_step = sem("front_step", FRONT_STEPS)
        mem_step = sem("mem_step", MEM_STEPS)
        back_step = sem("back_step", BACK_STEPS)

        loads = [(tokw_s, tok_w), (vec_s, vecs), (wqkv_s, wqkv), (wo_s, wo), (wr_s, wr), (br_s, br), (w1_s, w1),
                 (w2_s, w2), (b2_s, b2), (wp_s, wp), (wo1_s, wo1), (wg_s, wg), (bg_s, bg), (enum_s, expert_numbers), (we_s, we), (be_s, be),
                 (ident_s, ident), (hmask_s, head_mask), (pick_s, tok_pick), (tri_s, tri), (erow_s, expert_rows),
                 (pos_s, pos)]
        NSET = 7

        block = ctx.enter_context(nc.Block())

        @block.sync
        def _(sp):
            def load_x(b):
                sp.dma_start(xb[:, :, :], x[bass.ds(b, 1)].rearrange("o p c n -> p (o c) n")).then_inc(x_in, 16)

            def load_txt(b):
                sp.dma_start(h0[:, LX:L], txt[bass.ds(b, 1)].rearrange("o p n -> p (o n)")).then_inc(txt_in, 16)

            def front(b, more):
                sp.wait_ge(qkv_out, (b + 1) * 3)
                sp.dma_start(qkv_d.rearrange("j d n -> (j d) n"),
                             qkvT[:, :, :].rearrange("p a n -> p (a n)")).then_inc(qkv_stored, 16)
                sp.wait_ge(qkv_stored, (b + 1) * 16)
                for a in range(3):
                    for j in range(H):
                        sp.dma_start(qkd[1:DH + 1, a, :, j * T:(j + 1) * T],
                                     qkv_d[j, :, a * L:(a + 1) * L].rearrange("d (h t) -> d h t", h=H))\
                          .then_inc(qkd_in[a], 16)
                if more:
                    sp.wait_ge(tok_mm, b + 1)
                    load_x(b + 1)
                sp.wait_ge(ctx_out, (b + 1) * H)
                sp.dma_start(ctx_d.rearrange("j d n -> d j n"), ctxu[:, :, :]).then_inc(ctx_stored, 16)
                sp.wait_ge(ctx_stored, (b + 1) * 16)
                sp.dma_start(cfm[:, :], ctx_d[:, 1:DH + 1, :]).then_inc(cfm_in, 16)
                sp.dma_start(den[:, :], ctx_d[:, 0:1, :].to_broadcast([H, DH, L])).then_inc(cfm_in, 16)
                if more:
                    sp.wait_ge(h1_ready, b + 1)
                    load_txt(b + 1)

            def back(b):
                sp.wait_ge(fin_ready, b + 1)
                sp.dma_start(out[bass.ds(b, 1)].rearrange("o p n -> p (o n)"), fin[:, :]).then_inc(out_stored, 16)

            for dst, src in loads:
                sp.dma_start(dst[:], src).then_inc(consts_in, 16)
            load_x(0)
            load_txt(0)
            front(0, True)
            with sp.Fori(1, B - 1) as b:
                front(b, True)
                back(b - 1)
            front(B - 1, False)
            back(B - 2)
            back(B - 1)
            sp.wait_ge(out_stored, B * 16)

        @block.tensor
        def _(pe):
            mm = nc.tensor.matmul

            def mean(n, src, b):
                mm(P[:, 0, 0:L], mean_w[:, :], src[:, :], start=True, stop=True).then_inc(n.mean_mm, 1)
                pe.wait_ge(n.squared, b + 1)
                mm(P[:, 1, 0:L], mean_w[:, :], sq[:, :], start=True, stop=True).then_inc(n.var_mm, 1)

            def front(b):
                pe.wait_ge(x_in, (b + 1) * 16)
                for c in range(KC):
                    last = mm(P[:, 7, 0:PATCHES], tokw_s[:, c, :], xb[:, c, :], start=(c == 0), stop=(c == KC - 1))
                last.then_inc(tok_mm, 1)
                pe.wait_ge(h0_ready, b + 1)
                pe.wait_ge(txt_in, (b + 1) * 16)
                mean(ln1, h0, b)
                pe.wait_ge(ln1.ready, b + 1)
                for a in range(3):
                    mm(P[:, 2 + a, 0:L], wqkv_s[:, a, :], xn1[:, :], start=True, stop=True).then_inc(qkv_mm, 1)
                def scores(h):
                    if h:
                        pe.wait_ge(max_ready, b * H + h)
                    for t, (k0, nk) in enumerate(KT):
                        last = mm(P[0:nk, t, 0:L], qkd[:, 0, h, k0:k0 + nk],
                                  qkd[:, 1, h, :], start=True, stop=True)
                    last.then_inc(s_mm, 1)

                def values(h):
                    pe.wait_ge(probs, b * H + h + 1)
                    if h:
                        pe.wait_ge(ctx_out, b * H + h)
                    for t, (k0, nk) in enumerate(KT):
                        last = mm(P[0:DH + 1, 6, 0:L], vaug[0:nk, h, t, :], pT[0:nk, t, :],
                                  start=(t == 0), stop=(t == 2))
                    last.then_inc(pv_mm, 1)

                pe.wait_ge(row_cleared, b + 1)
                pe.wait_ge(qkd_in[0], (b + 1) * 16 * H)
                pe.wait_ge(qkd_in[1], (b + 1) * 16 * H)
                pe.wait_ge(qkd_in[2], (b + 1) * 16 * H)
                scores(0)
                for h in range(H):
                    for t, (k0, nk) in enumerate(KT):
                        c = (h * 3 + t) * (DH + 1)
                        last = nc.tensor.transpose(P[0:nk, 7, c:c + DH + 1],
                                                   qkd[:, 2, h, k0:k0 + nk],
                                                   ident_s[0:DH + 1, 0:DH + 1])
                last.then_inc(v_tr, 1)
                pe.wait_ge(vaug_ready, b + 1)
                for h in range(H):
                    pe.wait_ge(max_ready, b * H + h + 1)
                    if h:
                        pe.wait_ge(max_row, b * H + h)
                    for t, (k0, nk) in enumerate(KT):
                        last = nc.tensor.transpose(P[0:1, 7, t * RT:t * RT + nk], nmx[0:nk, t:t + 1],
                                                   ident_s[0:nk, 0:nk])
                    last.then_inc(max_tr, 1)
                    if h + 1 < H:
                        scores(h + 1)
                    pe.wait_ge(max_row, b * H + h + 1)
                    if h:
                        pe.wait_ge(probs, b * H + h)
                    for t, (k0, nk) in enumerate(KT):
                        last = mm(P[0:nk, 3 + t, 0:L], qkd[:, 1, h, k0:k0 + nk],
                                  qkd[:, 0, h, :], start=True, stop=True)
                    last.then_inc(st_mm, 1)
                    values(h)
                pe.wait_ge(cfm_ready, b + 1)
                mm(P[:, 2, 0:L], wo_s[:, :], cfm[:, :], start=True, stop=True).then_inc(wo_mm, 1)
                pe.wait_ge(y1_ready, b + 1)
                mean(lny, y1, b)
                pe.wait_ge(h1_ready, b + 1)
                mean(ln2, h1, b)
                pe.wait_ge(ln2.ready, b + 1)
                for t, s in RTILES:
                    last = mm(P[0:RT, 7, t * E1:(t + 1) * E1], x2[:, s:s + RT], wr_s[:, :], start=True, stop=True)
                last.then_inc(router_mm, 1)
                pe.wait_ge(comb_ready, b + 1)
                for t, s in RTILES:
                    last = nc.tensor.transpose(P[0:E1, 7, s:s + RT], comb[:, t, :], ident_s[0:RT, 0:RT])
                last.then_inc(comb_tr, 1)

                def up(e):
                    if e >= 2:
                        pe.wait_ge(gelu_done, b * (2 * E1) + 2 * (e - 1))
                    for k in range(2):
                        last = mm(P[:, 2 * (e % 2) + k, 0:L], w1_s[:, e, k * D:(k + 1) * D], x2[:, :],
                                  start=True, stop=True)
                    last.then_inc(up_mm, 1)

                up(0)
                pe.wait_ge(combT_ready, b + 1)
                mm(P[:, 6, 0:L], b2_s[:, :], combT[:, :], start=True, stop=False)
                for e in range(E1):
                    if e + 1 < E1:
                        up(e + 1)
                    if e >= 2:
                        pe.wait_ge(hs_ready, b * E1 + e - 1)
                    mm(P[:, 4 + e % 2, 0:L], erow_s[:, e, :], combT[:, :], start=True, stop=True).then_inc(bc_mm, 1)
                    pe.wait_ge(hs_ready, b * E1 + e + 1)
                    for k in range(2):
                        last = mm(P[:, 6, 0:L], w2_s[:, e, k, :], hs[:, e % 2, k, :],
                                  start=False, stop=(e == E1 - 1 and k == 1))
                    last.then_inc(down_mm, 1)

            def project(b):
                pe.wait_ge(h2_ready, b + 1)
                mean(ln3, h2, b)
                pe.wait_ge(ln3.ready, b + 1)
                for t in range(2):
                    mm(P[:, 2 + t, 0:3 * D + H], x3[:, t * 128:(t + 1) * 128], wp_s[:, :],
                       start=True, stop=True).then_inc(proj_mm, 1)
                pe.wait_ge(x3r_ready, b + 1)
                mm(P[:, 4, 0:3 * D + H], x3r[:, :, :], wp_s[:, :], start=True, stop=True).then_inc(proj_mm, 1)

            def back(b):
                pe.wait_ge(rd_ready, b + 1)
                for t in range(2):
                    nc.tensor.transpose(P[:, 2, t * 128:(t + 1) * 128],
                                        rd[:, t * H:(t + 1) * H, :].rearrange("p g v -> p (g v)"), ident_s[:, :])
                pe.wait_ge(spread_ready, b + 1)
                mm(P[:, 2, TOK2:L], spread[:, :, :].rearrange("p g v -> p (g v)"), pick_s[:, :],
                   start=True, stop=True).then_inc(so_mm, 1)
                pe.wait_ge(so_ready, b + 1)
                mm(P[:, 3, 0:L], wo1_s[:, :], so[:, :], start=True, stop=True).then_inc(wo1_mm, 1)
                pe.wait_ge(h3_ready, b + 1)
                mean(ln4, h3, b)
                pe.wait_ge(msum_ready, b + 1)
                mm(P[0:1, 7, 0:E2], msum[:, :], wg_s[:, :], start=True, stop=True).then_inc(score_mm, 1)
                pe.wait_ge(gate_ready, b + 1)
                mm(P[:, 4, 0:1], ones_row[:, :], stat[:, 3:4], start=True, stop=True).then_inc(gate_mm, 1)
                pe.wait_ge(wsel_ready, (b + 1) * 2)
                mm(P[:, 5, 0:L], wsel[:, :], x4[:, :], start=True, stop=True).then_inc(y2_mm, 1)

            pe.wait_ge(consts_in, 16 * len(loads))
            pe.wait_ge(consts_set, NSET)
            front(0)
            project(0)
            with pe.Fori(1, B) as b:
                front(b)
                back(b - 1)
                project(b)
            back(B - 1)

        @block.gpsimd
        def _(pool):
            pool.memset(zero_row[:, :], 0.0).then_inc(zeros_set, 1)
            pool.memset(qkd[0:1, 0, :, :], 0.0).then_inc(row_cleared, 1)
            pool.wait_ge(zeros_set, 1)
            zeros = zero_row[:, :].unsqueeze(1).to_broadcast([1, H, L])
            with pool.Fori(0, B - 1) as b:
                pool.wait_ge(st_mm, (b + 1) * H)
                nc.gpsimd.tensor_tensor(qkd[0:1, 0, :, :], zeros, zeros, ALU.add).then_inc(row_cleared, 1)

        @block.scalar
        def _(act):
            A = nc.scalar.activation

            def norm(n, b):
                act.wait_ge(n.centred, b + 1)
                A(sq[:, :], xc[:, :], ACT.Square).then_inc(n.squared, 1)
                act.wait_ge(n.var_mm, b + 1)
                A(sd[:, :], P[:, 1, 0:L], ACT.Sqrt, bias=eps_s[:, :]).then_inc(n.sd_ready, 1)

            def front(b):
                norm(ln1, b)
                for a, name in enumerate(("bq", "bk", "bv")):
                    act.wait_ge(qkv_mm, b * 3 + a + 1)
                    A(qkvT[:, a, :], P[:, 2 + a, 0:L], ACT.Identity, bias=vec(name)).then_inc(qkv_out, 1)
                for h in range(H):
                    act.wait_ge(max_tr, b * H + h + 1)
                    A(qkd[0:1, 0, h, :], P[0:1, 7, 0:L], ACT.Copy).then_inc(max_row, 1)
                    act.wait_ge(st_mm, b * H + h + 1)
                    if h:
                        act.wait_ge(pv_mm, b * H + h)
                    A(pT[:, :, :], P[0:RT, 3:6, 0:L], ACT.Exp, scale=DH ** -0.5).then_inc(probs, 1)
                    act.wait_ge(pv_mm, b * H + h + 1)
                    A(ctxu[:, :, h * T:(h + 1) * T], P[0:DH + 1, 6, 0:L].rearrange("p (j t) -> p j t", j=H),
                      ACT.Copy).then_inc(ctx_out, 1)
                norm(lny, b)
                act.wait_ge(lny.ready, b + 1)
                A(z2[:, :], z1[:, :], ACT.Identity, bias=vec("beta"), scale=vec("gamma")).then_inc(z_ready, 1)
                norm(ln2, b)
                act.wait_ge(lg_ready, b + 1)
                A(ex[:, :, :], lg[:, :, :], ACT.Exp).then_inc(ex_ready, 1)
                act.wait_ge(comb_tr, b + 1)
                A(combT[:, :], P[0:E1, 7, 0:L], ACT.Copy).then_inc(combT_ready, 1)
                for e in range(E1):
                    act.wait_ge(up_mm, b * E1 + e + 1)
                    if e >= 2:
                        act.wait_ge(hs_ready, b * E1 + e - 1)
                    for k in range(2):
                        A(gl[:, e % 2, k, :], P[:, 2 * (e % 2) + k, 0:L], ACT.Gelu,
                          bias=vec(f"b1_{2 * e + k}")).then_inc(gelu_done, 1)

            def project(b):
                norm(ln3, b)
                act.wait_ge(ln3.ready, b + 1)
                A(x3r[:, :, :], x3[:, TOK2:L].unsqueeze(1).to_broadcast([128, H, LEFT]), ACT.Copy).then_inc(x3r_ready, 1)
                for t in range(2):
                    act.wait_ge(proj_mm, b * 3 + t + 1)
                    qk = P[:, 2 + t, 0:2 * D].rearrange("p (a h d) -> p a h d", a=2, h=H)
                    g = slice(t * H, (t + 1) * H)
                    A(relu[:, :, g, 0:DH], qk, ACT.Relu)
                    A(relu[:, :, g, DH:PHI], qk, ACT.Relu, scale=-1.0)
                    A(val[:, g, :], P[:, 2 + t, 2 * D:3 * D].rearrange("p (h d) -> p h d", h=H), ACT.Copy)
                    A(bta[:, g], P[:, 2 + t, 3 * D:3 * D + H], ACT.Exp, scale=-1.0).then_inc(egate, 1)
                act.wait_ge(sel_ready, b + 1)
                qk = sel[:, 0:2 * DH].rearrange("p (a d) -> p a d", a=2)
                A(relu[:, :, G - 1, 0:DH], qk, ACT.Relu)
                A(relu[:, :, G - 1, DH:PHI], qk, ACT.Relu, scale=-1.0)
                A(val[:, G - 1, :], sel[:, 2 * DH:3 * DH], ACT.Copy)
                A(bta[:, G - 1:G], sel[:, 3 * DH:3 * DH + 1], ACT.Exp, scale=-1.0).then_inc(egate, 1)

            def back(b):
                act.wait_ge(so_mm, b + 1)
                A(so[:, :], P[:, 2, 0:L], ACT.Copy).then_inc(so_ready, 1)
                norm(ln4, b)
                act.wait_ge(sc_ready, b + 1)
                A(sc[:, :], sc[:, :], ACT.Exp, accum_out=stat[:, 1:2]).then_inc(sc_exp, 1)
                act.wait_ge(gate_mm, b + 1)
                A(gcol[:, :], P[:, 4, 0:1], ACT.Copy).then_inc(gcol_ready, 1)
                e = act.value_load(topi[0:1, 0:1], min_val=0, max_val=E2 - 1)
                act.wait_ge(gcol_ready, b + 1)
                A(wsel[:, :], we_s[:, bass.ds(e * D, D)], ACT.Copy, scale=gcol[:, :]).then_inc(wsel_ready, 1)
                A(bsel[:, :], be_s[:, bass.ds(e, 1)], ACT.Copy, scale=gcol[:, :]).then_inc(wsel_ready, 1)

            act.wait_ge(consts_in, 16 * len(loads))
            act.wait_ge(consts_set, NSET)
            front(0)
            project(0)
            with act.Fori(1, B) as b:
                front(b)
                back(b - 1)
                project(b)
            back(B - 1)

        @block.vector
        def _(dve):
            V = nc.vector
            fc = Chain(dve, front_step, FRONT_STEPS)
            mc = Chain(dve, mem_step, MEM_STEPS)
            bc = Chain(dve, back_step, BACK_STEPS)

            def norm(n, src, dst, b, chain):
                dve.wait_ge(n.mean_mm, b + 1)
                V.tensor_tensor(xc[:, :], src[:, :], P[:, 0, 0:L], ALU.subtract).then_inc(n.centred, 1)
                dve.wait_ge(n.sd_ready, b + 1)
                chain.link(V.reciprocal(rs[:, :], sd[:, :]))
                V.tensor_tensor(dst[:, :], xc[:, :], rs[:, :], ALU.mult).then_inc(n.ready, 1)

            def step(g):
                def k(a):
                    return khqh[:, a, g, :].unsqueeze(1).to_broadcast([128, DH, PHI])
                m = mem[:, g, :, :]
                mc.link(V.tensor_tensor(tmp[:, :, :], m, k(1), ALU.mult))
                mc.link(V.tensor_reduce(cc[:, :], tmp[:, :, :], AX.X, ALU.add))
                mc.link(V.tensor_tensor(cc[:, :], val[:, g, :], cc[:, :], ALU.subtract))
                mc.link(V.scalar_tensor_tensor(tmp[:, :, :], cc[:, :].unsqueeze(2).to_broadcast([128, DH, PHI]),
                                               bta[:, g:g + 1], k(1), ALU.mult, ALU.mult))
                mc.link(V.tensor_tensor(m, m, tmp[:, :, :], ALU.add))
                mc.link(V.tensor_tensor(tmp[:, :, :], m, k(0), ALU.mult))
                last = V.tensor_reduce(rd[:, g, :], tmp[:, :, :], AX.X, ALU.add)
                if g < G - 1:
                    mc.link(last)
                else:
                    last.then_inc(rd_ready, 1)

            def front(b, c):
                fc.start(b)
                dve.wait_ge(tok_mm, b + 1)
                V.tensor_tensor(h0[:, 1:LX], P[:, 7, 0:PATCHES], pos_s[:, 1:LX], ALU.add).then_inc(h0_ready, 1)
                dve.wait_ge(h0_ready, b + 1)
                dve.wait_ge(txt_in, (b + 1) * 16)
                norm(ln1, h0, xn1, b, fc)
                dve.wait_ge(v_tr, b + 1)
                pv = P[0:RT, 7, 0:H * 3 * (DH + 1)].rearrange("p (h t d) -> p h t d", h=H, t=3)
                V.tensor_copy(vaug[:, :, :, :], pv).then_inc(vaug_ready, 1)
                if c is not None:
                    mc.start(c)
                for h in range(H):
                    dve.wait_ge(s_mm, b * H + h + 1)
                    if h:
                        dve.wait_ge(max_tr, b * H + h)
                    V.tensor_reduce(nmx[:, :], P[0:RT, 0:3, 0:L], AX.X, ALU.max, negate=True).then_inc(max_ready, 1)
                    if c is not None:
                        step(h)
                dve.wait_ge(cfm_in, (b + 1) * 32)
                fc.link(V.reciprocal(den[:, :], den[:, :]))
                V.tensor_tensor(cfm[:, :], cfm[:, :], den[:, :], ALU.mult).then_inc(cfm_ready, 1)
                dve.wait_ge(wo_mm, b + 1)
                V.scalar_tensor_tensor(y1[:, :], P[:, 2, 0:L], vec("bo"), xn1[:, :], ALU.add, ALU.add).then_inc(y1_ready, 1)
                dve.wait_ge(y1_ready, b + 1)
                norm(lny, y1, z1, b, fc)
                dve.wait_ge(z_ready, b + 1)
                V.tensor_tensor(h1[:, :], h0[:, :], z2[:, :], ALU.add).then_inc(h1_ready, 1)
                dve.wait_ge(h1_ready, b + 1)
                norm(ln2, h1, x2, b, fc)
                dve.wait_ge(router_mm, b + 1)
                fc.link(V.tensor_tensor(lg[:, :, :], P[0:RT, 7, 0:3 * E1].rearrange("p (t e) -> p t e", t=3),
                                        br_s[0:RT, :].unsqueeze(1).to_broadcast([RT, 3, E1]), ALU.add))
                fc.link(V.tensor_reduce(r8[:, :], lg[:, :, :], AX.X, ALU.max))
                V.tensor_tensor(lg[:, :, :], lg[:, :, :], r8[:, :].unsqueeze(2).to_broadcast([RT, 3, E1]),
                                ALU.subtract).then_inc(lg_ready, 1)
                dve.wait_ge(ex_ready, b + 1)
                fc.link(V.tensor_reduce(r8[:, :], ex[:, :, :], AX.X, ALU.add))
                fc.link(V.reciprocal(r8[:, :], r8[:, :]))
                fc.link(V.tensor_tensor(ex[:, :, :], ex[:, :, :], r8[:, :].unsqueeze(2).to_broadcast([RT, 3, E1]),
                                        ALU.mult))
                mine = ex[:, :, :].unsqueeze(3).to_broadcast([RT, 3, E1, E1])
                other = ex[:, :, :].unsqueeze(2).to_broadcast([RT, 3, E1, E1])
                fc.link(V.tensor_tensor(cmp1[:, :, :, :], other, mine, ALU.is_gt))
                fc.link(V.tensor_tensor(cmp2[:, :, :, :], other, mine, ALU.is_equal))
                fc.link(V.tensor_tensor(cmp2[:, :, :, :], cmp2[:, :, :, :],
                                        tri_s[0:RT, :, :].unsqueeze(1).to_broadcast([RT, 3, E1, E1]), ALU.mult))
                fc.link(V.tensor_tensor(cmp1[:, :, :, :], cmp1[:, :, :, :], cmp2[:, :, :, :], ALU.add))
                fc.link(V.tensor_reduce(rank[:, :, :], cmp1[:, :, :, :], AX.X, ALU.add))
                V.scalar_tensor_tensor(comb[:, :, :], rank[:, :, :], 2.0, ex[:, :, :], ALU.is_lt, ALU.mult)\
                 .then_inc(comb_ready, 1)
                for e in range(E1):
                    dve.wait_ge(gelu_done, b * (2 * E1) + 2 * e + 2)
                    dve.wait_ge(bc_mm, b * E1 + e + 1)
                    if e >= 2:
                        dve.wait_ge(down_mm, b * E1 + e - 1)
                    V.tensor_tensor(hs[:, e % 2, :, :], gl[:, e % 2, :, :],
                                    P[:, 4 + e % 2, 0:L].unsqueeze(1).to_broadcast([128, 2, L]), ALU.mult)\
                     .then_inc(hs_ready, 1)
                    if c is not None:
                        step(H + e)

            def memory_end(c):
                step(G - 1)
                mc.end()

            def project(b):
                dve.wait_ge(down_mm, (b + 1) * E1)
                V.tensor_tensor(h2[:, :], h1[:, :], P[:, 6, 0:L], ALU.add).then_inc(h2_ready, 1)
                dve.wait_ge(h2_ready, b + 1)
                norm(ln3, h2, x3, b, fc)
                dve.wait_ge(proj_mm, (b + 1) * 3)
                hm = hmask_s[:, :]
                m4 = msk[:, 0:3 * D].rearrange("p (a h d) -> p a h d", a=3, h=H)
                p4 = P[:, 4, 0:3 * D].rearrange("p (a h d) -> p a h d", a=3, h=H)
                fc.link(V.tensor_tensor(m4, p4, hm.unsqueeze(1).unsqueeze(3).to_broadcast([128, 3, H, DH]), ALU.mult))
                fc.link(V.tensor_tensor(msk[:, 3 * D:], P[:, 4, 3 * D:3 * D + H], hm, ALU.mult))
                fc.link(V.tensor_reduce(sel[:, 0:3 * DH].rearrange("p (a d) -> p a d", a=3),
                                        m4.rearrange("p a h d -> p a d h"), AX.X, ALU.add))
                V.tensor_reduce(sel[:, 3 * DH:3 * DH + 1], msk[:, 3 * D:], AX.X, ALU.add).then_inc(sel_ready, 1)
                dve.wait_ge(egate, (b + 1) * 3)
                fc.link(V.tensor_scalar(bta[:, :], bta[:, :], 1.0, None, ALU.add))
                fc.link(V.reciprocal(bta[:, :], bta[:, :]))
                fc.link(V.tensor_tensor(feat[:, :, :, 1:PHI], relu[:, :, :, 1:PHI], relu[:, :, :, 0:PHI - 1], ALU.mult))
                fc.link(V.tensor_tensor(feat[:, :, :, 0:1], relu[:, :, :, 0:1], relu[:, :, :, PHI - 1:PHI], ALU.mult))
                fc.link(V.tensor_reduce(fsum[:, :, :], feat[:, :, :, :], AX.X, ALU.add))
                fc.link(V.tensor_scalar(fsum[:, :, :], fsum[:, :, :], 1e-6, None, ALU.add))
                fc.link(V.reciprocal(fsum[:, :, :], fsum[:, :, :]))
                fc.link(V.tensor_tensor(khqh[:, :, :, :], feat[:, :, :, :],
                                        fsum[:, :, :].unsqueeze(3).to_broadcast([128, 2, G, PHI]), ALU.mult))
                fc.end()

            def back(b, stored=True):
                bc.start(b)
                dve.wait_ge(rd_ready, b + 1)
                V.tensor_tensor(spread[:, :, :], rd[:, G - 1, :].unsqueeze(1).to_broadcast([128, H, DH]),
                                hmask_s[:, :].unsqueeze(2).to_broadcast([128, H, DH]), ALU.mult).then_inc(spread_ready, 1)
                dve.wait_ge(wo1_mm, b + 1)
                V.scalar_tensor_tensor(h3[:, :], P[:, 3, 0:L], vec("bo1"), h2[:, :], ALU.add, ALU.add).then_inc(h3_ready, 1)
                dve.wait_ge(h3_ready, b + 1)
                norm(ln4, h3, x4, b, bc)
                dve.wait_ge(ln4.ready, b + 1)
                V.tensor_reduce(msum[:, :], x4[:, :], AX.X, ALU.add).then_inc(msum_ready, 1)
                dve.wait_ge(score_mm, b + 1)
                bc.link(V.scalar_tensor_tensor(sc[:, :], P[0:1, 7, 0:E2], 1.0 / L, bg_s[:, :], ALU.mult, ALU.add))
                bc.link(V.tensor_reduce(stat[:, 0:1], sc[:, :], AX.X, ALU.max))
                V.tensor_scalar(sc[:, :], sc[:, :], stat[:, 0:1], None, ALU.subtract).then_inc(sc_ready, 1)
                dve.wait_ge(sc_exp, b + 1)
                bc.link(V.reciprocal(stat[:, 2:3], stat[:, 1:2]))
                bc.link(V.tensor_scalar(sc[:, :], sc[:, :], stat[:, 2:3], None, ALU.mult))
                bc.link(V.tensor_reduce(stat[:, 3:4], sc[:, :], AX.X, ALU.max))
                bc.link(V.tensor_scalar(notbest[:, :], sc[:, :], stat[:, 3:4], float(E2), ALU.is_lt, ALU.mult))
                bc.link(V.tensor_tensor(notbest[:, :], notbest[:, :], enum_s[:, :], ALU.add))
                bc.link(V.tensor_reduce(best[:, :], notbest[:, :], AX.X, ALU.min))
                V.tensor_copy(topi[:, :], best[:, :]).then_inc(gate_ready, 1)
                dve.wait_ge(y2_mm, b + 1)
                dve.wait_ge(wsel_ready, (b + 1) * 2)
                if stored:
                    dve.wait_ge(out_stored, b * 16)
                V.scalar_tensor_tensor(fin[:, :], P[:, 5, 0:L], bsel[:, :], h3[:, :], ALU.add, ALU.add)\
                 .then_inc(fin_ready, 1)
                bc.end()

            V.memset(mean_w[:, :], 1.0 / D).then_inc(consts_set, 1)
            V.memset(ones_row[:, :], 1.0).then_inc(consts_set, 1)
            V.memset(eps_s[:, :], 1e-5).then_inc(consts_set, 1)
            V.memset(qkd[0:1, 1:3, :, :], 1.0).then_inc(consts_set, 1)
            V.memset(mem[:, :, :, :], 0.0).then_inc(consts_set, 1)
            V.memset(P[:, :, :], 0.0).then_inc(consts_set, 1)
            dve.wait_ge(consts_in, 16 * len(loads))
            dve.wait_ge(consts_set, 6)
            V.tensor_scalar(pos_s[:, 1:LX], pos_s[:, 1:LX], vec("tok_b"), None, ALU.add).then_inc(consts_done, 1)
            V.tensor_scalar(h0[:, 0:1], pos_s[:, 0:1], vec("cls"), None, ALU.add).then_inc(consts_set, 1)
            dve.wait_ge(consts_done, 1)
            dve.wait_ge(consts_set, NSET)
            front(0, None)
            project(0)
            front(1, 0)
            memory_end(0)
            back(0, stored=False)
            project(1)
            with dve.Fori(2, B) as b:
                front(b, b - 1)
                memory_end(b - 1)
                back(b - 1)
                project(b)
            mc.start(B - 1)
            for g in range(G - 1):
                step(g)
            memory_end(B - 1)
            back(B - 1)


_OUT = (B, D, L)


def kernel(**inputs):
    import numpy as np
    import concourse.bacc as bacc
    from concourse.bass_utils import run_bass_kernel_spmd

    a = {k: np.asarray(v) for k, v in inputs.items()}

    def col(v):
        return v.reshape(-1, 128).T

    xs = a["x"].reshape(B, 3, 11, 16, 13, 16).transpose(0, 3, 5, 1, 2, 4).reshape(B, KC, 128, PATCHES)
    vecs = [a["L0_tok_b"], a["L0_tok_cls_token"].reshape(D), a["L0_attn_bq"], a["L0_attn_bk"], a["L0_attn_bv"],
            a["L0_attn_bo"], a["L0_attn_gamma"], a["L0_attn_beta"], a["L1_attn_bo"]]
    feeds = [
        ("x", xs.transpose(0, 2, 1, 3)),
        ("txt", a["txt"].transpose(0, 2, 1)),
        ("tok_w", a["L0_tok_W"].T.reshape(KC, 128, D).transpose(1, 0, 2)),
        ("pos", np.broadcast_to(a["L0_tok_pos_emb"].reshape(1, LX), (128, LX))),
        ("vecs", np.concatenate([v.reshape(D, 1) for v in vecs] + [col(a["L0_ffn_b1"].reshape(-1))], axis=1)),
        ("wqkv", np.stack([a["L0_attn_Wq"].T, a["L0_attn_Wk"].T, a["L0_attn_Wv"].T], axis=1)),
        ("wo", a["L0_attn_Wo"].T),
        ("wr", a["L0_ffn_Wr"].T),
        ("br", np.broadcast_to(a["L0_ffn_br"].reshape(1, E1), (128, E1))),
        ("w1", a["L0_ffn_W1"].transpose(1, 0, 2)),
        ("w2", a["L0_ffn_W2"].reshape(E1, 2, 128, D).transpose(2, 0, 1, 3)),
        ("b2", a["L0_ffn_b2"]),
        ("wp", np.concatenate([a["L1_attn_Wq"], a["L1_attn_Wk"], a["L1_attn_Wv"], a["L1_attn_Wg"]], axis=1)),
        ("wo1", a["L1_attn_Wo"]),
        ("wg", a["L1_ffn_Wg"]),
        ("bg", a["L1_ffn_bg"].reshape(1, E2)),
        ("we", a["L1_ffn_We"].transpose(1, 0, 2).reshape(D, E2 * D)),
        ("be", a["L1_ffn_be"].T),
        ("ident", np.eye(128, dtype=np.float32)),
        ("head_mask", np.repeat(np.eye(H, dtype=np.float32), LEFT, axis=0)),
        ("tok_pick", np.tile(np.eye(LEFT, dtype=np.float32), (H, 1))),
        ("tri", np.broadcast_to(np.tri(E1, k=-1, dtype=np.float32), (128, E1, E1))),
        ("expert_rows", np.repeat(np.eye(E1, dtype=np.float32)[:, :, None], 128, axis=2)),
        ("expert_numbers", np.arange(E2, dtype=np.float32).reshape(1, E2)),
    ]
    nc = bacc.Bacc("TRN2", target_bir_lowering=False, num_devices=1)
    arrays, args = {}, []
    for name, v in feeds:
        v = np.ascontiguousarray(v)
        arrays[f"in_{name}"] = v
        args.append(nc.dram_tensor(f"in_{name}", v.shape, mybir.dt.from_np(v.dtype), kind="ExternalInput").ap())
    out = nc.dram_tensor("out", _OUT, mybir.dt.float32, kind="ExternalOutput").ap()
    early_fusion(nc, *args, out)
    r = run_bass_kernel_spmd(nc, [arrays], core_ids=[0])
    return np.ascontiguousarray(r.results[0]["out"].transpose(0, 2, 1))
```

```python
import concourse.bass as bass
from concourse import mybir
from contextlib import ExitStack

B = 64
D = 128
PATCHES = 143
LX = PATCHES + 1
TXT = 128
L = LX + TXT
KC = 768 // 128
H = 8
DH = D // H
T = L // H
HALF = L // 2
E1 = 8
HID = 256
E2 = 16
PHI = 2 * DH
FK = H * PHI
FW = 3 * FK + D
RT = -(-L // 3)
TILES = ((0, 0), (1, RT), (2, L - RT))
KT = ((0, RT), (RT, RT), (2 * RT, L - 2 * RT))
SUB = 32
PAIRS = 16
QUADS = PAIRS // 4
GRP = 4
ROUTER_STEPS, FEATURE_STEPS, SOLVE_STEPS, GATE_STEPS = 11, 11, 2 * (SUB - 1), 10
MAX_STEPS, PART_STEPS = 5, 3
PARTS = 3
PAIRED = ((0, 0), (0, 1), (0, 2), (1, 0), (1, 1), (2, 0))
BLOCKS = len(PAIRED) * DH
ROWS = BLOCKS + PARTS
VECS = ("tok_b", "cls", "bq", "bk", "bv", "bo", "gamma", "beta", "bo1") + tuple(f"b1_{i}" for i in range(2 * E1))
NV = len(VECS)


class Chain:

    def __init__(self, eng, s, per_round):
        self.eng, self.s, self.per_round, self.n, self.r = eng, s, per_round, 0, 0

    def start(self, r):
        self.n, self.r = 0, r

    def link(self, ins):
        self.n += 1
        ins.then_inc(self.s, 1)
        self.eng.wait_ge(self.s, self.r * self.per_round + self.n)

    def end(self):
        assert self.n == self.per_round, (self.n, self.per_round)


def known(b, least):
    return not isinstance(b, int) or b >= least


def images(nc, x, txt, tok_w, pos, vecs, wqkv, wo, wr, br, w1, w2, b2, wp, ident, tri, expert_rows, h2_d, feat_d):
    f32 = mybir.dt.float32
    bf16 = mybir.dt.bfloat16
    ALU = mybir.AluOpType
    ACT = mybir.ActivationFunctionType
    AX = mybir.AxisListType

    ctx = ExitStack()
    with ctx:
        def sb(name, shape, dt=f32):
            return ctx.enter_context(nc.sbuf_tensor(name, shape, dt))

        def sem(name):
            return ctx.enter_context(nc.semaphore(name))

        tokw_s = sb("tokw_s", [128, KC, D])
        vec_s = sb("vec_s", [128, NV])
        wqkv_s = sb("wqkv_s", [128, 3, D])
        wo_s = sb("wo_s", [128, D])
        wr_s = sb("wr_s", [128, E1])
        br_s = sb("br_s", [128, E1])
        w1_s = sb("w1_s", [128, E1, HID])
        w2_s = sb("w2_s", [128, E1, 2, D])
        b2_s = sb("b2_s", [E1, D])
        wp_s = sb("wp_s", [128, 3 * D + H])
        ident_s = sb("ident_s", [128, 128])
        tri_s = sb("tri_s", [128, E1, E1])
        erow_s = sb("erow_s", [E1, E1, 128])
        pos_s = sb("pos_s", [128, LX])
        mean_w = sb("mean_w", [128, 128])
        ones_s = sb("ones_s", [128, 128])
        eps_s = sb("eps_s", [128, 1])
        ident_h = sb("ident_h", [128, 128], bf16)

        def vec(name):
            i = VECS.index(name)
            return vec_s[:, i:i + 1]

        xb = sb("xb", [128, KC, PATCHES])
        h0 = sb("h0", [128, 2, L])
        xn1 = sb("xn1", [128, 2, L])
        xc = sb("xc", [128, 2, L])
        sq = sb("sq", [128, 2, L])
        sd = sb("sd", [RT, 2, 3])
        rstd = sb("rstd", [RT, 2, 3])
        diag = sb("diag", [RT, 2, 3, RT])
        qkvT = sb("qkvT", [128, 3, L])
        parts = sb("parts", [128, 2, PARTS, L], bf16)
        left = sb("left", [128, 2, L])
        qs = sb("qs", [ROWS, H, L], bf16)
        ks = sb("ks", [ROWS, H, L], bf16)
        vd = sb("vd", [DH + 1, H, L])
        vaug = sb("vaug", [RT, H, 3, DH + 1])
        nmx = sb("nmx", [RT, 3])
        nleft = sb("nleft", [RT, 3])
        nparts = sb("nparts", [RT, 2, 3, PARTS], bf16)
        pT = sb("pT", [RT, 2, 3, L])
        ctxu = sb("ctxu", [DH + 1, H, L])
        cfm = sb("cfm", [128, L])
        den = sb("den", [128, L])
        y1 = sb("y1", [128, L])
        z1 = sb("z1", [128, L])
        z2 = sb("z2", [128, L])
        h1 = sb("h1", [128, L])
        x2 = sb("x2", [128, L])
        lg = sb("lg", [RT, 3, E1])
        ex = sb("ex", [RT, 3, E1])
        r8 = sb("r8", [RT, 3])
        cmp1 = sb("cmp1", [RT, 3, E1, E1])
        cmp2 = sb("cmp2", [RT, 3, E1, E1])
        rank = sb("rank", [RT, 3, E1])
        comb = sb("comb", [RT, 3, E1])
        combT = sb("combT", [E1, L])
        gl = sb("gl", [128, 2, 2, L])
        hs = sb("hs", [128, 2, 2, L])
        h2 = sb("h2", [128, L])
        x3 = sb("x3", [128, L])
        relu = sb("relu", [RT, 3, 2, H, PHI])
        prod = sb("prod", [RT, 3, 2 * H, PHI])
        fsum = sb("fsum", [RT, 3, 2 * H])
        val = sb("val", [RT, 3, H, DH])
        bta = sb("bta", [RT, 3, H])
        feat = sb("feat", [RT, 3, FW])

        P = ctx.enter_context(nc.psum_tensor("P1", [128, 8, 512], f32))
        qk_d = nc.dram_tensor("qk_d", [DH, 2, PARTS, H, L], bf16).ap()
        v_d = nc.dram_tensor("v_d", [DH, H, L], f32).ap()
        ctx_d = nc.dram_tensor("ctx_d", [H, DH + 1, L], f32).ap()

        consts_in = sem("consts_in")
        consts_set = sem("consts_set")
        pos_ready = sem("pos_ready")
        x_in = sem("x_in")
        txt_in = sem("txt_in")
        tok_mm = sem("tok_mm")
        h0_ready = sem("h0_ready")
        q_mm = sem("q_mm")
        k_mm = sem("k_mm")
        v_mm = sem("v_mm")
        q_out = sem("q_out")
        k_out = sem("k_out")
        v_out = sem("v_out")
        parts_ready = sem("parts_ready")
        part_step = sem("part_step")
        max_step = sem("max_step")
        qk_stored = sem("qk_stored")
        v_stored = sem("v_stored")
        qk_in = sem("qk_in")
        v_in = sem("v_in")
        v_tr = sem("v_tr")
        vaug_ready = sem("vaug_ready")
        s_mm = sem("s_mm")
        max_tr = sem("max_tr")
        max_row = sem("max_row")
        st_mm = sem("st_mm")
        probs = sem("probs")
        pv_mm = sem("pv_mm")
        ctx_out = sem("ctx_out")
        ctx_stored = sem("ctx_stored")
        cfm_in = sem("cfm_in")
        den_in = sem("den_in")
        cfm_ready = sem("cfm_ready")
        wo_mm = sem("wo_mm")
        y1_ready = sem("y1_ready")
        z2_ready = sem("z2_ready")
        h1_ready = sem("h1_ready")
        router_mm = sem("router_mm")
        lg_ready = sem("lg_ready")
        ex_ready = sem("ex_ready")
        comb_ready = sem("comb_ready")
        comb_tr = sem("comb_tr")
        combT_ready = sem("combT_ready")
        up_mm = sem("up_mm")
        gelu_done = sem("gelu_done")
        bc_mm = sem("bc_mm")
        hs_ready = sem("hs_ready")
        down_mm = sem("down_mm")
        h2_ready = sem("h2_ready")
        h2_stored = sem("h2_stored")
        proj_mm = sem("proj_mm")
        proj_out = sem("proj_out")
        feat_ready = sem("feat_ready")
        feat_stored = sem("feat_stored")
        router_step = sem("router_step")
        feature_step = sem("feature_step")

        class Norm:

            def __init__(self, name, half):
                self.half = half
                self.mean_mm = sem(name + "_mean_mm")
                self.centred = sem(name + "_centred")
                self.squared = sem(name + "_squared")
                self.var_mm = sem(name + "_var_mm")
                self.sd_ready = sem(name + "_sd_ready")
                self.rstd_ready = sem(name + "_rstd_ready")
                self.diag_ready = sem(name + "_diag_ready")
                self.bc_mm = sem(name + "_bc_mm")
                self.ready = sem(name + "_ready")

        ln1, lny, ln2, ln3 = Norm("ln1", 0), Norm("lny", 1), Norm("ln2", 1), Norm("ln3", 0)

        loads = [(tokw_s, tok_w), (vec_s, vecs), (wqkv_s, wqkv), (wo_s, wo), (wr_s, wr), (br_s, br), (w1_s, w1),
                 (w2_s, w2), (b2_s, b2), (wp_s, wp), (ident_s, ident), (tri_s, tri), (erow_s, expert_rows),
                 (pos_s, pos)]
        NSET = 8

        block = ctx.enter_context(nc.Block())

        def schedule(round_):
            round_(0, 0, with_features=False, tail=False, experts=False, project=False)
            round_(1, 1, with_features=False, project=False)
            round_(2, 0, with_features=False)
            round_(3, 1)
            round_(4, 0)
            with round_.eng.Fori(5, B - 2, 2) as i:
                round_(i, 1)
                round_(i + 1, 0)
            round_(B - 1, 1, start=False)
            round_(B, 0, heads=False, start=False)
            round_(B + 1, 1, heads=False, start=False, tail=False, experts=False)
            round_(B + 2, 0, heads=False, start=False, tail=False, experts=False, project=False)

        @block.sync
        def _(sp):
            def at(b):
                return b if isinstance(b, int) else sp.snap(b)

            def load_x(b):
                sp.dma_start(xb[:, :, :], x[bass.ds(b, 1)].rearrange("o p c n -> p (o c) n")).then_inc(x_in, 16)

            def load_txt(b, p):
                sp.dma_start(h0[:, p, LX:L], txt[bass.ds(b, 1)].rearrange("o p n -> p (o n)")).then_inc(txt_in, 16)

            def relayout(b):
                sp.wait_ge(v_out, b + 1)
                for j in range(H):
                    sp.dma_start(v_d[:, :, j * T:(j + 1) * T],
                                 qkvT[j * DH:(j + 1) * DH, 2, :].rearrange("d (h t) -> d h t", h=H)).then_inc(v_stored, 16)
                sp.wait_ge(parts_ready, b + 1)
                for j in range(H):
                    sp.dma_start(qk_d[:, :, :, :, j * T:(j + 1) * T].rearrange("d a c h t -> d (a c) h t"),
                                 parts[j * DH:(j + 1) * DH, :, :, :].rearrange("d a c (h t) -> d (a c) h t", h=H))\
                      .then_inc(qk_stored, 16)
                sp.wait_ge(v_stored, (b + 1) * 16 * H)
                sp.dma_start(vd[1:DH + 1, :, :], v_d).then_inc(v_in, 16)
                sp.wait_ge(qk_stored, (b + 1) * 16 * H)
                for a, dst in ((0, qs), (1, ks)):
                    for n, pair in enumerate(PAIRED):
                        sp.dma_start(dst[n * DH:(n + 1) * DH, :, :], qk_d[:, a, pair[a], :, :]).then_inc(qk_in, 16)

            class Round:
                eng = sp

                def __call__(self, i, p, with_features=True, heads=True, tail=True, experts=True, start=True,
                             project=True):
                    ahead, behind, last = at(i + 1), at(i - 1), at(i - 3)
                    if start:
                        sp.wait_ge(tok_mm, i + 1)
                        load_x(ahead)
                    if start and known(i, 1):
                        if tail:
                            sp.wait_ge(h1_ready, i)
                        load_txt(ahead, 1 - p)
                    if heads:
                        if tail and not start:
                            sp.wait_ge(h1_ready, i)
                        sp.wait_ge(ctx_out, (i + 1) * H)
                        sp.dma_start(ctx_d.rearrange("j d n -> d j n"), ctxu[:, :, :]).then_inc(ctx_stored, 16)
                        sp.wait_ge(ctx_stored, (i + 1) * 16)
                        sp.dma_start(cfm[:, :], ctx_d[:, 1:DH + 1, :]).then_inc(cfm_in, 16)
                        sp.dma_start(den[:, :], ctx_d[:, 0:1, :].to_broadcast([H, DH, L])).then_inc(den_in, 16)
                    if start:
                        relayout(i + 1)
                    if with_features:
                        sp.wait_ge(feat_ready, i - 2)
                        for t, s in TILES:
                            r = 2 * RT - s if t == 2 else 0
                            sp.dma_start(feat_d[bass.ds(last, 1), s + r:s + RT, :].rearrange("o p n -> (o p) n"),
                                         feat[r:RT, t, :]).then_inc(feat_stored, 16)
                    if experts:
                        sp.wait_ge(h2_ready, i)
                        sp.dma_start(h2_d[bass.ds(behind, 1)].rearrange("o p n -> p (o n)"), h2[:, :])\
                          .then_inc(h2_stored, 16)

            for dst, src in loads:
                sp.dma_start(dst[:], src).then_inc(consts_in, 16)
            load_x(0)
            load_txt(0, 0)
            sp.wait_ge(txt_in, 16)
            load_txt(1, 1)
            relayout(0)
            schedule(Round())
            sp.wait_ge(h2_stored, B * 16)
            sp.wait_ge(feat_stored, B * 48)

        @block.tensor
        def _(pe):
            mm = nc.tensor.matmul

            def mean(n, src):
                mm(P[:, 6, 0:L], mean_w[:, :], src, start=True, stop=True).then_inc(n.mean_mm, 1)

            def variance(n, b):
                pe.wait_ge(n.squared, b + 1)
                for t, s in TILES:
                    last = mm(P[0:RT, 7, t:t + 1], sq[:, n.half, s:s + RT], mean_w[:, 0:1], start=True, stop=True)
                last.then_inc(n.var_mm, 1)

            def spread(n, b):
                pe.wait_ge(n.diag_ready, b + 1)
                for t, s in TILES:
                    last = mm(P[:, 7, s:s + RT], ones_s[0:RT, :], diag[:, n.half, t, :], start=True, stop=True)
                last.then_inc(n.bc_mm, 1)

            def begin(k, b, p):
                if k == 0:
                    pe.wait_ge(x_in, (b + 1) * 16)
                    for c in range(KC):
                        last = mm(P[:, 6, 0:PATCHES], tokw_s[:, c, :], xb[:, c, :], start=(c == 0), stop=(c == KC - 1))
                    last.then_inc(tok_mm, 1)
                elif k == 1:
                    pe.wait_ge(h0_ready, b + 1)
                    pe.wait_ge(txt_in, (b + 1) * 16)
                    mean(ln1, h0[:, p, :])
                elif k == 2:
                    variance(ln1, b)
                elif k == 4:
                    spread(ln1, b)
                elif k == 5:
                    pe.wait_ge(ln1.ready, b + 1)
                    mm(P[:, 6, 0:L], wqkv_s[:, 0, :], xn1[:, p, :], start=True, stop=True).then_inc(q_mm, 1)
                    mm(P[:, 7, 0:L], wqkv_s[:, 1, :], xn1[:, p, :], start=True, stop=True).then_inc(k_mm, 1)
                elif k == 6:
                    pe.wait_ge(q_out, b + 1)
                    mm(P[:, 6, 0:L], wqkv_s[:, 2, :], xn1[:, p, :], start=True, stop=True).then_inc(v_mm, 1)

            def finish(k, b, after_begin):
                if k == 7:
                    pe.wait_ge(h2_ready, b + 1)
                    if after_begin:
                        pe.wait_ge(v_out, b + 4)
                    else:
                        pe.wait_ge(proj_out, b * 3)
                    mean(ln3, h2[:, :])
                elif k == 8:
                    if after_begin:
                        pe.wait_ge(k_out, b + 4)
                    variance(ln3, b)
                elif k == 10:
                    spread(ln3, b)
                elif k == 11:
                    pe.wait_ge(ln3.ready, b + 1)
                    for t in range(2):
                        mm(P[0:RT, 6 + t, 0:3 * D + H], x3[:, t * RT:(t + 1) * RT], wp_s[:, :],
                           start=True, stop=True).then_inc(proj_mm, 1)
                elif k == 12:
                    pe.wait_ge(proj_out, b * 3 + 1)
                    mm(P[0:RT, 6, 0:3 * D + H], x3[:, L - RT:L], wp_s[:, :], start=True, stop=True).then_inc(proj_mm, 1)

            def middle(k, b):
                if k == 1:
                    pe.wait_ge(cfm_ready, b + 1)
                    if known(b, 2):
                        pe.wait_ge(proj_out, (b - 1) * 3)
                    mm(P[:, 6, 0:L], wo_s[:, :], cfm[:, :], start=True, stop=True).then_inc(wo_mm, 1)
                elif k == 2:
                    pe.wait_ge(y1_ready, b + 1)
                    mean(lny, y1[:, :])
                elif k == 3:
                    variance(lny, b)
                elif k == 5:
                    spread(lny, b)
                elif k == 8:
                    pe.wait_ge(h1_ready, b + 1)
                    mean(ln2, h1[:, :])
                elif k == 9:
                    variance(ln2, b)
                elif k == 11:
                    spread(ln2, b)
                elif k == 12:
                    pe.wait_ge(ln2.ready, b + 1)
                    for t, s in TILES:
                        last = mm(P[0:RT, 7, t * E1:(t + 1) * E1], x2[:, s:s + RT], wr_s[:, :], start=True, stop=True)
                    last.then_inc(router_mm, 1)
                elif k == 15:
                    pe.wait_ge(comb_ready, b + 1)
                    for t, s in TILES:
                        last = nc.tensor.transpose(P[0:E1, 6, s:s + RT], comb[:, t, :], ident_s[0:RT, 0:RT])
                    last.then_inc(comb_tr, 1)

            def scores(b, h):
                for a in range(2):
                    for t, (k0, nk) in enumerate(KT):
                        last = mm(P[0:nk, a, t * HALF:(t + 1) * HALF], qs[0:BLOCKS, h, k0:k0 + nk],
                                  ks[0:BLOCKS, h, a * HALF:(a + 1) * HALF], start=True, stop=True)
                last.then_inc(s_mm, 1)

            def shifted(b, h):
                pe.wait_ge(max_row, b * H + h + 1)
                if h:
                    pe.wait_ge(probs, b * H + h)
                for a in range(2):
                    for t, (k0, nk) in enumerate(KT):
                        last = mm(P[0:nk, 2 + a, t * HALF:(t + 1) * HALF], ks[:, h, k0:k0 + nk],
                                  qs[:, h, a * HALF:(a + 1) * HALF], start=True, stop=True)
                last.then_inc(st_mm, 1)

            def values(b, h):
                pe.wait_ge(probs, b * H + h + 1)
                if h:
                    pe.wait_ge(ctx_out, b * H + h)
                for t, (k0, nk) in enumerate(KT):
                    last = mm(P[0:DH + 1, 4, 0:L], vaug[0:nk, h, t, :], pT[0:nk, h % 2, t, :],
                              start=(t == 0), stop=(t == 2))
                last.then_inc(pv_mm, 1)

            def up(b, e):
                if e >= 2:
                    pe.wait_ge(gelu_done, b * 2 * E1 + 2 * (e - 1))
                for k in range(2):
                    last = mm(P[:, 2 * (e % 2) + k, 0:L], w1_s[:, e, k * D:(k + 1) * D], x2[:, :],
                              start=True, stop=True)
                last.then_inc(up_mm, 1)

            def down(b, e):
                pe.wait_ge(hs_ready, b * E1 + e + 1)
                for k in range(2):
                    last = mm(P[:, 5, 0:L], w2_s[:, e, k, :], hs[:, e % 2, k, :],
                              start=False, stop=(e == E1 - 1 and k == 1))
                last.then_inc(down_mm, 1)

            def maxima(b, h):
                pe.wait_ge(max_step, (b * H + h + 1) * MAX_STEPS)
                if h:
                    pe.wait_ge(max_row, b * H + h)
                for t, (k0, nk) in enumerate(KT):
                    last = mm(P[0:PARTS, 5, k0:k0 + nk], nparts[0:nk, h % 2, t, :], ident_h[0:nk, 0:nk],
                              start=True, stop=True)
                last.then_inc(max_tr, 1)

            class Round:
                eng = pe

                def __call__(self, i, p, with_features=True, heads=True, tail=True, experts=True, start=True,
                             project=True):
                    if heads:
                        pe.wait_ge(qk_in, (i + 1) * 16 * 2 * len(PAIRED))
                        pe.wait_ge(v_in, (i + 1) * 16)
                        if known(i, 2):
                            pe.wait_ge(h2_ready, i - 1)
                        scores(i, 0)
                        for h in range(H):
                            for t, (k0, nk) in enumerate(KT):
                                c = (h * 3 + t) * (DH + 1)
                                last = nc.tensor.transpose(P[0:nk, 5, c:c + DH + 1], vd[:, h, k0:k0 + nk],
                                                           ident_s[0:DH + 1, 0:DH + 1])
                        last.then_inc(v_tr, 1)
                        pe.wait_ge(vaug_ready, i + 1)
                        maxima(i, 0)
                    for h in range(H):
                        if heads and h + 1 < H:
                            scores(i, h + 1)
                        if heads and h:
                            values(i, h - 1)
                        if tail:
                            middle(2 * h, i - 1)
                        if heads and h + 1 < H:
                            maxima(i, h + 1)
                        if heads:
                            shifted(i, h)
                        if tail:
                            middle(2 * h + 1, i - 1)
                    if heads:
                        values(i, H - 1)
                    if experts:
                        up(i - 1, 0)
                        pe.wait_ge(combT_ready, i)
                        if heads:
                            pe.wait_ge(ctx_out, (i + 1) * H)
                        mm(P[:, 5, 0:L], b2_s[:, :], combT[:, :], start=True, stop=False)
                    for e in range(E1):
                        if experts:
                            if e + 1 < E1:
                                up(i - 1, e + 1)
                            if e:
                                down(i - 1, e - 1)
                            mm(P[:, 4, 0:L], erow_s[:, e, :], combT[:, :], start=True, stop=True).then_inc(bc_mm, 1)
                        for k in (2 * e, 2 * e + 1):
                            if start:
                                begin(k, i + 1, 1 - p)
                            if project:
                                finish(k, i - 2, start)
                    if experts:
                        down(i - 1, E1 - 1)

            pe.wait_ge(consts_in, 16 * len(loads))
            pe.wait_ge(consts_set, NSET)
            for k in range(7):
                begin(k, 0, 0)
            pe.wait_ge(v_out, 1)
            schedule(Round())

        @block.scalar
        def _(act):
            A = nc.scalar.activation

            def squares(n, b):
                act.wait_ge(n.centred, b + 1)
                A(sq[:, n.half, :], xc[:, n.half, :], ACT.Square).then_inc(n.squared, 1)

            def deviation(n, b):
                act.wait_ge(n.var_mm, b + 1)
                A(sd[:, n.half, :], P[0:RT, 7, 0:3], ACT.Sqrt, bias=eps_s[0:RT, :]).then_inc(n.sd_ready, 1)

            def begin(k, b):
                if k == 1:
                    squares(ln1, b)
                elif k == 2:
                    deviation(ln1, b)
                elif k == 5:
                    act.wait_ge(q_mm, b + 1)
                    A(qkvT[:, 0, :], P[:, 6, 0:L], ACT.Identity, bias=vec("bq")).then_inc(q_out, 1)
                    act.wait_ge(k_mm, b + 1)
                    A(qkvT[:, 1, :], P[:, 7, 0:L], ACT.Identity, bias=vec("bk")).then_inc(k_out, 1)
                elif k == 6:
                    act.wait_ge(v_mm, b + 1)
                    A(qkvT[:, 2, :], P[:, 6, 0:L], ACT.Identity, bias=vec("bv")).then_inc(v_out, 1)

            def take(b, t):
                act.wait_ge(proj_mm, b * 3 + t + 1)
                src = P[0:RT, 6 + t % 2, :]
                kq = src[:, 0:2 * D].rearrange("p (a h d) -> p a h d", a=2, h=H)
                A(relu[:, t, :, :, 0:DH], kq, ACT.Relu)
                A(relu[:, t, :, :, DH:PHI], kq, ACT.Relu, scale=-1.0)
                A(val[:, t, :, :], src[:, 2 * D:3 * D].rearrange("p (h d) -> p h d", h=H), ACT.Copy)
                A(bta[:, t, :], src[:, 3 * D:3 * D + H], ACT.Tanh, scale=0.5).then_inc(proj_out, 1)

            def finish(k, b):
                if k == 7:
                    squares(ln3, b)
                elif k == 8:
                    deviation(ln3, b)
                elif k == 11:
                    if known(b, 1):
                        act.wait_ge(feat_ready, b)
                    take(b, 0)
                    take(b, 1)
                elif k == 12:
                    take(b, 2)

            def middle(k, b):
                if k == 2:
                    squares(lny, b)
                elif k == 3:
                    deviation(lny, b)
                elif k == 5:
                    act.wait_ge(lny.ready, b + 1)
                    A(z2[:, :], z1[:, :], ACT.Identity, bias=vec("beta"), scale=vec("gamma")).then_inc(z2_ready, 1)
                elif k == 8:
                    squares(ln2, b)
                elif k == 9:
                    deviation(ln2, b)
                elif k == 13:
                    act.wait_ge(lg_ready, b + 1)
                    A(ex[:, :, :], lg[:, :, :], ACT.Exp).then_inc(ex_ready, 1)
                elif k == 15:
                    act.wait_ge(comb_tr, b + 1)
                    A(combT[:, :], P[0:E1, 6, 0:L], ACT.Copy).then_inc(combT_ready, 1)

            def context(b, h):
                act.wait_ge(pv_mm, b * H + h + 1)
                if h == 0 and known(b, 1):
                    act.wait_ge(ctx_stored, b * 16)
                A(ctxu[:, :, h * T:(h + 1) * T], P[0:DH + 1, 4, 0:L].rearrange("p (j t) -> p j t", j=H),
                  ACT.Copy).then_inc(ctx_out, 1)

            def row(b, h):
                act.wait_ge(max_tr, b * H + h + 1)
                A(qs[BLOCKS:ROWS, h, :], P[0:PARTS, 5, 0:L], ACT.Copy).then_inc(max_row, 1)

            def gelu(b, e):
                act.wait_ge(up_mm, b * E1 + e + 1)
                if e >= 2:
                    act.wait_ge(hs_ready, b * E1 + e - 1)
                for k in range(2):
                    A(gl[:, e % 2, k, :], P[:, 2 * (e % 2) + k, 0:L], ACT.Gelu,
                      bias=vec(f"b1_{2 * e + k}")).then_inc(gelu_done, 1)

            class Round:
                eng = act

                def __call__(self, i, p, with_features=True, heads=True, tail=True, experts=True, start=True,
                             project=True):
                    if heads:
                        row(i, 0)
                    for h in range(H):
                        if heads and h:
                            context(i, h - 1)
                        if tail:
                            middle(2 * h, i - 1)
                        if heads and h + 1 < H:
                            row(i, h + 1)
                        if heads:
                            act.wait_ge(st_mm, i * H + h + 1)
                            A(pT[:, h % 2, :, :].rearrange("p t (a c) -> p a t c", a=2),
                              P[0:RT, 2:4, 0:3 * HALF].rearrange("p a (t c) -> p a t c", t=3),
                              ACT.Exp, scale=DH ** -0.5).then_inc(probs, 1)
                        if tail:
                            middle(2 * h + 1, i - 1)
                    if heads:
                        context(i, H - 1)
                    if experts:
                        gelu(i - 1, 0)
                    for e in range(E1):
                        if experts and e + 1 < E1:
                            gelu(i - 1, e + 1)
                        for k in (2 * e, 2 * e + 1):
                            if start:
                                begin(k, i + 1)
                            if project:
                                finish(k, i - 2)

            act.wait_ge(consts_in, 16 * len(loads))
            act.wait_ge(consts_set, NSET)
            for k in range(7):
                begin(k, 0)
            schedule(Round())

        @block.vector
        def _(dve):
            V = nc.vector
            mid = Chain(dve, router_step, ROUTER_STEPS)
            mem = Chain(dve, feature_step, FEATURE_STEPS)
            tops = Chain(dve, max_step, MAX_STEPS * H)
            split = Chain(dve, part_step, PART_STEPS)

            def centre(n, src, b):
                dve.wait_ge(n.mean_mm, b + 1)
                V.tensor_tensor(xc[:, n.half, :], src, P[:, 6, 0:L], ALU.subtract).then_inc(n.centred, 1)

            def invert(n, b):
                dve.wait_ge(n.sd_ready, b + 1)
                V.reciprocal(rstd[:, n.half, :], sd[:, n.half, :]).then_inc(n.rstd_ready, 1)
                dve.wait_ge(n.rstd_ready, b + 1)
                V.tensor_tensor(diag[:, n.half, :, :], ident_s[0:RT, 0:RT].unsqueeze(1).to_broadcast([RT, 3, RT]),
                                rstd[:, n.half, :].unsqueeze(2).to_broadcast([RT, 3, RT]), ALU.mult)\
                 .then_inc(n.diag_ready, 1)

            def scaled(n, dst, b):
                dve.wait_ge(n.bc_mm, b + 1)
                V.tensor_tensor(dst, xc[:, n.half, :], P[:, 7, 0:L], ALU.mult).then_inc(n.ready, 1)

            def begin(k, b, p):
                if k == 0:
                    dve.wait_ge(tok_mm, b + 1)
                    V.tensor_tensor(h0[:, p, 1:LX], P[:, 6, 0:PATCHES], pos_s[:, 1:LX], ALU.add).then_inc(h0_ready, 1)
                elif k == 1:
                    dve.wait_ge(h0_ready, b + 1)
                    dve.wait_ge(txt_in, (b + 1) * 16)
                    centre(ln1, h0[:, p, :], b)
                elif k == 3:
                    invert(ln1, b)
                elif k == 4:
                    scaled(ln1, xn1[:, p, :], b)
                elif k == 7:
                    split.start(b)
                    dve.wait_ge(q_out, b + 1)
                    dve.wait_ge(k_out, b + 1)
                    if known(b, 1):
                        dve.wait_ge(parts_ready, b)
                        dve.wait_ge(qk_stored, b * 16 * H)
                    split.link(V.tensor_copy(parts[:, :, 0, :], qkvT[:, 0:2, :]))
                    split.link(V.tensor_tensor(left[:, :, :], qkvT[:, 0:2, :], parts[:, :, 0, :], ALU.subtract))
                elif k == 8:
                    split.link(V.tensor_copy(parts[:, :, 1, :], left[:, :, :]))
                    split.end()
                    V.tensor_tensor(parts[:, :, 2, :], left[:, :, :], parts[:, :, 1, :], ALU.subtract)\
                     .then_inc(parts_ready, 1)

            def finish(k, b):
                if k == 7:
                    dve.wait_ge(h2_ready, b + 1)
                    centre(ln3, h2[:, :], b)
                elif k == 9:
                    invert(ln3, b)
                elif k == 10:
                    scaled(ln3, x3[:, :], b)

            def features(k, b):
                r = relu[:, :, :, :, :].rearrange("p t a h f -> p t (a h) f")
                g = bta[:, :, :].unsqueeze(3)
                if k == 1:
                    mem.start(b)
                    dve.wait_ge(proj_out, (b + 1) * 3)
                    mem.link(V.tensor_tensor(prod[:, :, :, 0:1], r[:, :, :, 0:1], r[:, :, :, PHI - 1:PHI], ALU.mult))
                elif k in (2, 4):
                    q = slice((k // 2 - 1) * H, k // 2 * H)
                    mem.link(V.tensor_tensor(prod[:, :, q, 1:PHI], r[:, :, q, 1:PHI], r[:, :, q, 0:PHI - 1], ALU.mult))
                elif k in (5, 6):
                    q = slice((k - 5) * H, (k - 4) * H)
                    mem.link(V.tensor_reduce(fsum[:, :, q], prod[:, :, q, :], AX.X, ALU.add))
                elif k == 7:
                    mem.link(V.tensor_scalar(fsum[:, :, :], fsum[:, :, :], 1e-6, None, ALU.add))
                    mem.link(V.reciprocal(fsum[:, :, :], fsum[:, :, :]))
                    mem.link(V.tensor_scalar(bta[:, :, :], bta[:, :, :], 0.5, 0.5, ALU.mult, ALU.add))
                    if known(b, 1):
                        dve.wait_ge(feat_stored, b * 48)
                elif k == 8:
                    for a in range(2):
                        c = 2 * FK * a
                        f = V.tensor_tensor(feat[:, :, c:c + FK].rearrange("p t (h f) -> p t h f", h=H),
                                            prod[:, :, a * H:(a + 1) * H, :],
                                            fsum[:, :, a * H:(a + 1) * H].unsqueeze(3).to_broadcast([RT, 3, H, PHI]),
                                            ALU.mult)
                        mem.link(f)
                elif k == 9:
                    mem.link(V.tensor_tensor(feat[:, :, FK:2 * FK].rearrange("p t (h f) -> p t h f", h=H),
                                             feat[:, :, 0:FK].rearrange("p t (h f) -> p t h f", h=H),
                                             g.to_broadcast([RT, 3, H, PHI]), ALU.mult))
                elif k == 10:
                    V.tensor_tensor(feat[:, :, 3 * FK:FW].rearrange("p t (h f) -> p t h f", h=H),
                                    val[:, :, :, :], g.to_broadcast([RT, 3, H, DH]), ALU.mult).then_inc(feat_ready, 1)
                    mem.end()

            def middle(k, b, p):
                if k == 0:
                    mid.start(b)
                    dve.wait_ge(den_in, (b + 1) * 16)
                    mid.link(V.reciprocal(den[:, :], den[:, :]))
                    dve.wait_ge(cfm_in, (b + 1) * 16)
                    V.tensor_tensor(cfm[:, :], cfm[:, :], den[:, :], ALU.mult).then_inc(cfm_ready, 1)
                elif k == 1:
                    dve.wait_ge(wo_mm, b + 1)
                    V.scalar_tensor_tensor(y1[:, :], P[:, 6, 0:L], vec("bo"), xn1[:, p, :], ALU.add, ALU.add)\
                     .then_inc(y1_ready, 1)
                elif k == 2:
                    dve.wait_ge(y1_ready, b + 1)
                    centre(lny, y1[:, :], b)
                elif k == 4:
                    invert(lny, b)
                elif k == 5:
                    scaled(lny, z1[:, :], b)
                elif k == 6:
                    dve.wait_ge(z2_ready, b + 1)
                    V.tensor_tensor(h1[:, :], h0[:, p, :], z2[:, :], ALU.add).then_inc(h1_ready, 1)
                elif k == 8:
                    dve.wait_ge(h1_ready, b + 1)
                    centre(ln2, h1[:, :], b)
                elif k == 10:
                    invert(ln2, b)
                elif k == 11:
                    scaled(ln2, x2[:, :], b)
                elif k == 12:
                    dve.wait_ge(router_mm, b + 1)
                    mid.link(V.tensor_tensor(lg[:, :, :], P[0:RT, 7, 0:3 * E1].rearrange("p (t e) -> p t e", t=3),
                                             br_s[0:RT, :].unsqueeze(1).to_broadcast([RT, 3, E1]), ALU.add))
                    mid.link(V.tensor_reduce(r8[:, :], lg[:, :, :], AX.X, ALU.max))
                    V.tensor_tensor(lg[:, :, :], lg[:, :, :], r8[:, :].unsqueeze(2).to_broadcast([RT, 3, E1]),
                                    ALU.subtract).then_inc(lg_ready, 1)
                elif k == 14:
                    dve.wait_ge(ex_ready, b + 1)
                    mid.link(V.tensor_reduce(r8[:, :], ex[:, :, :], AX.X, ALU.add))
                    mid.link(V.reciprocal(r8[:, :], r8[:, :]))
                    mid.link(V.tensor_tensor(ex[:, :, :], ex[:, :, :], r8[:, :].unsqueeze(2).to_broadcast([RT, 3, E1]),
                                             ALU.mult))
                    mine = ex[:, :, :].unsqueeze(3).to_broadcast([RT, 3, E1, E1])
                    other = ex[:, :, :].unsqueeze(2).to_broadcast([RT, 3, E1, E1])
                    mid.link(V.tensor_tensor(cmp1[:, :, :, :], other, mine, ALU.is_gt))
                    mid.link(V.tensor_tensor(cmp2[:, :, :, :], other, mine, ALU.is_equal))
                    mid.link(V.tensor_tensor(cmp2[:, :, :, :], cmp2[:, :, :, :],
                                             tri_s[0:RT, :, :].unsqueeze(1).to_broadcast([RT, 3, E1, E1]), ALU.mult))
                    mid.link(V.tensor_tensor(cmp1[:, :, :, :], cmp1[:, :, :, :], cmp2[:, :, :, :], ALU.add))
                    mid.link(V.tensor_reduce(rank[:, :, :], cmp1[:, :, :, :], AX.X, ALU.add))
                    V.scalar_tensor_tensor(comb[:, :, :], rank[:, :, :], 2.0, ex[:, :, :], ALU.is_lt, ALU.mult)\
                     .then_inc(comb_ready, 1)
                    mid.end()

            def maximum(b, h):
                if h == 0:
                    tops.start(b)
                dve.wait_ge(s_mm, b * H + h + 1)
                tops.link(V.tensor_reduce(nmx[:, :], P[0:RT, 0:2, 0:3 * HALF].rearrange("p a (t c) -> p t a c", t=3),
                                          AX.XY, ALU.max, negate=True))
                if h >= 2:
                    dve.wait_ge(max_tr, b * H + h - 1)
                part = [nparts[:, h % 2, :, c] for c in range(PARTS)]
                tops.link(V.tensor_copy(part[0], nmx[:, :]))
                tops.link(V.tensor_tensor(nleft[:, :], nmx[:, :], part[0], ALU.subtract))
                tops.link(V.tensor_copy(part[1], nleft[:, :]))
                tops.link(V.tensor_tensor(part[2], nleft[:, :], part[1], ALU.subtract))
                if h == H - 1:
                    tops.end()

            class Round:
                eng = dve

                def __call__(self, i, p, with_features=True, heads=True, tail=True, experts=True, start=True,
                             project=True):
                    if heads:
                        maximum(i, 0)
                        dve.wait_ge(v_tr, i + 1)
                        V.tensor_copy(vaug[:, :, :, :], P[0:RT, 5, 0:H * 3 * (DH + 1)].rearrange(
                            "p (h t d) -> p h t d", h=H, t=3)).then_inc(vaug_ready, 1)
                    for h in range(H):
                        if heads and h + 1 < H:
                            maximum(i, h + 1)
                        for k in (2 * h, 2 * h + 1):
                            if tail:
                                middle(k, i - 1, 1 - p)
                    for e in range(E1):
                        if experts:
                            dve.wait_ge(gelu_done, (i - 1) * 2 * E1 + 2 * e + 2)
                            dve.wait_ge(bc_mm, (i - 1) * E1 + e + 1)
                            if e >= 2:
                                dve.wait_ge(down_mm, (i - 1) * E1 + e - 1)
                            V.tensor_tensor(hs[:, e % 2, :, :], gl[:, e % 2, :, :],
                                            P[:, 4, 0:L].unsqueeze(1).to_broadcast([128, 2, L]), ALU.mult)\
                             .then_inc(hs_ready, 1)
                        for k in (2 * e, 2 * e + 1):
                            if start:
                                begin(k, i + 1, 1 - p)
                            if with_features:
                                features(k, i - 3)
                            if project:
                                finish(k, i - 2)
                    if experts:
                        dve.wait_ge(down_mm, i * E1)
                        if known(i, 2):
                            dve.wait_ge(h2_stored, (i - 1) * 16)
                        V.tensor_tensor(h2[:, :], h1[:, :], P[:, 5, 0:L], ALU.add).then_inc(h2_ready, 1)

            V.memset(mean_w[:, :], 1.0 / D).then_inc(consts_set, 1)
            V.memset(ones_s[:, :], 1.0).then_inc(consts_set, 1)
            V.memset(eps_s[:, :], 1e-5).then_inc(consts_set, 1)
            V.memset(ks[BLOCKS:ROWS, :, :], 1.0).then_inc(consts_set, 1)
            V.memset(vd[0:1, :, :], 1.0).then_inc(consts_set, 1)
            V.memset(P[:, :, :], 0.0).then_inc(consts_set, 1)
            dve.wait_ge(consts_in, 16 * len(loads))
            dve.wait_ge(consts_set, 6)
            V.tensor_copy(ident_h[:, :], ident_s[:, :]).then_inc(consts_set, 1)
            V.tensor_scalar(pos_s[:, 1:LX], pos_s[:, 1:LX], vec("tok_b"), None, ALU.add).then_inc(pos_ready, 1)
            V.tensor_scalar(h0[:, :, 0:1], pos_s[:, 0:1].unsqueeze(1).to_broadcast([128, 2, 1]), vec("cls"), None,
                            ALU.add).then_inc(consts_set, 1)
            dve.wait_ge(pos_ready, 1)
            dve.wait_ge(consts_set, NSET)
            for k in range(9):
                begin(k, 0, 0)
            schedule(Round())


def memory(nc, feat_d, ident, eye_blocks, read_mask, read_d):
    f32 = mybir.dt.float32
    ALU = mybir.AluOpType
    ACT = mybir.ActivationFunctionType
    NSUB = -(-L // SUB)
    LAST = (L - SUB) // 2

    ctx = ExitStack()
    with ctx:
        def sb(name, shape, dt=f32):
            return ctx.enter_context(nc.sbuf_tensor(name, shape, dt))

        def sem(name):
            return ctx.enter_context(nc.semaphore(name))

        ident2 = sb("ident2", [128, 128])
        eye_s = sb("eye_s", [128, SUB, 4, SUB])
        mask_s = sb("mask_s", [128, B])
        kin = sb("kin", [128, 2, 4, 3 * FK])
        vin = sb("vin", [128, PAIRS, D])
        kqt = sb("kqt", [128, 2, 6, 128])
        gram = sb("gram", [128, PAIRS, 4, 2, 2 * B])
        low = sb("low", [128, SUB, 4, SUB])
        inv = sb("inv", [128, SUB, 4, SUB])
        tmp = sb("tmp", [128, SUB, 4, SUB])
        invT = sb("invT", [128, 128, SUB])
        u1 = sb("u1", [128, 2, 4, D])
        r2 = sb("r2", [128, 2, 4, D])
        u2 = sb("u2", [128, 2, 4, D])
        osb = sb("osb", [128, PAIRS, D])
        P = ctx.enter_context(nc.psum_tensor("P2", [128, 8, 512], f32))

        consts2_in = sem("consts2_in")
        psum_set = sem("psum_set")
        k_loaded = [sem(f"k_loaded{c}") for c in range(2)]
        v_loaded = sem("v_loaded")
        kq_tr = sem("kq_tr")
        kqt_ready = sem("kqt_ready")
        gram_mm = sem("gram_mm")
        gram_out = sem("gram_out")
        gram_masked = sem("gram_masked")
        low_tr = sem("low_tr")
        low_even = sem("low_even")
        low_odd = sem("low_odd")
        inv_set = sem("inv_set")
        solve_step = sem("solve_step")
        inv_ready = sem("inv_ready")
        inv_tr = sem("inv_tr")
        invT_even = sem("invT_even")
        invT_odd = sem("invT_odd")
        u1_mm = sem("u1_mm")
        u1_ready = sem("u1_ready")
        r2_mm = sem("r2_mm")
        r2_ready = sem("r2_ready")
        u2_mm = sem("u2_mm")
        u2_ready = sem("u2_ready")
        o_mm = sem("o_mm")
        o_ready = sem("o_ready")
        read_stored = sem("read_stored")

        block = ctx.enter_context(nc.Block())
        feat_v = feat_d.rearrange("b (l k) f -> k b l f", k=2)
        read_v = read_d.rearrange("b (l k) f -> k b l f", k=2)
        NT = SUB // 4

        @block.sync
        def _(sp):
            def at(b):
                return b if isinstance(b, int) else sp.snap(b)

            def sub(n, p0):
                quads = [at(p0 + 4 * c) for c in range(QUADS)]
                for c in range(QUADS):
                    if c >= 2 or known(n, 1):
                        sp.wait_ge(kqt_ready, n * PAIRS + 4 * (c - 1))
                    for k in range(2):
                        sp.dma_start(kin[B * k:B * k + B, c % 2, :, :],
                                     feat_v[k][:, bass.ds(quads[c], 4), 0:3 * FK]).then_inc(k_loaded[c % 2], 16)
                if known(n, 1):
                    sp.wait_ge(r2_ready, n * QUADS)
                for k in range(2):
                    sp.dma_start(vin[B * k:B * k + B, :, :],
                                 feat_v[k][:, bass.ds(quads[0], PAIRS), 3 * FK:FW]).then_inc(v_loaded, 16)
                sp.wait_ge(o_ready, (n + 1) * QUADS)
                for k in range(2):
                    sp.dma_start(read_v[k][:, bass.ds(quads[0], PAIRS), :], osb[B * k:B * k + B, :, :])\
                      .then_inc(read_stored, 16)

            sp.dma_start(ident2[:, :], ident).then_inc(consts2_in, 16)
            sp.dma_start(eye_s[:, :, :, :], eye_blocks).then_inc(consts2_in, 16)
            sp.dma_start(mask_s[:, :], read_mask).then_inc(consts2_in, 16)
            sub(0, 0)
            with sp.Fori(1, NSUB - 1) as n:
                sub(n, n * PAIRS)
            sub(NSUB - 1, LAST)
            sp.wait_ge(read_stored, NSUB * 32)

        @block.tensor
        def _(pe):
            mm = nc.tensor.matmul

            def stream(c, q):
                pair, h = 4 * c + q // H, q % H
                return pair, h % 4, h // 4, h

            def sub(n):
                def turn(p):
                    if p >= 2:
                        pe.wait_ge(kqt_ready, n * PAIRS + p - 1)
                    if p % 4 == 0:
                        pe.wait_ge(k_loaded[p // 4 % 2], n * 64 + (p // 8 + 1) * 32)
                    for j in range(6):
                        last = nc.tensor.transpose(P[:, 4 + 2 * (p % 2) + j // 4, (j % 4) * 128:(j % 4 + 1) * 128],
                                                   kin[:, p // 4 % 2, p % 4, j * 128:(j + 1) * 128], ident2[:, :])
                    last.then_inc(kq_tr, 1)

                def products(p):
                    pe.wait_ge(kqt_ready, n * PAIRS + p + 1)
                    if p:
                        pe.wait_ge(gram_out, n * PAIRS + p)
                    for hd in range(2):
                        for k in range(2):
                            for g in range(4):
                                f = slice(PHI * g, PHI * (g + 1))
                                last = mm(P[B * k:B * k + B, g, hd * 2 * B:(hd + 1) * 2 * B],
                                          kqt[f, p % 2, hd, B * k:B * k + B],
                                          kqt[f, p % 2, 2 + hd:6:2, B * k:B * k + B],
                                          start=True, stop=True, tile_position=(PHI * g, B * k))
                    last.then_inc(gram_mm, 1)

                if known(n, 1):
                    pe.wait_ge(o_ready, n * QUADS)
                turn(0)
                for p in range(PAIRS):
                    if p + 1 < PAIRS:
                        turn(p + 1)
                    products(p)
                pe.wait_ge(gram_out, (n + 1) * PAIRS)
                for i in range(2 * NT):
                    blk, bank = i % 2, 4 + i % 4
                    if i >= 4:
                        pe.wait_ge(low_even if i % 2 == 0 else low_odd, n * NT + (i - 4) // 2 + 1)
                    for j in range(4):
                        t = blk * SUB + 4 * (i // 2) + j
                        last = nc.tensor.transpose(P[:, bank, j * 128:(j + 1) * 128],
                                                   gram[:, :, :, :, t].rearrange("p a g h -> p (a g h)"), ident2[:, :])
                    last.then_inc(low_tr, 1)
                pe.wait_ge(inv_ready, n + 1)
                for i in range(NT):
                    if i >= 4:
                        pe.wait_ge(invT_even if i % 2 == 0 else invT_odd, n * NT // 2 + (i - 4) // 2 + 1)
                    for j in range(4):
                        last = nc.tensor.transpose(P[:, 4 + i % 4, j * 128:(j + 1) * 128],
                                                   inv[:, 4 * i + j, :, :].rearrange("p q s -> p (q s)"), ident2[:, :])
                    last.then_inc(inv_tr, 1)
                pe.wait_ge(v_loaded, (n + 1) * 32)
                pe.wait_ge(invT_even, (n + 1) * NT // 2)
                pe.wait_ge(invT_odd, (n + 1) * NT // 2)
                pe.wait_ge(gram_masked, (n + 1) * PAIRS)

                def carry():
                    mm(P[0:2 * SUB, 7, 0:1], ident2[0:SUB, 0:2 * SUB], ident2[0:SUB, 0:1], start=True, stop=True)

                def first(c):
                    if c >= 2:
                        pe.wait_ge(u2_ready, n * QUADS + c - 1)
                    carry()
                    for q in range(4 * H):
                        pair, g, hd, h = stream(c, q)
                        for k in range(2):
                            f = slice(B * k, B * k + SUB)
                            last = mm(P[f, c % 2, q * DH:(q + 1) * DH], invT[f, pair * H + 2 * g + hd, :],
                                      vin[f, pair, h * DH:(h + 1) * DH], start=True, stop=True)
                    last.then_inc(u1_mm, 1)

                def across(c):
                    pe.wait_ge(u1_ready, n * QUADS + c + 1)
                    if c >= 2:
                        pe.wait_ge(r2_ready, n * QUADS + c - 1)
                    carry()
                    for q in range(4 * H):
                        pair, g, hd, h = stream(c, q)
                        for k in range(2):
                            f = slice(B * k, B * k + SUB)
                            last = mm(P[B * k + SUB:B * (k + 1), 2 + c % 2, q * DH:(q + 1) * DH],
                                      gram[f, pair, g, hd, SUB:B], u1[f, c % 2, q // H, h * DH:(h + 1) * DH],
                                      start=True, stop=True)
                    last.then_inc(r2_mm, 1)

                def second(c):
                    pe.wait_ge(r2_ready, n * QUADS + c + 1)
                    carry()
                    for q in range(4 * H):
                        pair, g, hd, h = stream(c, q)
                        for k in range(2):
                            f = slice(B * k + SUB, B * (k + 1))
                            last = mm(P[f, c % 2, q * DH:(q + 1) * DH], invT[f, pair * H + 2 * g + hd, :],
                                      r2[f, c % 2, q // H, h * DH:(h + 1) * DH], start=True, stop=True)
                    last.then_inc(u2_mm, 1)

                def read(c):
                    pe.wait_ge(u2_ready, n * QUADS + c + 1)
                    if c >= 2:
                        pe.wait_ge(o_ready, n * QUADS + c - 1)
                    carry()
                    for q in range(4 * H):
                        pair, g, hd, h = stream(c, q)
                        for k in range(2):
                            f = slice(B * k, B * (k + 1))
                            last = mm(P[f, 4 + c % 2, q * DH:(q + 1) * DH], gram[f, pair, g, hd, B:2 * B],
                                      u2[f, c % 2, q // H, h * DH:(h + 1) * DH], start=True, stop=True)
                    last.then_inc(o_mm, 1)

                for c in range(0, QUADS, 2):
                    first(c)
                    first(c + 1)
                    across(c)
                    across(c + 1)
                    second(c)
                    second(c + 1)
                    read(c)
                    read(c + 1)

            pe.wait_ge(consts2_in, 48)
            pe.wait_ge(psum_set, 1)
            sub(0)
            with pe.Fori(1, NSUB - 1) as n:
                sub(n)
            sub(NSUB - 1)

        @block.scalar
        def _(act):
            A = nc.scalar.activation

            def sub(n):
                def turned(p):
                    act.wait_ge(kq_tr, n * PAIRS + p + 1)
                    if p >= 2:
                        act.wait_ge(gram_mm, n * PAIRS + p - 1)
                    b = 4 + 2 * (p % 2)
                    A(kqt[:, p % 2, 0:4, :].rearrange("p j n -> p (j n)"), P[:, b, :], ACT.Copy)
                    A(kqt[:, p % 2, 4:6, :].rearrange("p j n -> p (j n)"), P[:, b + 1, 0:256], ACT.Copy)\
                     .then_inc(kqt_ready, 1)

                turned(0)
                for p in range(PAIRS):
                    if p + 1 < PAIRS:
                        turned(p + 1)
                    act.wait_ge(gram_mm, n * PAIRS + p + 1)
                    A(gram[:, p, :, :, :], P[:, 0:4, 0:4 * B].rearrange("p g (h n) -> p g h n", h=2), ACT.Copy)\
                     .then_inc(gram_out, 1)
                for i in range(0, 2 * NT, 2):
                    act.wait_ge(low_tr, n * 2 * NT + i + 1)
                    A(low[:, 4 * (i // 2):4 * (i // 2) + 4, 0:3:2, :],
                      P[:, 4 + i % 4, :].rearrange("p (t k s) -> p t k s", t=4, k=2)[:, :, :, 0:SUB],
                      ACT.Copy, scale=-1.0).then_inc(low_even, 1)
                for i in range(0, NT, 2):
                    act.wait_ge(inv_tr, n * NT + i + 1)
                    A(invT[:, :, 4 * i:4 * i + 4].rearrange("p q t -> p t q"),
                      P[:, 4 + i % 4, :].rearrange("p (t q) -> p t q", t=4), ACT.Copy).then_inc(invT_even, 1)

                def take_u1(c):
                    act.wait_ge(u1_mm, n * QUADS + c + 1)
                    A(u1[:, c % 2, :, :].rearrange("p a n -> p (a n)"), P[:, c % 2, :], ACT.Copy).then_inc(u1_ready, 1)

                def take_u2(c):
                    act.wait_ge(u2_mm, n * QUADS + c + 1)
                    A(u2[:, c % 2, :, :].rearrange("p a n -> p (a n)"), P[:, c % 2, :], ACT.Copy).then_inc(u2_ready, 1)

                for c in range(0, QUADS, 2):
                    take_u1(c)
                    take_u1(c + 1)
                    take_u2(c)
                    take_u2(c + 1)

            sub(0)
            with act.Fori(1, NSUB - 1) as n:
                sub(n)
            sub(NSUB - 1)

        @block.vector
        def _(dve):
            V = nc.vector
            chain = Chain(dve, solve_step, SOLVE_STEPS)

            def sub(n):
                chain.start(n)
                if known(n, 1):
                    dve.wait_ge(inv_tr, n * NT)
                V.tensor_copy(inv[:, :, :, :], eye_s[:, :, :, :]).then_inc(inv_set, 1)
                for p in range(PAIRS):
                    dve.wait_ge(gram_out, n * PAIRS + p + 1)
                    V.tensor_tensor(gram[:, p, :, :, B:2 * B], gram[:, p, :, :, B:2 * B],
                                    mask_s[:, :].unsqueeze(1).unsqueeze(1).to_broadcast([128, 4, 2, B]), ALU.mult)\
                     .then_inc(gram_masked, 1)
                for i in range(1, 2 * NT, 2):
                    dve.wait_ge(low_tr, n * 2 * NT + i + 1)
                    V.tensor_scalar(low[:, 4 * (i // 2):4 * (i // 2) + 4, 1:4:2, :],
                                    P[:, 4 + i % 4, :].rearrange("p (t k s) -> p t k s", t=4, k=2)[:, :, :, SUB:B],
                                    -1.0, None, ALU.mult).then_inc(low_odd, 1)
                dve.wait_ge(inv_set, n + 1)
                dve.wait_ge(low_even, (n + 1) * NT)
                dve.wait_ge(low_odd, (n + 1) * NT)
                for s in range(SUB - 1):
                    shape = [128, SUB - 1 - s, 4, s + 1]
                    below = slice(s + 1, SUB)
                    chain.link(V.tensor_tensor(tmp[:, below, :, 0:s + 1], low[:, below, :, s:s + 1].to_broadcast(shape),
                                               inv[:, s:s + 1, :, 0:s + 1].to_broadcast(shape), ALU.mult))
                    ins = V.tensor_tensor(inv[:, below, :, 0:s + 1], inv[:, below, :, 0:s + 1],
                                          tmp[:, below, :, 0:s + 1], ALU.add)
                    chain.link(ins)
                chain.end()
                V.tensor_copy(inv[:, 0:1, 0:1, 0:1], eye_s[:, 0:1, 0:1, 0:1]).then_inc(inv_ready, 1)
                for i in range(1, NT, 2):
                    dve.wait_ge(inv_tr, n * NT + i + 1)
                    V.tensor_copy(invT[:, :, 4 * i:4 * i + 4].rearrange("p q t -> p t q"),
                                  P[:, 4 + i % 4, :].rearrange("p (t q) -> p t q", t=4)).then_inc(invT_odd, 1)

                def rest(c):
                    dve.wait_ge(r2_mm, n * QUADS + c + 1)
                    V.tensor_tensor(r2[:, c % 2, :, :], vin[:, 4 * c:4 * c + 4, :],
                                    P[:, 2 + c % 2, :].rearrange("p (a n) -> p a n", a=4), ALU.subtract)\
                     .then_inc(r2_ready, 1)

                def take_o(c):
                    dve.wait_ge(o_mm, n * QUADS + c + 1)
                    if c == 0 and known(n, 1):
                        dve.wait_ge(read_stored, n * 32)
                    V.tensor_copy(osb[:, 4 * c:4 * c + 4, :], P[:, 4 + c % 2, :].rearrange("p (a n) -> p a n", a=4))\
                     .then_inc(o_ready, 1)

                for c in range(0, QUADS, 2):
                    rest(c)
                    rest(c + 1)
                    take_o(c)
                    take_o(c + 1)

            V.memset(P[:, :, :], 0.0).then_inc(psum_set, 1)
            dve.wait_ge(consts2_in, 48)
            sub(0)
            with dve.Fori(1, NSUB - 1) as n:
                sub(n)
            sub(NSUB - 1)


def experts_out(nc, read_d, h2_d, vecs, wo1, wg, bg, we, be, ident, expert_numbers, out):
    f32 = mybir.dt.float32
    u32 = mybir.dt.uint32
    ALU = mybir.AluOpType
    ACT = mybir.ActivationFunctionType
    AX = mybir.AxisListType
    R = B // GRP

    ctx = ExitStack()
    with ctx:
        def sb(name, shape, dt=f32):
            return ctx.enter_context(nc.sbuf_tensor(name, shape, dt))

        def sem(name):
            return ctx.enter_context(nc.semaphore(name))

        vec3 = sb("vec3", [128, NV])
        wo1_s = sb("wo1_s", [128, D])
        wg_s = sb("wg_s", [128, E2])
        bg_s = sb("bg_s", [1, E2])
        enum_s = sb("enum_s", [1, E2])
        we_s = sb("we_s", [128, E2 * D])
        be_s = sb("be_s", [128, E2])
        ident3 = sb("ident3", [128, 128])
        mean3 = sb("mean3", [128, 128])
        ones3 = sb("ones3", [128, 128])
        eps3 = sb("eps3", [128, 1])
        rd = sb("rd", [RT, GRP, 3, D])
        h2 = sb("h2b", [128, GRP, L])
        rf = sb("rf", [128, GRP, L])
        h3 = sb("h3", [128, GRP, L])
        xc = sb("xc3", [128, GRP, L])
        sq = sb("sq3", [128, GRP, L])
        sd = sb("sd3", [RT, GRP, 3])
        rstd = sb("rstd3", [RT, GRP, 3])
        diag = sb("diag3", [RT, GRP, 3, RT])
        x4 = sb("x4", [128, GRP, L])
        msum = sb("msum", [128, GRP])
        sc = sb("sc", [1, GRP, E2])
        top = sb("top", [1, GRP])
        tot = sb("tot", [1, GRP])
        gate = sb("gate", [1, GRP])
        worse = sb("worse", [1, GRP, E2])
        bestf = sb("bestf", [1, GRP])
        best = sb("best", [1, GRP], u32)
        gcol = sb("gcol", [128, GRP])
        wsel = sb("wsel", [128, GRP, D])
        bsel = sb("bsel", [128, GRP])
        fin = sb("fin", [128, GRP, L])
        P = ctx.enter_context(nc.psum_tensor("P3", [128, 8, 512], f32))

        consts3_in = sem("consts3_in")
        consts3_set = sem("consts3_set")
        read_in = sem("read_in")
        h2_in = sem("h2_in")
        read_tr = sem("read_tr")
        rf_ready = sem("rf_ready")
        wo1_mm = sem("wo1_mm")
        h3_ready = sem("h3_ready")
        mean_mm = sem("mean_mm")
        centred = sem("centred")
        squared = sem("squared")
        var_mm = sem("var_mm")
        sd_ready = sem("sd_ready")
        rstd_ready = sem("rstd_ready")
        diag_ready = sem("diag_ready")
        spread_mm = sem("spread_mm")
        x4_ready = sem("x4_ready")
        msum_ready = sem("msum_ready")
        score_mm = sem("score_mm")
        sc_ready = sem("sc_ready")
        sc_exp = sem("sc_exp")
        gate_step = sem("gate_step")
        gate_ready = sem("gate_ready")
        gate_mm = sem("gate_mm")
        gcol_ready = sem("gcol_ready")
        wsel_ready = sem("wsel_ready")
        bsel_ready = sem("bsel_ready")
        y_mm = sem("y_mm")
        fin_ready = sem("fin_ready")
        out_stored = sem("out_stored")

        loads = [(vec3, vecs), (wo1_s, wo1), (wg_s, wg), (bg_s, bg), (enum_s, expert_numbers), (we_s, we), (be_s, be),
                 (ident3, ident)]
        block = ctx.enter_context(nc.Block())

        @block.sync
        def _(sp):
            def at(b):
                return b if isinstance(b, int) else sp.snap(b)

            def load(firsts):
                for u in range(GRP):
                    for t, s in TILES:
                        sp.dma_start(rd[:, u, t, :], read_d[bass.ds(firsts[u], 1), s:s + RT, :]
                                     .rearrange("o p n -> (o p) n")).then_inc(read_in, 16)

            def load_h2(first):
                sp.dma_start(h2[:, :, :], h2_d[bass.ds(first, GRP)].rearrange("o p n -> p o n")).then_inc(h2_in, 16)

            def store(r, first):
                sp.wait_ge(fin_ready, (r + 1) * GRP)
                sp.dma_start(out[bass.ds(first, GRP)].rearrange("o p n -> p o n"), fin[:, :, :])\
                  .then_inc(out_stored, 16)

            for dst, src in loads:
                sp.dma_start(dst[:], src).then_inc(consts3_in, 16)
            load(range(GRP))
            load_h2(0)
            with sp.Fori(1, R) as r:
                images_ = [at(r * GRP + u) for u in range(GRP)]
                stored = at(r * GRP - GRP)
                sp.wait_ge(read_tr, r * GRP)
                load(images_)
                sp.wait_ge(h3_ready, r * GRP)
                load_h2(images_[0])
                store(r - 1, stored)
            store(R - 1, B - GRP)
            sp.wait_ge(out_stored, R * 16)

        @block.tensor
        def _(pe):
            mm = nc.tensor.matmul

            def group(r):
                pe.wait_ge(read_in, (r + 1) * 16 * 3 * GRP)
                for u in range(GRP):
                    if known(r, 1):
                        pe.wait_ge(fin_ready, r * GRP)
                    for t, s in TILES:
                        last = nc.tensor.transpose(P[:, 2 * u, s:s + RT], rd[:, u, t, :], ident3[0:RT, 0:RT])
                    last.then_inc(read_tr, 1)
                for u in range(GRP):
                    pe.wait_ge(rf_ready, r * GRP + u + 1)
                    mm(P[:, 2 * u, 0:L], wo1_s[:, :], rf[:, u, :], start=True, stop=True).then_inc(wo1_mm, 1)
                for u in range(GRP):
                    pe.wait_ge(h3_ready, r * GRP + u + 1)
                    mm(P[:, 2 * u, 0:L], mean3[:, :], h3[:, u, :], start=True, stop=True).then_inc(mean_mm, 1)
                for u in range(GRP):
                    pe.wait_ge(squared, r * GRP + u + 1)
                    for t, s in TILES:
                        last = mm(P[0:RT, 2 * u + 1, t:t + 1], sq[:, u, s:s + RT], mean3[:, 0:1], start=True, stop=True)
                    last.then_inc(var_mm, 1)
                for u in range(GRP):
                    pe.wait_ge(diag_ready, r * GRP + u + 1)
                    for t, s in TILES:
                        last = mm(P[:, 2 * u + 1, s:s + RT], ones3[0:RT, :], diag[:, u, t, :], start=True, stop=True)
                    last.then_inc(spread_mm, 1)
                pe.wait_ge(msum_ready, (r + 1) * GRP)
                for u in range(GRP):
                    last = mm(P[0:1, 1, u * E2:(u + 1) * E2], msum[:, u:u + 1], wg_s[:, :], start=True, stop=True)
                last.then_inc(score_mm, 1)
                pe.wait_ge(gate_ready, r + 1)
                mm(P[:, 3, 0:GRP], ones3[0:1, :], gate[:, :], start=True, stop=True).then_inc(gate_mm, 1)
                for u in range(GRP):
                    pe.wait_ge(wsel_ready, r * GRP + u + 1)
                    mm(P[:, 2 * u, 0:L], wsel[:, u, :], x4[:, u, :], start=True, stop=True).then_inc(y_mm, 1)

            pe.wait_ge(consts3_in, 16 * len(loads))
            pe.wait_ge(consts3_set, 3)
            group(0)
            with pe.Fori(1, R) as r:
                group(r)

        @block.scalar
        def _(act):
            A = nc.scalar.activation

            def group(r):
                for u in range(GRP):
                    act.wait_ge(read_tr, r * GRP + u + 1)
                    A(rf[:, u, :], P[:, 2 * u, 0:L], ACT.Copy).then_inc(rf_ready, 1)
                for u in range(GRP):
                    act.wait_ge(centred, r * GRP + u + 1)
                    A(sq[:, u, :], xc[:, u, :], ACT.Square).then_inc(squared, 1)
                for u in range(GRP):
                    act.wait_ge(var_mm, r * GRP + u + 1)
                    A(sd[:, u, :], P[0:RT, 2 * u + 1, 0:3], ACT.Sqrt, bias=eps3[0:RT, :]).then_inc(sd_ready, 1)
                act.wait_ge(sc_ready, r + 1)
                A(sc[:, :, :], sc[:, :, :], ACT.Exp).then_inc(sc_exp, 1)
                act.wait_ge(gate_mm, r + 1)
                A(gcol[:, :], P[:, 3, 0:GRP], ACT.Copy).then_inc(gcol_ready, 1)
                for u in range(GRP):
                    e = act.value_load(best[0:1, u:u + 1], min_val=0, max_val=E2 - 1)
                    act.wait_ge(gcol_ready, r + 1)
                    A(wsel[:, u, :], we_s[:, bass.ds(e * D, D)], ACT.Copy, scale=gcol[:, u:u + 1]).then_inc(wsel_ready, 1)
                    A(bsel[:, u:u + 1], be_s[:, bass.ds(e, 1)], ACT.Copy, scale=gcol[:, u:u + 1]).then_inc(bsel_ready, 1)

            act.wait_ge(consts3_in, 16 * len(loads))
            act.wait_ge(consts3_set, 3)
            group(0)
            with act.Fori(1, R) as r:
                group(r)

        @block.vector
        def _(dve):
            V = nc.vector
            chain = Chain(dve, gate_step, GATE_STEPS)

            def group(r):
                chain.start(r)
                dve.wait_ge(h2_in, (r + 1) * 16)
                for u in range(GRP):
                    dve.wait_ge(wo1_mm, r * GRP + u + 1)
                    V.scalar_tensor_tensor(h3[:, u, :], P[:, 2 * u, 0:L], vec3[:, 8:9], h2[:, u, :], ALU.add, ALU.add)\
                     .then_inc(h3_ready, 1)
                for u in range(GRP):
                    dve.wait_ge(mean_mm, r * GRP + u + 1)
                    dve.wait_ge(h3_ready, r * GRP + u + 1)
                    V.tensor_tensor(xc[:, u, :], h3[:, u, :], P[:, 2 * u, 0:L], ALU.subtract).then_inc(centred, 1)
                for u in range(GRP):
                    dve.wait_ge(sd_ready, r * GRP + u + 1)
                    V.reciprocal(rstd[:, u, :], sd[:, u, :]).then_inc(rstd_ready, 1)
                    dve.wait_ge(rstd_ready, r * GRP + u + 1)
                    V.tensor_tensor(diag[:, u, :, :], ident3[0:RT, 0:RT].unsqueeze(1).to_broadcast([RT, 3, RT]),
                                    rstd[:, u, :].unsqueeze(2).to_broadcast([RT, 3, RT]), ALU.mult)\
                     .then_inc(diag_ready, 1)
                for u in range(GRP):
                    dve.wait_ge(spread_mm, r * GRP + u + 1)
                    V.tensor_tensor(x4[:, u, :], xc[:, u, :], P[:, 2 * u + 1, 0:L], ALU.mult).then_inc(x4_ready, 1)
                dve.wait_ge(x4_ready, (r + 1) * GRP)
                V.tensor_reduce(msum[:, :], x4[:, :, :], AX.X, ALU.add).then_inc(msum_ready, GRP)
                dve.wait_ge(score_mm, r + 1)
                wide = [1, GRP, E2]
                chain.link(V.tensor_scalar(sc[:, :, :], P[0:1, 1, 0:GRP * E2].rearrange("p (u e) -> p u e", u=GRP),
                                           1.0 / L, None, ALU.mult))
                chain.link(V.tensor_tensor(sc[:, :, :], sc[:, :, :], bg_s[:, :].unsqueeze(1).to_broadcast(wide), ALU.add))
                chain.link(V.tensor_reduce(top[:, :], sc[:, :, :], AX.X, ALU.max))
                V.tensor_tensor(sc[:, :, :], sc[:, :, :], top[:, :].unsqueeze(2).to_broadcast(wide), ALU.subtract)\
                 .then_inc(sc_ready, 1)
                dve.wait_ge(sc_exp, r + 1)
                chain.link(V.tensor_reduce(tot[:, :], sc[:, :, :], AX.X, ALU.add))
                chain.link(V.reciprocal(tot[:, :], tot[:, :]))
                chain.link(V.tensor_tensor(sc[:, :, :], sc[:, :, :], tot[:, :].unsqueeze(2).to_broadcast(wide), ALU.mult))
                chain.link(V.tensor_reduce(gate[:, :], sc[:, :, :], AX.X, ALU.max))
                chain.link(V.tensor_tensor(worse[:, :, :], sc[:, :, :], gate[:, :].unsqueeze(2).to_broadcast(wide),
                                           ALU.is_lt))
                chain.link(V.scalar_tensor_tensor(worse[:, :, :], worse[:, :, :], float(E2),
                                                  enum_s[:, :].unsqueeze(1).to_broadcast(wide), ALU.mult, ALU.add))
                chain.link(V.tensor_reduce(bestf[:, :], worse[:, :, :], AX.X, ALU.min))
                chain.end()
                V.tensor_copy(best[:, :], bestf[:, :]).then_inc(gate_ready, 1)
                if known(r, 1):
                    dve.wait_ge(out_stored, r * 16)
                for u in range(GRP):
                    dve.wait_ge(y_mm, r * GRP + u + 1)
                    dve.wait_ge(bsel_ready, r * GRP + u + 1)
                    V.scalar_tensor_tensor(fin[:, u, :], P[:, 2 * u, 0:L], bsel[:, u:u + 1], h3[:, u, :], ALU.add, ALU.add)\
                     .then_inc(fin_ready, 1)

            V.memset(mean3[:, :], 1.0 / D).then_inc(consts3_set, 1)
            V.memset(ones3[:, :], 1.0).then_inc(consts3_set, 1)
            V.memset(eps3[:, :], 1e-5).then_inc(consts3_set, 1)
            dve.wait_ge(consts3_in, 16 * len(loads))
            group(0)
            with dve.Fori(1, R) as r:
                group(r)


def early_fusion(nc, x, txt, tok_w, pos, vecs, wqkv, wo, wr, br, w1, w2, b2, wp, wo1, wg, bg, we, be,
                 ident, tri, expert_rows, eye_blocks, read_mask, expert_numbers, out):
    f32 = mybir.dt.float32
    h2_d = nc.dram_tensor("h2_d", [B, D, L], f32).ap()
    feat_d = nc.dram_tensor("feat_d", [B, L, FW], f32).ap()
    read_d = nc.dram_tensor("read_d", [B, L, D], f32).ap()
    images(nc, x, txt, tok_w, pos, vecs, wqkv, wo, wr, br, w1, w2, b2, wp, ident, tri, expert_rows, h2_d, feat_d)
    memory(nc, feat_d, ident, eye_blocks, read_mask, read_d)
    experts_out(nc, read_d, h2_d, vecs, wo1, wg, bg, we, be, ident, expert_numbers, out)


_OUT = (B, D, L)


def kernel(**inputs):
    import numpy as np
    import concourse.bacc as bacc
    from concourse.bass_utils import run_bass_kernel_spmd

    a = {k: np.asarray(v) for k, v in inputs.items()}

    def col(v):
        return v.reshape(-1, 128).T

    xs = a["x"].reshape(B, 3, 11, 16, 13, 16).transpose(0, 3, 5, 1, 2, 4).reshape(B, KC, 128, PATCHES)
    vecs = [a["L0_tok_b"], a["L0_tok_cls_token"].reshape(D), a["L0_attn_bq"], a["L0_attn_bk"], a["L0_attn_bv"],
            a["L0_attn_bo"], a["L0_attn_gamma"], a["L0_attn_beta"], a["L1_attn_bo"]]
    feeds = [
        ("x", xs.transpose(0, 2, 1, 3)),
        ("txt", a["txt"].transpose(0, 2, 1)),
        ("tok_w", a["L0_tok_W"].T.reshape(KC, 128, D).transpose(1, 0, 2)),
        ("pos", np.broadcast_to(a["L0_tok_pos_emb"].reshape(1, LX), (128, LX))),
        ("vecs", np.concatenate([v.reshape(D, 1) for v in vecs] + [col(a["L0_ffn_b1"].reshape(-1))], axis=1)),
        ("wqkv", np.stack([a["L0_attn_Wq"].T, a["L0_attn_Wk"].T, a["L0_attn_Wv"].T], axis=1)),
        ("wo", a["L0_attn_Wo"].T),
        ("wr", a["L0_ffn_Wr"].T),
        ("br", np.broadcast_to(a["L0_ffn_br"].reshape(1, E1), (128, E1))),
        ("w1", a["L0_ffn_W1"].transpose(1, 0, 2)),
        ("w2", a["L0_ffn_W2"].reshape(E1, 2, 128, D).transpose(2, 0, 1, 3)),
        ("b2", a["L0_ffn_b2"]),
        ("wp", np.concatenate([a["L1_attn_Wk"], a["L1_attn_Wq"], a["L1_attn_Wv"], a["L1_attn_Wg"]], axis=1)),
        ("wo1", a["L1_attn_Wo"]),
        ("wg", a["L1_ffn_Wg"]),
        ("bg", a["L1_ffn_bg"].reshape(1, E2)),
        ("we", a["L1_ffn_We"].transpose(1, 0, 2).reshape(D, E2 * D)),
        ("be", a["L1_ffn_be"].T),
        ("ident", np.eye(128, dtype=np.float32)),
        ("tri", np.broadcast_to(np.tri(E1, k=-1, dtype=np.float32), (128, E1, E1))),
        ("expert_rows", np.repeat(np.eye(E1, dtype=np.float32)[:, :, None], 128, axis=2)),
        ("eye_blocks", np.broadcast_to(np.eye(SUB, dtype=np.float32)[None, :, None, :], (128, SUB, 4, SUB))),
        ("read_mask", np.tile(np.triu(np.ones((B, B), np.float32)), (2, 1))),
        ("expert_numbers", np.arange(E2, dtype=np.float32).reshape(1, E2)),
    ]
    nc = bacc.Bacc("TRN2", target_bir_lowering=False, num_devices=1)
    arrays, args = {}, []
    for name, v in feeds:
        v = np.ascontiguousarray(v)
        arrays[f"in_{name}"] = v
        args.append(nc.dram_tensor(f"in_{name}", v.shape, mybir.dt.from_np(v.dtype), kind="ExternalInput").ap())
    out = nc.dram_tensor("out", _OUT, mybir.dt.float32, kind="ExternalOutput").ap()
    early_fusion(nc, *args, out)
    r = run_bass_kernel_spmd(nc, [arrays], core_ids=[0])
    return np.ascontiguousarray(r.results[0]["out"].transpose(0, 2, 1))
```

```python
import concourse.bass as bass
from concourse import mybir
from contextlib import ExitStack

B = 64
D = 128
PATCHES = 143
LX = PATCHES + 1
TXT = 128
L = LX + TXT
KC = 768 // 128
H = 8
DH = D // H
T = L // H
HALF = L // 2
E1 = 8
HID = 256
E2 = 16
PHI = 2 * DH
FK = H * PHI
FW = 3 * FK + D
RT = -(-L // 3)
TILES = ((0, 0), (1, RT), (2, L - RT))
KT = ((0, RT), (RT, RT), (2 * RT, L - 2 * RT))
SUB = 32
PAIRS = 16
QUADS = PAIRS // 4
GRP = 4
ROUTER_STEPS, FEATURE_STEPS, SOLVE_STEPS, GATE_STEPS = 10, 4, 2 * (SUB - 1), 10
MAX_STEPS, PART_STEPS, PROD_STEPS, COMB_STEPS = 4, 3, 4, 3
PARTS = 3
GATES = PARTS * E1
LAST = 2 * E1
PAIRED = ((0, 0), (0, 1), (0, 2), (1, 0), (1, 1), (2, 0))
BLOCKS = len(PAIRED) * DH
ROWS = BLOCKS + PARTS
CTX_ROWS = 3 * 32 + DH + 1
VECS = ("tok_b", "cls", "bq", "bk", "bv", "bo", "gamma", "beta", "bo1") + tuple(f"b1_{i}" for i in range(2 * E1))
NV = len(VECS)


class Chain:

    def __init__(self, eng, s, per_round):
        self.eng, self.s, self.per_round, self.n, self.r = eng, s, per_round, 0, 0

    def start(self, r):
        self.n, self.r = 0, r

    def link(self, ins):
        self.n += 1
        ins.then_inc(self.s, 1)
        self.eng.wait_ge(self.s, self.r * self.per_round + self.n)

    def end(self):
        assert self.n == self.per_round, (self.n, self.per_round)


def known(b, least):
    return not isinstance(b, int) or b >= least


def there(b):
    return not isinstance(b, int) or 0 <= b < B


def images(nc, x, txt, tok_w, pos, vecs, wqkv, wo, wr, br, w1, w2, b2, wp, ident, tri, expert_rows, h2_d, feat_d):
    f32 = mybir.dt.float32
    bf16 = mybir.dt.bfloat16
    ALU = mybir.AluOpType
    ACT = mybir.ActivationFunctionType
    AX = mybir.AxisListType

    ctx = ExitStack()
    with ctx:
        def sb(name, shape, dt=f32):
            return ctx.enter_context(nc.sbuf_tensor(name, shape, dt))

        def sem(name):
            return ctx.enter_context(nc.semaphore(name))

        tokw_s = sb("tokw_s", [128, KC, D])
        vec_s = sb("vec_s", [128, NV])
        wqkv_s = sb("wqkv_s", [128, 3, D])
        wo_s = sb("wo_s", [128, D])
        wr_s = sb("wr_s", [128, E1])
        br_s = sb("br_s", [128, E1])
        w1_s = sb("w1_s", [128, E1, HID])
        w2_s = sb("w2_s", [128, E1, 2, D])
        b2_s = sb("b2_s", [GATES, D])
        b2_left = sb("b2_left", [GATES, D])
        b2_h = sb("b2_h", [GATES, PARTS, D], bf16)
        wp_s = sb("wp_s", [128, 3 * D + H])
        ident_s = sb("ident_s", [128, 128])
        tri_s = sb("tri_s", [128, E1, E1])
        erow_s = sb("erow_s", [GATES, E1, 128])
        erow_h = sb("erow_h", [GATES, E1, 128], bf16)
        pos_s = sb("pos_s", [128, LX])
        mean_w = sb("mean_w", [128, 128])
        ones_s = sb("ones_s", [128, 128])
        eps_s = sb("eps_s", [128, 1])
        ident_h = sb("ident_h", [128, 128], bf16)

        def vec(name):
            i = VECS.index(name)
            return vec_s[:, i:i + 1]

        xb = sb("xb", [128, KC, PATCHES])
        h0 = sb("h0", [128, 2, L])
        kept = sb("kept", [128, L])
        xn1 = sb("xn1", [128, 2, L])
        xc = sb("xc", [128, 2, L])
        text = sb("text", [128, TXT])
        sq = sb("sq", [128, 2, L])
        sd = sb("sd", [RT, 2, 3])
        rstd = sb("rstd", [RT, 2, 3])
        diag = sb("diag", [RT, 2, 3, RT])
        qkvT = sb("qkvT", [128, 3, L])
        parts = sb("parts", [128, 2, PARTS, L], bf16)
        left = sb("left", [128, 2, L])
        qs = sb("qs", [ROWS, H, L], bf16)
        ks = sb("ks", [ROWS, H, L], bf16)
        vd = sb("vd", [DH + 1, H, L])
        vaug = sb("vaug", [RT, H, 3, DH + 1])
        nmx = sb("nmx", [RT, 2, 3])
        nleft = sb("nleft", [RT, 3])
        nparts = sb("nparts", [RT, 2, 3, PARTS], bf16)
        pT = sb("pT", [RT, H, 3, L])
        ctxu = sb("ctxu", [CTX_ROWS, 2, L])
        cfm = sb("cfm", [128, L])
        den = sb("den", [128, L])
        y1 = sb("y1", [128, L])
        z1 = sb("z1", [128, L])
        z2 = sb("z2", [128, L])
        h1 = sb("h1", [128, 2, L])
        x2 = sb("x2", [128, 2, L])
        lg = sb("lg", [RT, 3, E1])
        ex = sb("ex", [RT, 3, E1])
        r8 = sb("r8", [RT, 3])
        cmp1 = sb("cmp1", [RT, 3, E1, E1])
        cmp2 = sb("cmp2", [RT, 3, E1, E1])
        rank = sb("rank", [RT, 3, E1])
        comb = sb("comb", [RT, 3, E1])
        comb_left = sb("comb_left", [RT, 3, E1])
        comb_parts = sb("comb_parts", [RT, 3, PARTS, E1], bf16)
        combT = sb("combT", [GATES, 2, L], bf16)
        gl = sb("gl", [128, 2, 2, L])
        hs = sb("hs", [128, 2, 2, L])
        h2 = sb("h2", [128, L])
        x3 = sb("x3", [128, L])
        relu = sb("relu", [RT, 2, 3, 2, H, PHI])
        prod = sb("prod", [RT, 3, 2 * H, PHI])
        fsum = sb("fsum", [RT, 3, 2 * H])
        val = sb("val", [RT, 2, 3, H, DH])
        bta = sb("bta", [RT, 2, 3, H])
        feat = sb("feat", [RT, 3, FW])

        P = ctx.enter_context(nc.psum_tensor("P1", [128, 8, 512], f32))
        qk_d = nc.dram_tensor("qk_d", [DH, 2, PARTS, H, L], bf16).ap()
        v_d = nc.dram_tensor("v_d", [DH, H, L], f32).ap()
        ctx_d = nc.dram_tensor("ctx_d", [H, DH + 1, L], f32).ap()

        consts_in = sem("consts_in")
        consts_set = sem("consts_set")
        pos_ready = sem("pos_ready")
        x_in = sem("x_in")
        txt_in = sem("txt_in")
        text_ready = sem("text_ready")
        tok_mm = sem("tok_mm")
        h0_ready = sem("h0_ready")
        q_mm = sem("q_mm")
        k_mm = sem("k_mm")
        v_mm = sem("v_mm")
        q_out = sem("q_out")
        k_out = sem("k_out")
        v_out = sem("v_out")
        parts_ready = sem("parts_ready")
        part_step = sem("part_step")
        kept_ready = sem("kept_ready")
        max_ready = sem("max_ready")
        max_step = sem("max_step")
        prod_step = sem("prod_step")
        sums_ready = sem("sums_ready")
        gated_step = sem("gated_step")
        qk_stored = sem("qk_stored")
        v_stored = sem("v_stored")
        qk_in = sem("qk_in")
        v_in = sem("v_in")
        v_tr = sem("v_tr")
        vaug_ready = sem("vaug_ready")
        s_mm = sem("s_mm")
        max_tr = sem("max_tr")
        max_row = sem("max_row")
        st_mm = sem("st_mm")
        probs = sem("probs")
        pv_mm = sem("pv_mm")
        ctx_out = sem("ctx_out")
        ctx_stored = sem("ctx_stored")
        cfm_in = sem("cfm_in")
        den_in = sem("den_in")
        den_ready = sem("den_ready")
        cfm_ready = sem("cfm_ready")
        wo_mm = sem("wo_mm")
        y1_ready = sem("y1_ready")
        z2_ready = sem("z2_ready")
        h1_ready = sem("h1_ready")
        router_mm = sem("router_mm")
        lg_ready = sem("lg_ready")
        ex_ready = sem("ex_ready")
        comb_ready = sem("comb_ready")
        comb_step = sem("comb_step")
        comb_split = sem("comb_split")
        comb_tr = sem("comb_tr")
        b2_step = sem("b2_step")
        combT_ready = sem("combT_ready")
        up_mm = sem("up_mm")
        gelu_done = sem("gelu_done")
        bc_mm = sem("bc_mm")
        hs_ready = sem("hs_ready")
        down_mm = sem("down_mm")
        h2_ready = sem("h2_ready")
        h2_stored = sem("h2_stored")
        proj_mm = sem("proj_mm")
        proj_out = sem("proj_out")
        feat_ready = sem("feat_ready")
        feat_stored = sem("feat_stored")
        router_step = sem("router_step")
        feature_step = sem("feature_step")

        class Norm:

            def __init__(self, name):
                self.mean_mm = sem(name + "_mean_mm")
                self.centred = sem(name + "_centred")
                self.squared = sem(name + "_squared")
                self.var_mm = sem(name + "_var_mm")
                self.sd_ready = sem(name + "_sd_ready")
                self.rstd_ready = sem(name + "_rstd_ready")
                self.diag_ready = sem(name + "_diag_ready")
                self.bc_mm = sem(name + "_bc_mm")
                self.ready = sem(name + "_ready")

        ln_a, ln_b = Norm("ln_a"), Norm("ln_b")

        def halves(first, second):
            return range(0 if there(first) else 1, 2 if there(second) else 1)

        loads = [(tokw_s, tok_w), (vec_s, vecs), (wqkv_s, wqkv), (wo_s, wo), (wr_s, wr), (br_s, br), (w1_s, w1),
                 (w2_s, w2), (b2_s, b2), (wp_s, wp), (ident_s, ident), (tri_s, tri), (erow_s, expert_rows),
                 (pos_s, pos)]
        NSET = 8

        block = ctx.enter_context(nc.Block())

        def schedule(round_):
            for i in range(5):
                round_(i, i % 2)
            with round_.eng.Fori(5, B - 4, 2) as i:
                round_(i, 1)
                round_(i + 1, 0)
            for i in range(B - 3, B + 4):
                round_(i, i % 2)

        @block.sync
        def _(sp):
            def at(b):
                return b if isinstance(b, int) else sp.snap(b)

            def load_x(b):
                sp.dma_start(xb[:, :, :], x[bass.ds(b, 1)].rearrange("o p c n -> p (o c) n")).then_inc(x_in, 16)

            def load_text(b):
                sp.dma_start(text[:, :], txt[bass.ds(b, 1)].rearrange("o p n -> p (o n)")).then_inc(txt_in, 16)

            def store_qkv(b):
                sp.wait_ge(v_out, b + 1)
                for j in range(H):
                    sp.dma_start(v_d[:, :, j * T:(j + 1) * T],
                                 qkvT[j * DH:(j + 1) * DH, 2, :].rearrange("d (h t) -> d h t", h=H)).then_inc(v_stored, 16)
                sp.wait_ge(parts_ready, b + 1)
                for j in range(H):
                    sp.dma_start(qk_d[:, :, :, :, j * T:(j + 1) * T].rearrange("d a c h t -> d (a c) h t"),
                                 parts[j * DH:(j + 1) * DH, :, :, :].rearrange("d a c (h t) -> d (a c) h t", h=H))\
                      .then_inc(qk_stored, 16)

            def load_qkv(b):
                sp.wait_ge(v_stored, (b + 1) * 16 * H)
                sp.dma_start(vd[1:DH + 1, :, :], v_d).then_inc(v_in, 16)
                sp.wait_ge(qk_stored, (b + 1) * 16 * H)
                for a, dst in ((0, qs), (1, ks)):
                    for n, pair in enumerate(PAIRED):
                        sp.dma_start(dst[n * DH:(n + 1) * DH, :, :], qk_d[:, a, pair[a], :, :]).then_inc(qk_in, 16)

            def store_contexts(c):
                for g in range(4):
                    h = 4 * c + g
                    sp.dma_start(ctx_d[:, :, h * T:(h + 1) * T].rearrange("j r t -> r j t"),
                                 ctxu[32 * g:32 * g + DH + 1, c, :].rearrange("r (j t) -> r j t", j=H))\
                      .then_inc(ctx_stored, 16)

            class Round:
                eng = sp

                def __call__(self, i, p):
                    beyond, ahead, behind, last = at(i + 2), at(i + 1), at(i - 2), at(i - 4)
                    if there(i + 2):
                        sp.wait_ge(tok_mm, i + 2)
                        load_x(beyond)
                    if there(i + 1):
                        sp.wait_ge(text_ready, i + 1)
                        load_text(ahead)
                        store_qkv(i + 1)
                    if there(i):
                        sp.wait_ge(ctx_out, i * 2 + 1)
                        if there(i - 1):
                            sp.wait_ge(h1_ready, i)
                        store_contexts(0)
                        sp.wait_ge(ctx_out, i * 2 + 2)
                        store_contexts(1)
                        if there(i + 1):
                            load_qkv(i + 1)
                        sp.wait_ge(ctx_stored, (i + 1) * 16 * H)
                        sp.dma_start(cfm[:, :], ctx_d[:, 1:DH + 1, :]).then_inc(cfm_in, 16)
                        sp.dma_start(den[:, :], ctx_d[:, 0:1, :].to_broadcast([H, DH, L])).then_inc(den_in, 16)
                    if there(i - 4):
                        sp.wait_ge(feat_ready, i - 3)
                        for t, s in TILES:
                            r = 2 * RT - s if t == 2 else 0
                            sp.dma_start(feat_d[bass.ds(last, 1), s + r:s + RT, :].rearrange("o p n -> (o p) n"),
                                         feat[r:RT, t, :]).then_inc(feat_stored, 16)
                    if there(i - 2):
                        sp.wait_ge(h2_ready, i - 1)
                        sp.dma_start(h2_d[bass.ds(behind, 1)].rearrange("o p n -> p (o n)"), h2[:, :])\
                          .then_inc(h2_stored, 16)

            for dst, src in loads:
                sp.dma_start(dst[:], src).then_inc(consts_in, 16)
            load_x(0)
            load_text(0)
            sp.wait_ge(tok_mm, 1)
            load_x(1)
            store_qkv(0)
            load_qkv(0)
            schedule(Round())
            sp.wait_ge(h2_stored, B * 16)
            sp.wait_ge(feat_stored, B * 48)

        @block.tensor
        def _(pe):
            mm = nc.tensor.matmul

            def mean(half, src):
                return mm(P[:, 6 + half, 0:L], mean_w[:, :], src, start=True, stop=True)

            def variance(n, r, which):
                pe.wait_ge(n.squared, r + 1)
                for half in which:
                    for t, s in TILES:
                        last = mm(P[0:RT, 6, 3 * half + t:3 * half + t + 1], sq[:, half, s:s + RT], mean_w[:, 0:1],
                                  start=True, stop=True)
                last.then_inc(n.var_mm, 1)

            def spread(n, r, which):
                pe.wait_ge(n.diag_ready, r + 1)
                for half in which:
                    for t, s in TILES:
                        last = mm(P[:, 6 + half, s:s + RT], ones_s[0:RT, :], diag[:, half, t, :], start=True, stop=True)
                last.then_inc(n.bc_mm, 1)

            def tokens(b):
                pe.wait_ge(x_in, (b + 1) * 16)
                if known(b, 1):
                    pe.wait_ge(k_out, b)
                if known(b, 5):
                    pe.wait_ge(proj_out, (b - 4) * 3)
                for c in range(KC):
                    last = mm(P[:, 7, 0:PATCHES], tokw_s[:, c, :], xb[:, c, :], start=(c == 0), stop=(c == KC - 1))
                last.then_inc(tok_mm, 1)

            def first(k, i, p):
                which = halves(i - 1, i + 1)
                if k == 0 and there(i - 1):
                    pe.wait_ge(cfm_ready, i)
                    if known(i, 2):
                        pe.wait_ge(combT_ready, i - 1)
                    mm(P[:, 6, 0:L], wo_s[:, :], cfm[:, :], start=True, stop=True).then_inc(wo_mm, 1)
                elif k == 2 and which:
                    if there(i + 1):
                        pe.wait_ge(h0_ready, i + 2)
                        pe.wait_ge(text_ready, i + 2)
                        last = mean(1, h0[:, 1 - p, :])
                    if there(i - 1):
                        pe.wait_ge(y1_ready, i)
                        last = mean(0, y1[:, :])
                    last.then_inc(ln_a.mean_mm, 1)
                elif k == 5 and which:
                    variance(ln_a, i + 1, which)
                elif k == 9 and which:
                    spread(ln_a, i + 1, which)
                elif k == 11 and there(i + 1):
                    pe.wait_ge(ln_a.ready, i + 2)
                    mm(P[:, 6, 0:L], wqkv_s[:, 0, :], xn1[:, 1 - p, :], start=True, stop=True).then_inc(q_mm, 1)
                    mm(P[:, 7, 0:L], wqkv_s[:, 1, :], xn1[:, 1 - p, :], start=True, stop=True).then_inc(k_mm, 1)
                elif k == 13 and there(i + 1):
                    pe.wait_ge(q_out, i + 2)
                    mm(P[:, 6, 0:L], wqkv_s[:, 2, :], xn1[:, 1 - p, :], start=True, stop=True).then_inc(v_mm, 1)

            def second(k, i, p):
                which = halves(i - 1, i - 3)
                b = i - 3
                if k == 0 and which:
                    if there(i - 1):
                        pe.wait_ge(h1_ready, i)
                        if there(i + 1):
                            pe.wait_ge(v_out, i + 2)
                        last = mean(0, h1[:, 1 - p, :])
                    else:
                        pe.wait_ge(combT_ready, B)
                    if there(b):
                        if there(i + 1):
                            pe.wait_ge(k_out, i + 2)
                        elif known(b, 1):
                            pe.wait_ge(proj_out, b * 3)
                        pe.wait_ge(h2_ready, b + 1)
                        last = mean(1, h2[:, :])
                    last.then_inc(ln_b.mean_mm, 1)
                elif k == 2 and which:
                    variance(ln_b, i - 1, which)
                elif k == 5 and which:
                    spread(ln_b, i - 1, which)
                elif k == 6:
                    if which:
                        pe.wait_ge(ln_b.ready, i)
                    if there(i - 1):
                        for t, s in TILES:
                            last = mm(P[0:RT, 6, t * E1:(t + 1) * E1], x2[:, 1 - p, s:s + RT], wr_s[:, :],
                                      start=True, stop=True)
                        last.then_inc(router_mm, 1)
                    if there(b):
                        mm(P[0:RT, 7, 0:3 * D + H], x3[:, 0:RT], wp_s[:, :], start=True, stop=True).then_inc(proj_mm, 1)
                elif k == 8 and there(b):
                    if there(i - 1):
                        pe.wait_ge(lg_ready, i)
                    mm(P[0:RT, 6, 0:3 * D + H], x3[:, RT:2 * RT], wp_s[:, :], start=True, stop=True).then_inc(proj_mm, 1)
                elif k == 10 and there(b):
                    pe.wait_ge(proj_out, b * 3 + 1)
                    mm(P[0:RT, 7, 0:3 * D + H], x3[:, L - RT:L], wp_s[:, :], start=True, stop=True).then_inc(proj_mm, 1)
                elif k == LAST and there(i - 1):
                    pe.wait_ge(comb_split, i)
                    if there(b):
                        pe.wait_ge(proj_out, b * 3 + 2)
                    for t, s in TILES:
                        last = mm(P[0:GATES, 6, s:s + RT], comb_parts[:, t, :, :].rearrange("p c e -> p (c e)"),
                                  ident_h[0:RT, 0:RT], start=True, stop=True)
                    last.then_inc(comb_tr, 1)

            def scores(b, h):
                for a in range(2):
                    for t, (k0, nk) in enumerate(KT):
                        last = mm(P[0:nk, a, t * HALF:(t + 1) * HALF], qs[0:BLOCKS, h, k0:k0 + nk],
                                  ks[0:BLOCKS, h, a * HALF:(a + 1) * HALF], start=True, stop=True)
                last.then_inc(s_mm, 1)

            def start(b):
                pe.wait_ge(qk_in, (b + 1) * 16 * 2 * len(PAIRED))
                scores(b, 0)

            def shifted(b, h):
                pe.wait_ge(max_row, b * H + h + 1)
                if h:
                    pe.wait_ge(probs, b * H + h)
                for a in range(2):
                    for t, (k0, nk) in enumerate(KT):
                        last = mm(P[0:nk, 2 + a, t * HALF:(t + 1) * HALF], ks[:, h, k0:k0 + nk],
                                  qs[:, h, a * HALF:(a + 1) * HALF], start=True, stop=True)
                last.then_inc(st_mm, 1)

            def values(b, c):
                pe.wait_ge(probs, b * H + 4 * c + 4)
                if c:
                    pe.wait_ge(ctx_out, b * 2 + 1)
                for t, (k0, nk) in enumerate(KT):
                    for g in range(4):
                        last = mm(P[32 * g:32 * g + DH + 1, 4, 0:L], vaug[0:nk, 4 * c + g, t, :],
                                  pT[0:nk, 4 * c + g, t, :], start=(t == 0), stop=(t == 2), tile_position=(0, 32 * g))
                last.then_inc(pv_mm, 1)

            def up(b, e, p):
                if e >= 2:
                    pe.wait_ge(gelu_done, b * 2 * E1 + 2 * (e - 1))
                for k in range(2):
                    last = mm(P[:, 2 * (e % 2) + k, 0:L], w1_s[:, e, k * D:(k + 1) * D], x2[:, p, :],
                              start=True, stop=True)
                last.then_inc(up_mm, 1)

            def down(b, e):
                pe.wait_ge(hs_ready, b * E1 + e + 1)
                for k in range(2):
                    last = mm(P[:, 5, 0:L], w2_s[:, e, k, :], hs[:, e % 2, k, :],
                              start=False, stop=(e == E1 - 1 and k == 1))
                last.then_inc(down_mm, 1)

            def maxima(b, h):
                pe.wait_ge(max_step, (b * H + h + 1) * MAX_STEPS)
                if h:
                    pe.wait_ge(max_row, b * H + h)
                for t, (k0, nk) in enumerate(KT):
                    last = mm(P[0:PARTS, 5, k0:k0 + nk], nparts[0:nk, h % 2, t, :], ident_h[0:nk, 0:nk],
                              start=True, stop=True)
                last.then_inc(max_tr, 1)

            class Round:
                eng = pe

                def __call__(self, i, p):
                    heads, experts = there(i), there(i - 2)
                    if heads:
                        pe.wait_ge(v_in, (i + 1) * 16)
                        if known(i, 3):
                            pe.wait_ge(h2_ready, i - 2)
                        pe.wait_ge(max_ready, i * H + 1)
                        scores(i, 1)
                        for h in range(H):
                            for t, (k0, nk) in enumerate(KT):
                                c = (h * 3 + t) * (DH + 1)
                                last = nc.tensor.transpose(P[0:nk, 5, c:c + DH + 1], vd[:, h, k0:k0 + nk],
                                                           ident_s[0:DH + 1, 0:DH + 1])
                        last.then_inc(v_tr, 1)
                        pe.wait_ge(vaug_ready, i + 1)
                        maxima(i, 0)
                    for h in range(H):
                        if heads and h + 2 < H:
                            pe.wait_ge(max_ready, i * H + h + 2)
                            scores(i, h + 2)
                        if heads and h == 5:
                            values(i, 0)
                        first(2 * h, i, p)
                        if heads and h + 1 < H:
                            maxima(i, h + 1)
                        if heads:
                            shifted(i, h)
                        first(2 * h + 1, i, p)
                    if experts:
                        up(i - 2, 0, p)
                        pe.wait_ge(combT_ready, i - 1)
                        if not heads:
                            pe.wait_ge(h2_ready, i - 2)
                        for c in range(PARTS):
                            mm(P[:, 5, 0:L], b2_h[:, c, :], combT[:, p, :], start=c == 0, stop=False)
                    if heads:
                        values(i, 1)
                    for e in range(E1):
                        if experts:
                            if e + 1 < E1:
                                up(i - 2, e + 1, p)
                            if e:
                                down(i - 2, e - 1)
                            if e == 0 and heads:
                                pe.wait_ge(ctx_out, (i + 1) * 2)
                            mm(P[:, 4, 0:L], erow_h[:, e, :], combT[:, p, :], start=True, stop=True).then_inc(bc_mm, 1)
                        if e == E1 - 1 and there(i + 1):
                            if experts:
                                pe.wait_ge(gelu_done, ((i - 2) * E1 + E1 - 1) * 2)
                            start(i + 1)
                        for k in (2 * e, 2 * e + 1):
                            second(k, i, p)
                    if there(i + 2):
                        tokens(i + 2)
                    if experts:
                        down(i - 2, E1 - 1)
                    second(LAST, i, p)

            pe.wait_ge(consts_in, 16 * len(loads))
            pe.wait_ge(consts_set, NSET)
            tokens(0)
            for k in range(16):
                first(k, -1, 1)
            pe.wait_ge(v_out, 1)
            tokens(1)
            start(0)
            schedule(Round())

        @block.gpsimd
        def _(pool):
            tt = nc.gpsimd.tensor_tensor

            def copy(dst, src):
                one = ones_s[0:src.shape[0], 0:1]
                for _ in range(len(src.shape) - 2):
                    one = one.unsqueeze(1)
                return tt(dst, src, one.to_broadcast(list(src.shape)), ALU.mult)

            tops = Chain(pool, max_step, MAX_STEPS * H)
            split = Chain(pool, part_step, PART_STEPS)
            prods = Chain(pool, prod_step, PROD_STEPS)
            gated = Chain(pool, gated_step, 1)
            gates = Chain(pool, comb_step, COMB_STEPS)

            def maximum_parts(b, h):
                if h == 0:
                    tops.start(b)
                pool.wait_ge(max_ready, b * H + h + 1)
                if h >= 2:
                    pool.wait_ge(max_tr, b * H + h - 1)
                part = [nparts[:, h % 2, :, c] for c in range(PARTS)]
                top = nmx[:, h % 2, :]
                tops.link(copy(part[0], top))
                tops.link(tt(nleft[:, :], top, part[0], ALU.subtract))
                tops.link(copy(part[1], nleft[:, :]))
                tops.link(tt(part[2], nleft[:, :], part[1], ALU.subtract))
                if h == H - 1:
                    tops.end()

            def split_qk(b):
                split.start(b)
                pool.wait_ge(q_out, b + 1)
                pool.wait_ge(k_out, b + 1)
                if known(b, 1):
                    pool.wait_ge(parts_ready, b)
                    pool.wait_ge(qk_stored, b * 16 * H)
                qk = qkvT[:, 0:2, :]
                split.link(copy(parts[:, :, 0, :], qk))
                split.link(tt(left[:, :, :], qk, parts[:, :, 0, :], ALU.subtract))
                split.link(copy(parts[:, :, 1, :], left[:, :, :]))
                split.end()
                tt(parts[:, :, 2, :], left[:, :, :], parts[:, :, 1, :], ALU.subtract).then_inc(parts_ready, 1)

            def split_gates(b):
                gates.start(b)
                pool.wait_ge(comb_ready, b + 1)
                if known(b, 1):
                    pool.wait_ge(comb_tr, b)
                gates.link(copy(comb_parts[:, :, 0, :], comb[:, :, :]))
                gates.link(tt(comb_left[:, :, :], comb[:, :, :], comb_parts[:, :, 0, :], ALU.subtract))
                gates.link(copy(comb_parts[:, :, 1, :], comb_left[:, :, :]))
                gates.end()
                tt(comb_parts[:, :, 2, :], comb_left[:, :, :], comb_parts[:, :, 1, :], ALU.subtract)\
                    .then_inc(comb_split, 1)

            def products(k, b, f):
                r = relu[:, f, :, :, :, :].rearrange("p t a h f -> p t (a h) f")
                if k == 2:
                    prods.start(b)
                    pool.wait_ge(proj_out, (b + 1) * 3)
                    if known(b, 1):
                        pool.wait_ge(feat_ready, b)
                    prods.link(tt(prod[:, :, :, 0:1], r[:, :, :, 0:1], r[:, :, :, PHI - 1:PHI], ALU.mult))
                elif k in (3, 4, 5):
                    t = k - 3
                    prods.link(tt(prod[:, t, :, 1:PHI], r[:, t, :, 1:PHI], r[:, t, :, 0:PHI - 1], ALU.mult))
                    if t == 2:
                        prods.end()

            def features(b, f):
                pool.wait_ge(sums_ready, b + 1)
                if known(b, 1):
                    pool.wait_ge(feat_stored, b * 48)
                wide = [RT, 3, H, PHI]
                heads = [feat[:, :, c * FK:(c + 1) * FK].rearrange("p t (h f) -> p t h f", h=H) for c in range(3)]
                gate = bta[:, f, :, :].unsqueeze(3)
                gated.start(b)
                gated.link(tt(heads[0], prod[:, :, 0:H, :], fsum[:, :, 0:H].unsqueeze(3).to_broadcast(wide), ALU.mult))
                gated.end()
                tt(heads[2], prod[:, :, H:2 * H, :], fsum[:, :, H:2 * H].unsqueeze(3).to_broadcast(wide), ALU.mult)
                tt(heads[1], heads[0], gate.to_broadcast(wide), ALU.mult)
                tt(feat[:, :, 3 * FK:FW].rearrange("p t (h f) -> p t h f", h=H), val[:, f, :, :, :],
                   gate.to_broadcast([RT, 3, H, DH]), ALU.mult).then_inc(feat_ready, 1)

            class Round:
                eng = pool

                def __call__(self, i, p):
                    if there(i - 1):
                        pool.wait_ge(h0_ready, i)
                        pool.wait_ge(text_ready, i)
                        if known(i, 2):
                            pool.wait_ge(h1_ready, i - 1)
                        copy(kept[:, :], h0[:, 1 - p, :]).then_inc(kept_ready, 1)
                    for h in range(H):
                        if there(i):
                            maximum_parts(i, h)
                        if there(i - 4):
                            products(h, i - 4, p)
                    if there(i + 1):
                        split_qk(i + 1)
                    if there(i - 4):
                        features(i - 4, p)
                    if there(i - 1):
                        split_gates(i - 1)

            pool.wait_ge(consts_set, NSET)
            split_qk(0)
            schedule(Round())

        @block.scalar
        def _(act):
            A = nc.scalar.activation

            def squares(n, r, which):
                act.wait_ge(n.centred, r + 1)
                f = slice(which[0], which[-1] + 1)
                A(sq[:, f, :], xc[:, f, :], ACT.Square).then_inc(n.squared, 1)

            def deviation(n, r, which):
                act.wait_ge(n.var_mm, r + 1)
                f = slice(which[0], which[-1] + 1)
                A(sd[:, f, :], P[0:RT, 6, 3 * f.start:3 * f.stop].rearrange("p (h t) -> p h t", t=3), ACT.Sqrt,
                  bias=eps_s[0:RT, :]).then_inc(n.sd_ready, 1)

            def first(k, i, p):
                which = halves(i - 1, i + 1)
                if k == 0 and there(i + 1):
                    act.wait_ge(txt_in, (i + 2) * 16)
                    if there(i - 1):
                        act.wait_ge(kept_ready, i)
                    A(h0[:, 1 - p, LX:L], text[:, :], ACT.Copy).then_inc(text_ready, 1)
                elif k == 2 and which:
                    squares(ln_a, i + 1, which)
                elif k == 5 and which:
                    deviation(ln_a, i + 1, which)
                elif k == 9 and there(i - 1):
                    act.wait_ge(ln_a.ready, i + 2)
                    A(z2[:, :], z1[:, :], ACT.Identity, bias=vec("beta"), scale=vec("gamma")).then_inc(z2_ready, 1)
                elif k == 11 and there(i + 1):
                    act.wait_ge(q_mm, i + 2)
                    A(qkvT[:, 0, :], P[:, 6, 0:L], ACT.Identity, bias=vec("bq")).then_inc(q_out, 1)
                    act.wait_ge(k_mm, i + 2)
                    A(qkvT[:, 1, :], P[:, 7, 0:L], ACT.Identity, bias=vec("bk")).then_inc(k_out, 1)
                elif k == 13 and there(i + 1):
                    act.wait_ge(v_mm, i + 2)
                    A(qkvT[:, 2, :], P[:, 6, 0:L], ACT.Identity, bias=vec("bv")).then_inc(v_out, 1)

            def take(b, t, f):
                act.wait_ge(proj_mm, b * 3 + t + 1)
                src = P[0:RT, 7 - t % 2, :]
                kq = src[:, 0:2 * D].rearrange("p (a h d) -> p a h d", a=2, h=H)
                A(relu[:, f, t, :, :, 0:DH], kq, ACT.Relu)
                A(relu[:, f, t, :, :, DH:PHI], kq, ACT.Relu, scale=-1.0)
                A(val[:, f, t, :, :], src[:, 2 * D:3 * D].rearrange("p (h d) -> p h d", h=H), ACT.Copy)
                A(bta[:, f, t, :], src[:, 3 * D:3 * D + H], ACT.Tanh, scale=0.5).then_inc(proj_out, 1)

            def second(k, i, p):
                which = halves(i - 1, i - 3)
                b = i - 3
                if k == 0 and which:
                    squares(ln_b, i - 1, which)
                elif k == 2 and which:
                    deviation(ln_b, i - 1, which)
                elif k == 7 and there(b):
                    if known(b, 2):
                        act.wait_ge(feat_ready, b - 1)
                    take(b, 0, 1 - p)
                elif k == 9:
                    if there(b):
                        take(b, 1, 1 - p)
                    if there(i - 1):
                        act.wait_ge(lg_ready, i)
                        A(ex[:, :, :], lg[:, :, :], ACT.Exp).then_inc(ex_ready, 1)
                elif k == 10 and there(b):
                    take(b, 2, 1 - p)
                elif k == LAST and there(i - 1):
                    act.wait_ge(comb_tr, i)
                    A(combT[:, 1 - p, :], P[0:GATES, 6, 0:L], ACT.Copy).then_inc(combT_ready, 1)

            def context(b, c):
                act.wait_ge(pv_mm, b * 2 + c + 1)
                if known(b, 1):
                    act.wait_ge(ctx_stored, b * 16 * H)
                A(ctxu[:, c, :], P[0:CTX_ROWS, 4, 0:L], ACT.Copy).then_inc(ctx_out, 1)

            def row(b, h):
                act.wait_ge(max_tr, b * H + h + 1)
                A(qs[BLOCKS:ROWS, h, :], P[0:PARTS, 5, 0:L], ACT.Copy).then_inc(max_row, 1)

            def gelu(b, e):
                act.wait_ge(up_mm, b * E1 + e + 1)
                if e >= 2:
                    act.wait_ge(hs_ready, b * E1 + e - 1)
                for k in range(2):
                    A(gl[:, e % 2, k, :], P[:, 2 * (e % 2) + k, 0:L], ACT.Gelu,
                      bias=vec(f"b1_{2 * e + k}")).then_inc(gelu_done, 1)

            class Round:
                eng = act

                def __call__(self, i, p):
                    heads, experts = there(i), there(i - 2)
                    if heads:
                        row(i, 0)
                    for h in range(H):
                        if heads and h == 5:
                            context(i, 0)
                        first(2 * h, i, p)
                        if heads and h + 1 < H:
                            row(i, h + 1)
                        if heads:
                            act.wait_ge(st_mm, i * H + h + 1)
                            A(pT[:, h, :, :].rearrange("p t (a c) -> p a t c", a=2),
                              P[0:RT, 2:4, 0:3 * HALF].rearrange("p a (t c) -> p a t c", t=3),
                              ACT.Exp, scale=DH ** -0.5).then_inc(probs, 1)
                        first(2 * h + 1, i, p)
                    if heads:
                        context(i, 1)
                    if experts:
                        gelu(i - 2, 0)
                    for e in range(E1):
                        if experts and e + 1 < E1:
                            gelu(i - 2, e + 1)
                        for k in (2 * e, 2 * e + 1):
                            second(k, i, p)
                    second(LAST, i, p)

            act.wait_ge(consts_in, 16 * len(loads))
            act.wait_ge(consts_set, NSET)
            for k in range(16):
                first(k, -1, 1)
            schedule(Round())

        @block.vector
        def _(dve):
            V = nc.vector
            mid = Chain(dve, router_step, ROUTER_STEPS)
            mem = Chain(dve, feature_step, FEATURE_STEPS)

            def centre(n, r, sources):
                dve.wait_ge(n.mean_mm, r + 1)
                for half, src in sources:
                    last = V.tensor_tensor(xc[:, half, :], src, P[:, 6 + half, 0:L], ALU.subtract)
                last.then_inc(n.centred, 1)

            def invert(n, r, which):
                dve.wait_ge(n.sd_ready, r + 1)
                f = slice(which[0], which[-1] + 1)
                shape = [RT, len(which), 3, RT]
                V.reciprocal(rstd[:, f, :], sd[:, f, :]).then_inc(n.rstd_ready, 1)
                dve.wait_ge(n.rstd_ready, r + 1)
                V.tensor_tensor(diag[:, f, :, :], ident_s[0:RT, 0:RT].unsqueeze(1).unsqueeze(1).to_broadcast(shape),
                                rstd[:, f, :].unsqueeze(3).to_broadcast(shape), ALU.mult).then_inc(n.diag_ready, 1)

            def scaled(n, r, targets):
                dve.wait_ge(n.bc_mm, r + 1)
                for half, dst in targets:
                    last = V.tensor_tensor(dst, xc[:, half, :], P[:, 6 + half, 0:L], ALU.mult)
                last.then_inc(n.ready, 1)

            def first(k, i, p):
                ends, begins = there(i - 1), there(i + 1)
                if k == 0:
                    if begins:
                        dve.wait_ge(tok_mm, i + 2)
                        if ends:
                            dve.wait_ge(kept_ready, i)
                        V.tensor_tensor(h0[:, 1 - p, 1:LX], P[:, 7, 0:PATCHES], pos_s[:, 1:LX], ALU.add)\
                         .then_inc(h0_ready, 1)
                    if ends:
                        dve.wait_ge(wo_mm, i)
                        V.scalar_tensor_tensor(y1[:, :], P[:, 6, 0:L], vec("bo"), xn1[:, 1 - p, :], ALU.add, ALU.add)\
                         .then_inc(y1_ready, 1)
                elif k == 2 and (ends or begins):
                    if begins:
                        dve.wait_ge(h0_ready, i + 2)
                        dve.wait_ge(text_ready, i + 2)
                    if ends:
                        dve.wait_ge(y1_ready, i)
                    centre(ln_a, i + 1, begins * [(1, h0[:, 1 - p, :])] + ends * [(0, y1[:, :])])
                elif k == 8 and (ends or begins):
                    invert(ln_a, i + 1, halves(i - 1, i + 1))
                elif k == 9 and (ends or begins):
                    scaled(ln_a, i + 1, begins * [(1, xn1[:, 1 - p, :])] + ends * [(0, z1[:, :])])
                elif k == 10 and ends:
                    dve.wait_ge(z2_ready, i)
                    dve.wait_ge(kept_ready, i)
                    if known(i, 3):
                        dve.wait_ge(h2_ready, i - 2)
                    V.tensor_tensor(h1[:, 1 - p, :], kept[:, :], z2[:, :], ALU.add).then_inc(h1_ready, 1)

            def invert_sums(b, c):
                dve.wait_ge(den_in, (b + 1) * 16)
                part = den[:, c * HALF:(c + 1) * HALF]
                V.reciprocal(part, part).then_inc(den_ready, 1)

            def divide(b):
                dve.wait_ge(den_ready, (b + 1) * 2)
                dve.wait_ge(cfm_in, (b + 1) * 16)
                V.tensor_tensor(cfm[:, :], cfm[:, :], den[:, :], ALU.mult).then_inc(cfm_ready, 1)

            def second(k, i, p):
                routes, b = there(i - 1), i - 3
                if k == 0 and (routes or there(b)):
                    if routes:
                        dve.wait_ge(h1_ready, i)
                    if there(b):
                        dve.wait_ge(h2_ready, b + 1)
                    centre(ln_b, i - 1, routes * [(0, h1[:, 1 - p, :])] + there(b) * [(1, h2[:, :])])
                elif k == 3 and (routes or there(b)):
                    invert(ln_b, i - 1, halves(i - 1, b))
                elif k == 5 and (routes or there(b)):
                    scaled(ln_b, i - 1, routes * [(0, x2[:, 1 - p, :])] + there(b) * [(1, x3[:, :])])
                elif k == 7 and routes:
                    mid.start(i - 1)
                    dve.wait_ge(router_mm, i)
                    mid.link(V.tensor_tensor(lg[:, :, :], P[0:RT, 6, 0:3 * E1].rearrange("p (t e) -> p t e", t=3),
                                             br_s[0:RT, :].unsqueeze(1).to_broadcast([RT, 3, E1]), ALU.add))
                    mid.link(V.tensor_reduce(r8[:, :], lg[:, :, :], AX.X, ALU.max))
                    V.tensor_tensor(lg[:, :, :], lg[:, :, :], r8[:, :].unsqueeze(2).to_broadcast([RT, 3, E1]),
                                    ALU.subtract).then_inc(lg_ready, 1)
                elif k == 11 and routes:
                    dve.wait_ge(ex_ready, i)
                    mid.link(V.tensor_reduce(r8[:, :], ex[:, :, :], AX.X, ALU.add))
                    mid.link(V.reciprocal(r8[:, :], r8[:, :]))
                    mid.link(V.tensor_tensor(ex[:, :, :], ex[:, :, :], r8[:, :].unsqueeze(2).to_broadcast([RT, 3, E1]),
                                             ALU.mult))
                    mine = ex[:, :, :].unsqueeze(3).to_broadcast([RT, 3, E1, E1])
                    other = ex[:, :, :].unsqueeze(2).to_broadcast([RT, 3, E1, E1])
                    mid.link(V.tensor_tensor(cmp1[:, :, :, :], other, mine, ALU.is_gt))
                elif k == 12 and routes:
                    mine = ex[:, :, :].unsqueeze(3).to_broadcast([RT, 3, E1, E1])
                    other = ex[:, :, :].unsqueeze(2).to_broadcast([RT, 3, E1, E1])
                    mid.link(V.tensor_tensor(cmp2[:, :, :, :], other, mine, ALU.is_equal))
                    mid.link(V.tensor_tensor(cmp2[:, :, :, :], cmp2[:, :, :, :],
                                             tri_s[0:RT, :, :].unsqueeze(1).to_broadcast([RT, 3, E1, E1]), ALU.mult))
                    mid.link(V.tensor_tensor(cmp1[:, :, :, :], cmp1[:, :, :, :], cmp2[:, :, :, :], ALU.add))
                    mid.link(V.tensor_reduce(rank[:, :, :], cmp1[:, :, :, :], AX.X, ALU.add))
                    V.scalar_tensor_tensor(comb[:, :, :], rank[:, :, :], 2.0, ex[:, :, :], ALU.is_lt, ALU.mult)\
                     .then_inc(comb_ready, 1)
                    mid.end()

            def sums(k, b, f):
                if k in (1, 3):
                    q = slice(k // 2 * H, (k // 2 + 1) * H)
                    if k == 1:
                        mem.start(b)
                        dve.wait_ge(prod_step, (b + 1) * PROD_STEPS)
                    mem.link(V.tensor_reduce(fsum[:, :, q], prod[:, :, q, :], AX.X, ALU.add))
                elif k == 6:
                    mem.link(V.tensor_scalar(fsum[:, :, :], fsum[:, :, :], 1e-6, None, ALU.add))
                    mem.link(V.reciprocal(fsum[:, :, :], fsum[:, :, :]))
                    mem.end()
                    V.tensor_scalar(bta[:, f, :, :], bta[:, f, :, :], 0.5, 0.5, ALU.mult, ALU.add)\
                     .then_inc(sums_ready, 1)

            def maximum(b, h):
                dve.wait_ge(s_mm, b * H + h + 1)
                if h >= 2:
                    dve.wait_ge(max_step, (b * H + h - 1) * MAX_STEPS)
                V.tensor_reduce(nmx[:, h % 2, :], P[0:RT, 0:2, 0:3 * HALF].rearrange("p a (t c) -> p t a c", t=3),
                                AX.XY, ALU.max, negate=True).then_inc(max_ready, 1)

            class Round:
                eng = dve

                def __call__(self, i, p):
                    heads, experts = there(i), there(i - 2)
                    if heads:
                        dve.wait_ge(v_tr, i + 1)
                        V.tensor_copy(vaug[:, :, :, :], P[0:RT, 5, 0:H * 3 * (DH + 1)].rearrange(
                            "p (h t d) -> p h t d", h=H, t=3)).then_inc(vaug_ready, 1)
                        maximum(i, 1)
                    for h in range(H):
                        if heads and h + 2 < H:
                            maximum(i, h + 2)
                        for k in (2 * h, 2 * h + 1):
                            first(k, i, p)
                    for e in range(E1):
                        if experts:
                            dve.wait_ge(gelu_done, (i - 2) * 2 * E1 + 2 * e + 2)
                            dve.wait_ge(bc_mm, (i - 2) * E1 + e + 1)
                            if e >= 2:
                                dve.wait_ge(down_mm, (i - 2) * E1 + e - 1)
                            V.tensor_tensor(hs[:, e % 2, :, :], gl[:, e % 2, :, :],
                                            P[:, 4, 0:L].unsqueeze(1).to_broadcast([128, 2, L]), ALU.mult)\
                             .then_inc(hs_ready, 1)
                        if e == E1 - 1 and there(i + 1):
                            maximum(i + 1, 0)
                        for k in (2 * e, 2 * e + 1):
                            if there(i - 4):
                                sums(k, i - 4, p)
                            second(k, i, p)
                            if k == 2 * E1 - 1 and heads:
                                invert_sums(i, 0)
                    if experts:
                        dve.wait_ge(down_mm, (i - 1) * E1)
                        if known(i, 3):
                            dve.wait_ge(h2_stored, (i - 2) * 16)
                        V.tensor_tensor(h2[:, :], h1[:, p, :], P[:, 5, 0:L], ALU.add).then_inc(h2_ready, 1)
                    if heads:
                        invert_sums(i, 1)
                        divide(i)

            V.memset(mean_w[:, :], 1.0 / D).then_inc(consts_set, 1)
            V.memset(ones_s[:, :], 1.0).then_inc(consts_set, 1)
            V.memset(eps_s[:, :], 1e-5).then_inc(consts_set, 1)
            V.memset(ks[BLOCKS:ROWS, :, :], 1.0).then_inc(consts_set, 1)
            V.memset(vd[0:1, :, :], 1.0).then_inc(consts_set, 1)
            V.memset(P[:, :, :], 0.0).then_inc(consts_set, 1)
            dve.wait_ge(consts_in, 16 * len(loads))
            dve.wait_ge(consts_set, 6)
            V.tensor_copy(erow_h[:, :, :], erow_s[:, :, :])
            b2_chain = Chain(dve, b2_step, PARTS)
            b2_chain.link(V.tensor_copy(b2_h[:, 0, :], b2_s[:, :]))
            b2_chain.link(V.tensor_tensor(b2_left[:, :], b2_s[:, :], b2_h[:, 0, :], ALU.subtract))
            b2_chain.link(V.tensor_copy(b2_h[:, 1, :], b2_left[:, :]))
            b2_chain.end()
            V.tensor_tensor(b2_h[:, 2, :], b2_left[:, :], b2_h[:, 1, :], ALU.subtract)
            V.tensor_copy(ident_h[:, :], ident_s[:, :]).then_inc(consts_set, 1)
            V.tensor_scalar(pos_s[:, 1:LX], pos_s[:, 1:LX], vec("tok_b"), None, ALU.add).then_inc(pos_ready, 1)
            V.tensor_scalar(h0[:, :, 0:1], pos_s[:, 0:1].unsqueeze(1).to_broadcast([128, 2, 1]), vec("cls"), None,
                            ALU.add).then_inc(consts_set, 1)
            dve.wait_ge(pos_ready, 1)
            dve.wait_ge(consts_set, NSET)
            for k in range(16):
                first(k, -1, 1)
            maximum(0, 0)
            schedule(Round())


def memory(nc, feat_d, ident, eye_blocks, read_mask, read_d):
    f32 = mybir.dt.float32
    ALU = mybir.AluOpType
    ACT = mybir.ActivationFunctionType
    NSUB = -(-L // SUB)
    LAST = (L - SUB) // 2

    ctx = ExitStack()
    with ctx:
        def sb(name, shape, dt=f32):
            return ctx.enter_context(nc.sbuf_tensor(name, shape, dt))

        def sem(name):
            return ctx.enter_context(nc.semaphore(name))

        ident2 = sb("ident2", [128, 128])
        eye_s = sb("eye_s", [128, SUB, 4, SUB])
        mask_s = sb("mask_s", [128, B])
        kin = sb("kin", [128, 2, 4, 3 * FK])
        vin = sb("vin", [128, PAIRS, D])
        kqt = sb("kqt", [128, 2, 6, 128])
        gram = sb("gram", [128, PAIRS, 4, 2, 2 * B])
        low = sb("low", [128, SUB, 4, SUB])
        inv = sb("inv", [128, SUB, 4, SUB])
        tmp = sb("tmp", [128, SUB, 4, SUB])
        invT = sb("invT", [128, 128, SUB])
        u1 = sb("u1", [128, 2, 4, D])
        r2 = sb("r2", [128, 2, 4, D])
        u2 = sb("u2", [128, 2, 4 * H, 2, DH])
        osb = sb("osb", [128, QUADS, 2 * 2 * D])
        P = ctx.enter_context(nc.psum_tensor("P2", [128, 8, 512], f32))

        consts2_in = sem("consts2_in")
        psum_set = sem("psum_set")
        k_loaded = [sem(f"k_loaded{c}") for c in range(2)]
        v_loaded = sem("v_loaded")
        kq_tr = sem("kq_tr")
        kqt_ready = sem("kqt_ready")
        gram_mm = sem("gram_mm")
        gram_out = sem("gram_out")
        gram_masked = sem("gram_masked")
        low_tr = sem("low_tr")
        low_even = sem("low_even")
        low_odd = sem("low_odd")
        inv_set = sem("inv_set")
        solve_step = sem("solve_step")
        inv_ready = sem("inv_ready")
        inv_tr = sem("inv_tr")
        invT_even = sem("invT_even")
        invT_odd = sem("invT_odd")
        u1_mm = sem("u1_mm")
        u1_ready = sem("u1_ready")
        r2_mm = sem("r2_mm")
        r2_ready = sem("r2_ready")
        u2_mm = sem("u2_mm")
        u2_ready = sem("u2_ready")
        o_mm = sem("o_mm")
        o_ready = sem("o_ready")
        read_stored = sem("read_stored")

        block = ctx.enter_context(nc.Block())
        feat_v = feat_d.rearrange("b (l k) f -> k b l f", k=2)
        read_v = read_d.rearrange("b (m u x) f -> u b m (x f)", u=2, x=4)
        NT = SUB // 4

        @block.sync
        def _(sp):
            def at(b):
                return b if isinstance(b, int) else sp.snap(b)

            def sub(n, p0, m0):
                quads = [at(p0 + 4 * c) for c in range(QUADS)]
                first_quad = at(m0)
                for c in range(QUADS):
                    if c >= 2 or known(n, 1):
                        sp.wait_ge(kqt_ready, n * PAIRS + 4 * (c - 1))
                    for k in range(2):
                        sp.dma_start(kin[B * k:B * k + B, c % 2, :, :],
                                     feat_v[k][:, bass.ds(quads[c], 4), 0:3 * FK]).then_inc(k_loaded[c % 2], 16)
                if known(n, 1):
                    sp.wait_ge(r2_ready, n * QUADS)
                for k in range(2):
                    sp.dma_start(vin[B * k:B * k + B, :, :],
                                 feat_v[k][:, bass.ds(quads[0], PAIRS), 3 * FK:FW]).then_inc(v_loaded, 16)
                sp.wait_ge(o_ready, (n + 1) * QUADS)
                for u in range(2):
                    sp.dma_start(read_v[u][:, bass.ds(first_quad, QUADS), :], osb[B * u:B * u + B, :, :])\
                      .then_inc(read_stored, 16)

            sp.dma_start(ident2[:, :], ident).then_inc(consts2_in, 16)
            sp.dma_start(eye_s[:, :, :, :], eye_blocks).then_inc(consts2_in, 16)
            sp.dma_start(mask_s[:, :], read_mask).then_inc(consts2_in, 16)
            sub(0, 0, 0)
            with sp.Fori(1, NSUB - 1) as n:
                sub(n, n * PAIRS, n * QUADS)
            sub(NSUB - 1, LAST, LAST // 4)
            sp.wait_ge(read_stored, NSUB * 32)

        @block.tensor
        def _(pe):
            mm = nc.tensor.matmul

            def stream(c, q):
                pair, h = 4 * c + q // H, q % H
                return pair, h % 4, h // 4, h

            def sub(n):
                def turn(p):
                    if p >= 2:
                        pe.wait_ge(kqt_ready, n * PAIRS + p - 1)
                    if p % 4 == 0:
                        pe.wait_ge(k_loaded[p // 4 % 2], n * 64 + (p // 8 + 1) * 32)
                    for j in range(6):
                        last = nc.tensor.transpose(P[:, 4 + 2 * (p % 2) + j // 4, (j % 4) * 128:(j % 4 + 1) * 128],
                                                   kin[:, p // 4 % 2, p % 4, j * 128:(j + 1) * 128], ident2[:, :])
                    last.then_inc(kq_tr, 1)

                def products(p):
                    pe.wait_ge(kqt_ready, n * PAIRS + p + 1)
                    if p:
                        pe.wait_ge(gram_out, n * PAIRS + p)
                    for hd in range(2):
                        for k in range(2):
                            for g in range(4):
                                f = slice(PHI * g, PHI * (g + 1))
                                last = mm(P[B * k:B * k + B, g, hd * 2 * B:(hd + 1) * 2 * B],
                                          kqt[f, p % 2, hd, B * k:B * k + B],
                                          kqt[f, p % 2, 2 + hd:6:2, B * k:B * k + B],
                                          start=True, stop=True, tile_position=(PHI * g, B * k))
                    last.then_inc(gram_mm, 1)

                if known(n, 1):
                    pe.wait_ge(o_ready, n * QUADS)
                turn(0)
                for p in range(PAIRS):
                    if p + 1 < PAIRS:
                        turn(p + 1)
                    products(p)
                pe.wait_ge(gram_out, (n + 1) * PAIRS)
                for i in range(2 * NT):
                    blk, bank = i % 2, 4 + i % 4
                    if i >= 4:
                        pe.wait_ge(low_even if i % 2 == 0 else low_odd, n * NT + (i - 4) // 2 + 1)
                    for j in range(4):
                        t = blk * SUB + 4 * (i // 2) + j
                        last = nc.tensor.transpose(P[:, bank, j * 128:(j + 1) * 128],
                                                   gram[:, :, :, :, t].rearrange("p a g h -> p (a g h)"), ident2[:, :])
                    last.then_inc(low_tr, 1)
                pe.wait_ge(inv_ready, n + 1)
                for i in range(NT):
                    if i >= 4:
                        pe.wait_ge(invT_even if i % 2 == 0 else invT_odd, n * NT // 2 + (i - 4) // 2 + 1)
                    for j in range(4):
                        last = nc.tensor.transpose(P[:, 4 + i % 4, j * 128:(j + 1) * 128],
                                                   inv[:, 4 * i + j, :, :].rearrange("p q s -> p (q s)"), ident2[:, :])
                    last.then_inc(inv_tr, 1)
                pe.wait_ge(v_loaded, (n + 1) * 32)
                pe.wait_ge(invT_even, (n + 1) * NT // 2)
                pe.wait_ge(invT_odd, (n + 1) * NT // 2)
                pe.wait_ge(gram_masked, (n + 1) * PAIRS)

                def carry():
                    mm(P[0:2 * SUB, 7, 0:1], ident2[0:SUB, 0:2 * SUB], ident2[0:SUB, 0:1], start=True, stop=True)

                def first(c):
                    if c >= 2:
                        pe.wait_ge(u2_ready, n * QUADS + c - 1)
                    carry()
                    for q in range(4 * H):
                        pair, g, hd, h = stream(c, q)
                        for k in range(2):
                            f = slice(B * k, B * k + SUB)
                            last = mm(P[f, c % 2, q * DH:(q + 1) * DH], invT[f, pair * H + 2 * g + hd, :],
                                      vin[f, pair, h * DH:(h + 1) * DH], start=True, stop=True)
                    last.then_inc(u1_mm, 1)

                def across(c):
                    pe.wait_ge(u1_ready, n * QUADS + c + 1)
                    if c >= 2:
                        pe.wait_ge(r2_ready, n * QUADS + c - 1)
                    carry()
                    for q in range(4 * H):
                        pair, g, hd, h = stream(c, q)
                        for k in range(2):
                            f = slice(B * k, B * k + SUB)
                            last = mm(P[B * k + SUB:B * (k + 1), 2 + c % 2, q * DH:(q + 1) * DH],
                                      gram[f, pair, g, hd, SUB:B], u1[f, c % 2, q // H, h * DH:(h + 1) * DH],
                                      start=True, stop=True)
                    last.then_inc(r2_mm, 1)

                def second(c):
                    pe.wait_ge(r2_ready, n * QUADS + c + 1)
                    carry()
                    for q in range(4 * H):
                        pair, g, hd, h = stream(c, q)
                        for k in range(2):
                            f = slice(B * k + SUB, B * (k + 1))
                            last = mm(P[f, c % 2, q * DH:(q + 1) * DH], invT[f, pair * H + 2 * g + hd, :],
                                      r2[f, c % 2, q // H, h * DH:(h + 1) * DH], start=True, stop=True)
                    last.then_inc(u2_mm, 1)

                def read(c):
                    pe.wait_ge(u2_ready, n * QUADS + c + 1)
                    if c >= 2:
                        pe.wait_ge(o_ready, n * QUADS + c - 1)
                    carry()
                    for x in range(2 * H):
                        for u in range(2):
                            q = 2 * H * u + x
                            pair, g, hd, h = stream(c, q)
                            last = mm(P[B * u:B * (u + 1), 4 + c % 2, x * 2 * DH:(x + 1) * 2 * DH],
                                      gram[:, pair, g, hd, B:2 * B],
                                      u2[:, c % 2, q, :, :].rearrange("p k d -> p (k d)"),
                                      start=True, stop=True, tile_position=(0, B * u))
                    last.then_inc(o_mm, 1)

                for c in range(0, QUADS, 2):
                    first(c)
                    first(c + 1)
                    across(c)
                    across(c + 1)
                    second(c)
                    second(c + 1)
                    read(c)
                    read(c + 1)

            pe.wait_ge(consts2_in, 48)
            pe.wait_ge(psum_set, 2)
            sub(0)
            with pe.Fori(1, NSUB - 1) as n:
                sub(n)
            sub(NSUB - 1)

        @block.scalar
        def _(act):
            A = nc.scalar.activation

            def sub(n):
                def turned(p):
                    act.wait_ge(kq_tr, n * PAIRS + p + 1)
                    if p >= 2:
                        act.wait_ge(gram_mm, n * PAIRS + p - 1)
                    b = 4 + 2 * (p % 2)
                    A(kqt[:, p % 2, 0:4, :].rearrange("p j n -> p (j n)"), P[:, b, :], ACT.Copy)
                    A(kqt[:, p % 2, 4:6, :].rearrange("p j n -> p (j n)"), P[:, b + 1, 0:256], ACT.Copy)\
                     .then_inc(kqt_ready, 1)

                turned(0)
                for p in range(PAIRS):
                    if p + 1 < PAIRS:
                        turned(p + 1)
                    act.wait_ge(gram_mm, n * PAIRS + p + 1)
                    A(gram[:, p, :, :, :], P[:, 0:4, 0:4 * B].rearrange("p g (h n) -> p g h n", h=2), ACT.Copy)\
                     .then_inc(gram_out, 1)
                for i in range(0, 2 * NT, 2):
                    act.wait_ge(low_tr, n * 2 * NT + i + 1)
                    A(low[:, 4 * (i // 2):4 * (i // 2) + 4, 0:3:2, :],
                      P[:, 4 + i % 4, :].rearrange("p (t k s) -> p t k s", t=4, k=2)[:, :, :, 0:SUB],
                      ACT.Copy, scale=-1.0).then_inc(low_even, 1)
                for i in range(0, NT, 2):
                    act.wait_ge(inv_tr, n * NT + i + 1)
                    A(invT[:, :, 4 * i:4 * i + 4].rearrange("p q t -> p t q"),
                      P[:, 4 + i % 4, :].rearrange("p (t q) -> p t q", t=4), ACT.Copy).then_inc(invT_even, 1)

                def take_u1(c):
                    act.wait_ge(u1_mm, n * QUADS + c + 1)
                    A(u1[:, c % 2, :, :].rearrange("p a n -> p (a n)"), P[:, c % 2, :], ACT.Copy).then_inc(u1_ready, 1)

                def take_u2(c):
                    act.wait_ge(u2_mm, n * QUADS + c + 1)
                    A(u2[0:B, c % 2, :, 0, :], P[0:B, c % 2, :].rearrange("p (q d) -> p q d", d=DH), ACT.Copy)
                    A(u2[B:2 * B, c % 2, :, 1, :], P[B:2 * B, c % 2, :].rearrange("p (q d) -> p q d", d=DH), ACT.Copy)\
                     .then_inc(u2_ready, 1)

                for c in range(0, QUADS, 2):
                    take_u1(c)
                    take_u1(c + 1)
                    take_u2(c)
                    take_u2(c + 1)

            act.wait_ge(psum_set, 2)
            sub(0)
            with act.Fori(1, NSUB - 1) as n:
                sub(n)
            sub(NSUB - 1)

        @block.vector
        def _(dve):
            V = nc.vector
            chain = Chain(dve, solve_step, SOLVE_STEPS)

            def sub(n):
                chain.start(n)
                if known(n, 1):
                    dve.wait_ge(inv_tr, n * NT)
                V.tensor_copy(inv[:, :, :, :], eye_s[:, :, :, :]).then_inc(inv_set, 1)
                for p in range(PAIRS):
                    dve.wait_ge(gram_out, n * PAIRS + p + 1)
                    V.tensor_tensor(gram[:, p, :, :, B:2 * B], gram[:, p, :, :, B:2 * B],
                                    mask_s[:, :].unsqueeze(1).unsqueeze(1).to_broadcast([128, 4, 2, B]), ALU.mult)\
                     .then_inc(gram_masked, 1)
                for i in range(1, 2 * NT, 2):
                    dve.wait_ge(low_tr, n * 2 * NT + i + 1)
                    V.tensor_scalar(low[:, 4 * (i // 2):4 * (i // 2) + 4, 1:4:2, :],
                                    P[:, 4 + i % 4, :].rearrange("p (t k s) -> p t k s", t=4, k=2)[:, :, :, SUB:B],
                                    -1.0, None, ALU.mult).then_inc(low_odd, 1)
                dve.wait_ge(inv_set, n + 1)
                dve.wait_ge(low_even, (n + 1) * NT)
                dve.wait_ge(low_odd, (n + 1) * NT)
                for s in range(SUB - 1):
                    shape = [128, SUB - 1 - s, 4, s + 1]
                    below = slice(s + 1, SUB)
                    chain.link(V.tensor_tensor(tmp[:, below, :, 0:s + 1], low[:, below, :, s:s + 1].to_broadcast(shape),
                                               inv[:, s:s + 1, :, 0:s + 1].to_broadcast(shape), ALU.mult))
                    ins = V.tensor_tensor(inv[:, below, :, 0:s + 1], inv[:, below, :, 0:s + 1],
                                          tmp[:, below, :, 0:s + 1], ALU.add)
                    chain.link(ins)
                chain.end()
                V.tensor_copy(inv[:, 0:1, 0:1, 0:1], eye_s[:, 0:1, 0:1, 0:1]).then_inc(inv_ready, 1)
                for i in range(1, NT, 2):
                    dve.wait_ge(inv_tr, n * NT + i + 1)
                    V.tensor_copy(invT[:, :, 4 * i:4 * i + 4].rearrange("p q t -> p t q"),
                                  P[:, 4 + i % 4, :].rearrange("p (t q) -> p t q", t=4)).then_inc(invT_odd, 1)

                def rest(c):
                    dve.wait_ge(r2_mm, n * QUADS + c + 1)
                    V.tensor_tensor(r2[:, c % 2, :, :], vin[:, 4 * c:4 * c + 4, :],
                                    P[:, 2 + c % 2, :].rearrange("p (a n) -> p a n", a=4), ALU.subtract)\
                     .then_inc(r2_ready, 1)

                def take_o(c):
                    dve.wait_ge(o_mm, n * QUADS + c + 1)
                    if c == 0 and known(n, 1):
                        dve.wait_ge(read_stored, n * 32)
                    for a in range(2):
                        last = V.tensor_copy(
                            osb[:, c, 2 * a * D:2 * (a + 1) * D].rearrange("p (k h d) -> p k h d", k=2, h=H),
                            P[:, 4 + c % 2, 2 * a * D:2 * (a + 1) * D].rearrange("p (h k d) -> p k h d", k=2, h=H))
                    last.then_inc(o_ready, 1)

                for c in range(0, QUADS, 2):
                    rest(c)
                    rest(c + 1)
                    take_o(c)
                    take_o(c + 1)

            V.memset(P[:, :, :], 0.0).then_inc(psum_set, 1)
            V.memset(u2[:, :, :, :, :], 0.0).then_inc(psum_set, 1)
            dve.wait_ge(consts2_in, 48)
            sub(0)
            with dve.Fori(1, NSUB - 1) as n:
                sub(n)
            sub(NSUB - 1)


def experts_out(nc, read_d, h2_d, vecs, wo1, wg, bg, we, be, ident, expert_numbers, out):
    f32 = mybir.dt.float32
    u32 = mybir.dt.uint32
    ALU = mybir.AluOpType
    ACT = mybir.ActivationFunctionType
    AX = mybir.AxisListType
    R = B // GRP

    ctx = ExitStack()
    with ctx:
        def sb(name, shape, dt=f32):
            return ctx.enter_context(nc.sbuf_tensor(name, shape, dt))

        def sem(name):
            return ctx.enter_context(nc.semaphore(name))

        vec3 = sb("vec3", [128, NV])
        wo1_s = sb("wo1_s", [128, D])
        wg_s = sb("wg_s", [128, E2])
        bg_s = sb("bg_s", [1, E2])
        enum_s = sb("enum_s", [1, E2])
        we_s = sb("we_s", [128, E2 * D])
        be_s = sb("be_s", [128, E2])
        ident3 = sb("ident3", [128, 128])
        mean3 = sb("mean3", [128, 128])
        ones3 = sb("ones3", [128, 128])
        eps3 = sb("eps3", [128, 1])
        rd = sb("rd", [RT, GRP, 3, D])
        h2 = sb("h2b", [128, GRP, L])
        rf = sb("rf", [128, GRP, L])
        h3 = sb("h3", [128, GRP, L])
        xc = sb("xc3", [128, GRP, L])
        sq = sb("sq3", [128, GRP, L])
        sd = sb("sd3", [RT, GRP, 3])
        rstd = sb("rstd3", [RT, GRP, 3])
        diag = sb("diag3", [RT, GRP, 3, RT])
        x4 = sb("x4", [128, GRP, L])
        msum = sb("msum", [128, GRP])
        sc = sb("sc", [1, GRP, E2])
        top = sb("top", [1, GRP])
        tot = sb("tot", [1, GRP])
        gate = sb("gate", [1, GRP])
        worse = sb("worse", [1, GRP, E2])
        bestf = sb("bestf", [1, GRP])
        best = sb("best", [1, GRP], u32)
        gcol = sb("gcol", [128, GRP])
        wsel = sb("wsel", [128, GRP, D])
        bsel = sb("bsel", [128, GRP])
        fin = sb("fin", [128, GRP, L])
        P = ctx.enter_context(nc.psum_tensor("P3", [128, 8, 512], f32))

        consts3_in = sem("consts3_in")
        consts3_set = sem("consts3_set")
        read_in = sem("read_in")
        h2_in = sem("h2_in")
        read_tr = sem("read_tr")
        rf_ready = sem("rf_ready")
        wo1_mm = sem("wo1_mm")
        h3_ready = sem("h3_ready")
        mean_mm = sem("mean_mm")
        centred = sem("centred")
        squared = sem("squared")
        var_mm = sem("var_mm")
        sd_ready = sem("sd_ready")
        rstd_ready = sem("rstd_ready")
        diag_ready = sem("diag_ready")
        spread_mm = sem("spread_mm")
        x4_ready = sem("x4_ready")
        msum_ready = sem("msum_ready")
        score_mm = sem("score_mm")
        sc_ready = sem("sc_ready")
        sc_exp = sem("sc_exp")
        gate_step = sem("gate_step")
        gate_ready = sem("gate_ready")
        gate_mm = sem("gate_mm")
        gcol_ready = sem("gcol_ready")
        wsel_ready = sem("wsel_ready")
        bsel_ready = sem("bsel_ready")
        y_mm = sem("y_mm")
        fin_ready = sem("fin_ready")
        out_stored = sem("out_stored")

        loads = [(vec3, vecs), (wo1_s, wo1), (wg_s, wg), (bg_s, bg), (enum_s, expert_numbers), (we_s, we), (be_s, be),
                 (ident3, ident)]
        block = ctx.enter_context(nc.Block())

        @block.sync
        def _(sp):
            def at(b):
                return b if isinstance(b, int) else sp.snap(b)

            def load(firsts):
                for u in range(GRP):
                    for t, s in TILES:
                        sp.dma_start(rd[:, u, t, :], read_d[bass.ds(firsts[u], 1), s:s + RT, :]
                                     .rearrange("o p n -> (o p) n")).then_inc(read_in, 16)

            def load_h2(first):
                sp.dma_start(h2[:, :, :], h2_d[bass.ds(first, GRP)].rearrange("o p n -> p o n")).then_inc(h2_in, 16)

            def store(r, first):
                sp.wait_ge(fin_ready, (r + 1) * GRP)
                sp.dma_start(out[bass.ds(first, GRP)].rearrange("o p n -> p o n"), fin[:, :, :])\
                  .then_inc(out_stored, 16)

            for dst, src in loads:
                sp.dma_start(dst[:], src).then_inc(consts3_in, 16)
            load(range(GRP))
            load_h2(0)
            with sp.Fori(1, R) as r:
                images_ = [at(r * GRP + u) for u in range(GRP)]
                stored = at(r * GRP - GRP)
                sp.wait_ge(read_tr, r * GRP)
                load(images_)
                sp.wait_ge(h3_ready, r * GRP)
                load_h2(images_[0])
                store(r - 1, stored)
            store(R - 1, B - GRP)
            sp.wait_ge(out_stored, R * 16)

        @block.tensor
        def _(pe):
            mm = nc.tensor.matmul

            def group(r):
                pe.wait_ge(read_in, (r + 1) * 16 * 3 * GRP)
                for u in range(GRP):
                    if known(r, 1):
                        pe.wait_ge(fin_ready, r * GRP)
                    for t, s in TILES:
                        last = nc.tensor.transpose(P[:, 2 * u, s:s + RT], rd[:, u, t, :], ident3[0:RT, 0:RT])
                    last.then_inc(read_tr, 1)
                for u in range(GRP):
                    pe.wait_ge(rf_ready, r * GRP + u + 1)
                    mm(P[:, 2 * u, 0:L], wo1_s[:, :], rf[:, u, :], start=True, stop=True).then_inc(wo1_mm, 1)
                for u in range(GRP):
                    pe.wait_ge(h3_ready, r * GRP + u + 1)
                    mm(P[:, 2 * u, 0:L], mean3[:, :], h3[:, u, :], start=True, stop=True).then_inc(mean_mm, 1)
                for u in range(GRP):
                    pe.wait_ge(squared, r * GRP + u + 1)
                    for t, s in TILES:
                        last = mm(P[0:RT, 2 * u + 1, t:t + 1], sq[:, u, s:s + RT], mean3[:, 0:1], start=True, stop=True)
                    last.then_inc(var_mm, 1)
                for u in range(GRP):
                    pe.wait_ge(diag_ready, r * GRP + u + 1)
                    for t, s in TILES:
                        last = mm(P[:, 2 * u + 1, s:s + RT], ones3[0:RT, :], diag[:, u, t, :], start=True, stop=True)
                    last.then_inc(spread_mm, 1)
                pe.wait_ge(msum_ready, (r + 1) * GRP)
                for u in range(GRP):
                    last = mm(P[0:1, 1, u * E2:(u + 1) * E2], msum[:, u:u + 1], wg_s[:, :], start=True, stop=True)
                last.then_inc(score_mm, 1)
                pe.wait_ge(gate_ready, r + 1)
                mm(P[:, 3, 0:GRP], ones3[0:1, :], gate[:, :], start=True, stop=True).then_inc(gate_mm, 1)
                for u in range(GRP):
                    pe.wait_ge(wsel_ready, r * GRP + u + 1)
                    mm(P[:, 2 * u, 0:L], wsel[:, u, :], x4[:, u, :], start=True, stop=True).then_inc(y_mm, 1)

            pe.wait_ge(consts3_in, 16 * len(loads))
            pe.wait_ge(consts3_set, 3)
            group(0)
            with pe.Fori(1, R) as r:
                group(r)

        @block.scalar
        def _(act):
            A = nc.scalar.activation

            def group(r):
                for u in range(GRP):
                    act.wait_ge(read_tr, r * GRP + u + 1)
                    A(rf[:, u, :], P[:, 2 * u, 0:L], ACT.Copy).then_inc(rf_ready, 1)
                for u in range(GRP):
                    act.wait_ge(centred, r * GRP + u + 1)
                    A(sq[:, u, :], xc[:, u, :], ACT.Square).then_inc(squared, 1)
                for u in range(GRP):
                    act.wait_ge(var_mm, r * GRP + u + 1)
                    A(sd[:, u, :], P[0:RT, 2 * u + 1, 0:3], ACT.Sqrt, bias=eps3[0:RT, :]).then_inc(sd_ready, 1)
                act.wait_ge(sc_ready, r + 1)
                A(sc[:, :, :], sc[:, :, :], ACT.Exp).then_inc(sc_exp, 1)
                act.wait_ge(gate_mm, r + 1)
                A(gcol[:, :], P[:, 3, 0:GRP], ACT.Copy).then_inc(gcol_ready, 1)
                for u in range(GRP):
                    e = act.value_load(best[0:1, u:u + 1], min_val=0, max_val=E2 - 1)
                    act.wait_ge(gcol_ready, r + 1)
                    A(wsel[:, u, :], we_s[:, bass.ds(e * D, D)], ACT.Copy, scale=gcol[:, u:u + 1]).then_inc(wsel_ready, 1)
                    A(bsel[:, u:u + 1], be_s[:, bass.ds(e, 1)], ACT.Copy, scale=gcol[:, u:u + 1]).then_inc(bsel_ready, 1)

            act.wait_ge(consts3_in, 16 * len(loads))
            act.wait_ge(consts3_set, 3)
            group(0)
            with act.Fori(1, R) as r:
                group(r)

        @block.vector
        def _(dve):
            V = nc.vector
            chain = Chain(dve, gate_step, GATE_STEPS)

            def group(r):
                chain.start(r)
                dve.wait_ge(h2_in, (r + 1) * 16)
                for u in range(GRP):
                    dve.wait_ge(wo1_mm, r * GRP + u + 1)
                    V.scalar_tensor_tensor(h3[:, u, :], P[:, 2 * u, 0:L], vec3[:, 8:9], h2[:, u, :], ALU.add, ALU.add)\
                     .then_inc(h3_ready, 1)
                for u in range(GRP):
                    dve.wait_ge(mean_mm, r * GRP + u + 1)
                    dve.wait_ge(h3_ready, r * GRP + u + 1)
                    V.tensor_tensor(xc[:, u, :], h3[:, u, :], P[:, 2 * u, 0:L], ALU.subtract).then_inc(centred, 1)
                for u in range(GRP):
                    dve.wait_ge(sd_ready, r * GRP + u + 1)
                    V.reciprocal(rstd[:, u, :], sd[:, u, :]).then_inc(rstd_ready, 1)
                    dve.wait_ge(rstd_ready, r * GRP + u + 1)
                    V.tensor_tensor(diag[:, u, :, :], ident3[0:RT, 0:RT].unsqueeze(1).to_broadcast([RT, 3, RT]),
                                    rstd[:, u, :].unsqueeze(2).to_broadcast([RT, 3, RT]), ALU.mult)\
                     .then_inc(diag_ready, 1)
                for u in range(GRP):
                    dve.wait_ge(spread_mm, r * GRP + u + 1)
                    V.tensor_tensor(x4[:, u, :], xc[:, u, :], P[:, 2 * u + 1, 0:L], ALU.mult).then_inc(x4_ready, 1)
                dve.wait_ge(x4_ready, (r + 1) * GRP)
                V.tensor_reduce(msum[:, :], x4[:, :, :], AX.X, ALU.add).then_inc(msum_ready, GRP)
                dve.wait_ge(score_mm, r + 1)
                wide = [1, GRP, E2]
                chain.link(V.tensor_scalar(sc[:, :, :], P[0:1, 1, 0:GRP * E2].rearrange("p (u e) -> p u e", u=GRP),
                                           1.0 / L, None, ALU.mult))
                chain.link(V.tensor_tensor(sc[:, :, :], sc[:, :, :], bg_s[:, :].unsqueeze(1).to_broadcast(wide), ALU.add))
                chain.link(V.tensor_reduce(top[:, :], sc[:, :, :], AX.X, ALU.max))
                V.tensor_tensor(sc[:, :, :], sc[:, :, :], top[:, :].unsqueeze(2).to_broadcast(wide), ALU.subtract)\
                 .then_inc(sc_ready, 1)
                dve.wait_ge(sc_exp, r + 1)
                chain.link(V.tensor_reduce(tot[:, :], sc[:, :, :], AX.X, ALU.add))
                chain.link(V.reciprocal(tot[:, :], tot[:, :]))
                chain.link(V.tensor_tensor(sc[:, :, :], sc[:, :, :], tot[:, :].unsqueeze(2).to_broadcast(wide), ALU.mult))
                chain.link(V.tensor_reduce(gate[:, :], sc[:, :, :], AX.X, ALU.max))
                chain.link(V.tensor_tensor(worse[:, :, :], sc[:, :, :], gate[:, :].unsqueeze(2).to_broadcast(wide),
                                           ALU.is_lt))
                chain.link(V.scalar_tensor_tensor(worse[:, :, :], worse[:, :, :], float(E2),
                                                  enum_s[:, :].unsqueeze(1).to_broadcast(wide), ALU.mult, ALU.add))
                chain.link(V.tensor_reduce(bestf[:, :], worse[:, :, :], AX.X, ALU.min))
                chain.end()
                V.tensor_copy(best[:, :], bestf[:, :]).then_inc(gate_ready, 1)
                if known(r, 1):
                    dve.wait_ge(out_stored, r * 16)
                for u in range(GRP):
                    dve.wait_ge(y_mm, r * GRP + u + 1)
                    dve.wait_ge(bsel_ready, r * GRP + u + 1)
                    V.scalar_tensor_tensor(fin[:, u, :], P[:, 2 * u, 0:L], bsel[:, u:u + 1], h3[:, u, :], ALU.add, ALU.add)\
                     .then_inc(fin_ready, 1)

            V.memset(mean3[:, :], 1.0 / D).then_inc(consts3_set, 1)
            V.memset(ones3[:, :], 1.0).then_inc(consts3_set, 1)
            V.memset(eps3[:, :], 1e-5).then_inc(consts3_set, 1)
            dve.wait_ge(consts3_in, 16 * len(loads))
            group(0)
            with dve.Fori(1, R) as r:
                group(r)


def early_fusion(nc, x, txt, tok_w, pos, vecs, wqkv, wo, wr, br, w1, w2, b2, wp, wo1, wg, bg, we, be,
                 ident, tri, expert_rows, eye_blocks, read_mask, expert_numbers, out):
    f32 = mybir.dt.float32
    h2_d = nc.dram_tensor("h2_d", [B, D, L], f32).ap()
    feat_d = nc.dram_tensor("feat_d", [B, L, FW], f32).ap()
    read_d = nc.dram_tensor("read_d", [B, L, D], f32).ap()
    images(nc, x, txt, tok_w, pos, vecs, wqkv, wo, wr, br, w1, w2, b2, wp, ident, tri, expert_rows, h2_d, feat_d)
    memory(nc, feat_d, ident, eye_blocks, read_mask, read_d)
    experts_out(nc, read_d, h2_d, vecs, wo1, wg, bg, we, be, ident, expert_numbers, out)


_OUT = (B, D, L)


def kernel(**inputs):
    import numpy as np
    import concourse.bacc as bacc
    from concourse.bass_utils import run_bass_kernel_spmd

    a = {k: np.asarray(v) for k, v in inputs.items()}

    def col(v):
        return v.reshape(-1, 128).T

    xs = a["x"].reshape(B, 3, 11, 16, 13, 16).transpose(0, 3, 5, 1, 2, 4).reshape(B, KC, 128, PATCHES)
    vecs = [a["L0_tok_b"], a["L0_tok_cls_token"].reshape(D), a["L0_attn_bq"], a["L0_attn_bk"], a["L0_attn_bv"],
            a["L0_attn_bo"], a["L0_attn_gamma"], a["L0_attn_beta"], a["L1_attn_bo"]]
    feeds = [
        ("x", xs.transpose(0, 2, 1, 3)),
        ("txt", a["txt"].transpose(0, 2, 1)),
        ("tok_w", a["L0_tok_W"].T.reshape(KC, 128, D).transpose(1, 0, 2)),
        ("pos", np.broadcast_to(a["L0_tok_pos_emb"].reshape(1, LX), (128, LX))),
        ("vecs", np.concatenate([v.reshape(D, 1) for v in vecs] + [col(a["L0_ffn_b1"].reshape(-1))], axis=1)),
        ("wqkv", np.stack([a["L0_attn_Wq"].T, a["L0_attn_Wk"].T, a["L0_attn_Wv"].T], axis=1)),
        ("wo", a["L0_attn_Wo"].T),
        ("wr", a["L0_ffn_Wr"].T),
        ("br", np.broadcast_to(a["L0_ffn_br"].reshape(1, E1), (128, E1))),
        ("w1", a["L0_ffn_W1"].transpose(1, 0, 2)),
        ("w2", a["L0_ffn_W2"].reshape(E1, 2, 128, D).transpose(2, 0, 1, 3)),
        ("b2", np.tile(a["L0_ffn_b2"], (PARTS, 1))),
        ("wp", np.concatenate([a["L1_attn_Wk"], a["L1_attn_Wq"], a["L1_attn_Wv"], a["L1_attn_Wg"]], axis=1)),
        ("wo1", a["L1_attn_Wo"]),
        ("wg", a["L1_ffn_Wg"]),
        ("bg", a["L1_ffn_bg"].reshape(1, E2)),
        ("we", a["L1_ffn_We"].transpose(1, 0, 2).reshape(D, E2 * D)),
        ("be", a["L1_ffn_be"].T),
        ("ident", np.eye(128, dtype=np.float32)),
        ("tri", np.broadcast_to(np.tri(E1, k=-1, dtype=np.float32), (128, E1, E1))),
        ("expert_rows", np.tile(np.eye(E1, dtype=np.float32)[:, :, None], (PARTS, 1, 128))),
        ("eye_blocks", np.broadcast_to(np.eye(SUB, dtype=np.float32)[None, :, None, :], (128, SUB, 4, SUB))),
        ("read_mask", np.tile(np.triu(np.ones((B, B), np.float32)), (2, 1))),
        ("expert_numbers", np.arange(E2, dtype=np.float32).reshape(1, E2)),
    ]
    nc = bacc.Bacc("TRN2", target_bir_lowering=False, num_devices=1)
    arrays, args = {}, []
    for name, v in feeds:
        v = np.ascontiguousarray(v)
        arrays[f"in_{name}"] = v
        args.append(nc.dram_tensor(f"in_{name}", v.shape, mybir.dt.from_np(v.dtype), kind="ExternalInput").ap())
    out = nc.dram_tensor("out", _OUT, mybir.dt.float32, kind="ExternalOutput").ap()
    early_fusion(nc, *args, out)
    r = run_bass_kernel_spmd(nc, [arrays], core_ids=[0])
    return np.ascontiguousarray(r.results[0]["out"].transpose(0, 2, 1))
```
